# Optimizing a Trainium2 kernel written in Bass

```python
import numpy as np
import jax
import jax.numpy as jnp

def _softmax(x, axis=-1):
    return jax.nn.softmax(x, axis=axis)

def _gelu(x):
    return jax.nn.gelu(x, approximate=True)

def _silu(x):
    return jax.nn.silu(x)

def _sigmoid(x):
    return jax.nn.sigmoid(x)

def _layernorm(x, axis=-1, eps=1e-05):
    m = jnp.mean(x, axis=axis, keepdims=True)
    v = jnp.var(x, axis=axis, keepdims=True)
    return (x - m) / jnp.sqrt(v + eps)

def _scatter_add(tgt, idx, src, axis=0):
    return tgt.at[idx].add(src)

def _segment_sum(src, seg, n):
    return jax.ops.segment_sum(src, seg, n)
kernel_name = 'mk_conv_seq_d2_conv_nchw256_r2_6fe9de'

def setup_inputs(seed: int=0):
    np.random.seed(seed)
    _w = jnp.asarray

    def _rec_inputs():
        import jax
        import jax.numpy as jnp
        _gk = jax.random.key(seed)
        x = 7.22e-05 + 1 * jax.random.normal(jax.random.fold_in(_gk, 1), (8, 128, 32, 32), jnp.float32)
        return x
    x = _rec_inputs()

    def _L0_conv_setup():
        import jax, jax.numpy as jnp
        import numpy as np
        B, C, H, W = (8, 128, 32, 32)
        GROUPS = 16
        EPS = 1e-06

        def _conv1x1(h, w, b):
            return jnp.einsum('bchw,oc->bohw', h, w) + b[None, :, None, None]
        key = jax.random.key(seed)
        ks = jax.random.split(key, 11)
        s = 1.0 / np.sqrt(C)
        return {'x': jax.random.normal(ks[0], (B, C, H, W), dtype=jnp.float32), 'norm_w': jnp.ones((C,), dtype=jnp.float32), 'norm_b': jnp.zeros((C,), dtype=jnp.float32), 'wq': jax.random.normal(ks[1], (C, C), dtype=jnp.float32) * s, 'bq': jnp.zeros((C,), dtype=jnp.float32), 'wk': jax.random.normal(ks[2], (C, C), dtype=jnp.float32) * s, 'bk': jnp.zeros((C,), dtype=jnp.float32), 'wv': jax.random.normal(ks[3], (C, C), dtype=jnp.float32) * s, 'bv': jnp.zeros((C,), dtype=jnp.float32), 'wp': jax.random.normal(ks[4], (C, C), dtype=jnp.float32) * s, 'bp': jnp.zeros((C,), dtype=jnp.float32)}
    _L0_conv_all = _L0_conv_setup()
    _L0_conv_in = {k: v for k, v in _L0_conv_all.items() if k in ('norm_w', 'norm_b', 'wq', 'bq', 'wk', 'bk', 'wv', 'bv', 'wp', 'bp')}
    del _L0_conv_all

    def _L1_conv_setup():
        import jax, jax.numpy as jnp
        import numpy as np
        M = 7
        EPS = 1e-08

        def _aniso_kernels(params):
            theta = jnp.arctan2(params[:, 0], params[:, 1]) / 2.0 + jnp.pi / 2.0
            lam1 = jnp.exp(params[:, 2])
            lam2 = 1.0 / (lam1 + EPS)
            lin = jnp.linspace(-(M // 2), M // 2, M, dtype=params.dtype)
            yy, xx = jnp.meshgrid(lin, lin, indexing='ij')
            cos_t = jnp.cos(theta)[:, None, None]
            sin_t = jnp.sin(theta)[:, None, None]
            x_rot = xx * cos_t + yy * sin_t
            y_rot = -xx * sin_t + yy * cos_t
            k = jnp.exp(-(x_rot ** 2 / (2.0 * lam1[:, None, None] ** 2) + y_rot ** 2 / (2.0 * lam2[:, None, None] ** 2)))
            return k / (k.sum(axis=(1, 2), keepdims=True) + EPS)
        key = jax.random.key(seed)
        ks = jax.random.split(key, 6)
        B, C, H, W = (8, 128, 64, 64)
        return {'x': jax.random.normal(ks[0], (B, C, H, W), dtype=jnp.float32), 'w1': jax.random.normal(ks[1], (M * M, 32), dtype=jnp.float32) * 0.1, 'b1': jnp.zeros((32,), dtype=jnp.float32), 'w2': jax.random.normal(ks[2], (32, 3), dtype=jnp.float32) * 0.1, 'b2': jnp.zeros((3,), dtype=jnp.float32), 'wr': jax.random.normal(ks[3], (128, 128), dtype=jnp.float32) * (1.0 / 16.0)}
    _L1_conv_all = _L1_conv_setup()
    _L1_conv_in = {k: v for k, v in _L1_conv_all.items() if k in ('w1', 'b1', 'w2', 'b2', 'wr')}
    del _L1_conv_all
    return {'x': x, 'L0_conv_norm_w': _L0_conv_in['norm_w'], 'L0_conv_norm_b': _L0_conv_in['norm_b'], 'L0_conv_wq': _L0_conv_in['wq'], 'L0_conv_bq': _L0_conv_in['bq'], 'L0_conv_wk': _L0_conv_in['wk'], 'L0_conv_bk': _L0_conv_in['bk'], 'L0_conv_wv': _L0_conv_in['wv'], 'L0_conv_bv': _L0_conv_in['bv'], 'L0_conv_wp': _L0_conv_in['wp'], 'L0_conv_bp': _L0_conv_in['bp'], 'L1_conv_w1': _L1_conv_in['w1'], 'L1_conv_b1': _L1_conv_in['b1'], 'L1_conv_w2': _L1_conv_in['w2'], 'L1_conv_b2': _L1_conv_in['b2'], 'L1_conv_wr': _L1_conv_in['wr']}

def reference(x, L0_conv_norm_w, L0_conv_norm_b, L0_conv_wq, L0_conv_bq, L0_conv_wk, L0_conv_bk, L0_conv_wv, L0_conv_bv, L0_conv_wp, L0_conv_bp, L1_conv_w1, L1_conv_b1, L1_conv_w2, L1_conv_b2, L1_conv_wr):
    import jax
    import jax.numpy as jnp

    def _L0_conv_ref(x, norm_w, norm_b, wq, bq, wk, bk, wv, bv, wp, bp):
        import jax, jax.numpy as jnp
        import numpy as np
        B, C, H, W = (8, 128, 32, 32)
        GROUPS = 16
        EPS = 1e-06

        def _conv1x1(h, w, b):
            return jnp.einsum('bchw,oc->bohw', h, w) + b[None, :, None, None]
        b, c, h, w = x.shape
        n = h * w
        xg = x.reshape(b, GROUPS, c // GROUPS, h, w)
        mu = xg.mean(axis=(2, 3, 4), keepdims=True)
        var = xg.var(axis=(2, 3, 4), keepdims=True)
        hn = ((xg - mu) * jax.lax.rsqrt(var + EPS)).reshape(b, c, h, w)
        hn = hn * norm_w[None, :, None, None] + norm_b[None, :, None, None]
        q = _conv1x1(hn, wq, bq).reshape(b, c, n)
        k = _conv1x1(hn, wk, bk).reshape(b, c, n)
        v = _conv1x1(hn, wv, bv).reshape(b, c, n)
        att = jnp.einsum('bci,bcj->bij', q, k) * c ** (-0.5)
        att = jax.nn.softmax(att, axis=2)
        out = jnp.einsum('bcj,bij->bci', v, att).reshape(b, c, h, w)
        return x + _conv1x1(out, wp, bp)

    def _L1_conv_ref(x, w1, b1, w2, b2, wr):
        import jax, jax.numpy as jnp
        import numpy as np
        M = 7
        EPS = 1e-08

        def _aniso_kernels(params):
            theta = jnp.arctan2(params[:, 0], params[:, 1]) / 2.0 + jnp.pi / 2.0
            lam1 = jnp.exp(params[:, 2])
            lam2 = 1.0 / (lam1 + EPS)
            lin = jnp.linspace(-(M // 2), M // 2, M, dtype=params.dtype)
            yy, xx = jnp.meshgrid(lin, lin, indexing='ij')
            cos_t = jnp.cos(theta)[:, None, None]
            sin_t = jnp.sin(theta)[:, None, None]
            x_rot = xx * cos_t + yy * sin_t
            y_rot = -xx * sin_t + yy * cos_t
            k = jnp.exp(-(x_rot ** 2 / (2.0 * lam1[:, None, None] ** 2) + y_rot ** 2 / (2.0 * lam2[:, None, None] ** 2)))
            return k / (k.sum(axis=(1, 2), keepdims=True) + EPS)
        B, C, H, W = x.shape
        xf = jnp.fft.fftshift(jnp.fft.fft2(x, norm='ortho'), axes=(-2, -1))
        mag = jnp.abs(xf).mean(axis=1)
        h0, w0 = (H // 2 - M // 2, W // 2 - M // 2)
        center = mag[:, h0:h0 + M, w0:w0 + M].reshape(B, M * M)
        hid = jax.nn.relu(center @ w1 + b1)
        params = hid @ w2 + b2
        kern = _aniso_kernels(params)
        stacked = jnp.concatenate([xf.real, xf.imag], axis=1)
        pad = [(M // 2, M // 2)] * 2

        def conv_one(img, k):
            return jax.lax.conv_general_dilated(img[:, None], k[None, None], (1, 1), pad)[:, 0]
        filt = jax.vmap(conv_one)(stacked, kern)
        real_f, imag_f = (filt[:, :C], filt[:, C:])
        rr = jnp.einsum('bchw,oc->bohw', real_f, wr)
        ii = jnp.einsum('bchw,oc->bohw', imag_f, wr)
        out_f = jnp.fft.ifftshift(jax.lax.complex(rr, ii), axes=(-2, -1))
        return jnp.fft.ifft2(out_f, norm='ortho').real + x

    def _gn(v, G=32, eps=1e-05):
        B_, C_, H_, W_ = v.shape
        g = v.reshape(B_, G, C_ // G, H_, W_)
        m = jnp.mean(g, axis=(2, 3, 4), keepdims=True)
        s = jnp.var(g, axis=(2, 3, 4), keepdims=True)
        return ((g - m) / jnp.sqrt(s + eps)).reshape(v.shape)

    def _ln_c(v, eps=1e-06):
        m = jnp.mean(v, axis=1, keepdims=True)
        s = jnp.var(v, axis=1, keepdims=True)
        return (v - m) / jnp.sqrt(s + eps)

    def _ln_t(v, eps=1e-05):
        m = jnp.mean(v, axis=-1, keepdims=True)
        s = jnp.var(v, axis=-1, keepdims=True)
        return (v - m) / jnp.sqrt(s + eps)

    def _to_tokens(v):
        B_, C_, H_, W_ = v.shape
        return v.reshape(B_, C_, H_ * W_).transpose(0, 2, 1)

    def _from_tokens(t, like):
        B_, C_, H_, W_ = like.shape
        return t.transpose(0, 2, 1).reshape(B_, C_, H_, W_)
    x = _L0_conv_ref(x, L0_conv_norm_w, L0_conv_norm_b, L0_conv_wq, L0_conv_bq, L0_conv_wk, L0_conv_bk, L0_conv_wv, L0_conv_bv, L0_conv_wp, L0_conv_bp)
    x = _L1_conv_ref(x, L1_conv_w1, L1_conv_b1, L1_conv_w2, L1_conv_b2, L1_conv_wr)
    return x

_drawn_inputs = setup_inputs


def setup_inputs(seed=0):
    import zlib

    import numpy as np

    out = dict(_drawn_inputs(seed))
    spreads = {'L0_conv_norm_w': (1.0, 0.2),
     'L0_conv_norm_b': (0.0, 0.1),
     'L0_conv_bq': (0.0, 0.697),
     'L0_conv_bk': (0.0, 2.0),
     'L0_conv_bv': (0.0, 0.1),
     'L0_conv_bp': (0.0, 0.1),
     'L1_conv_b1': (0.0, 0.8),
     'L1_conv_b2': (0.0, 2.0)}
    factors = {'L1_conv_w1': 2.789}
    for name, (base, spread) in spreads.items():
        noise = np.random.default_rng([zlib.crc32(name.encode()), seed]).standard_normal(out[name].shape)
        drawn = base * np.exp(spread * noise) if base else spread * noise
        out[name] = jnp.asarray(drawn.astype(out[name].dtype))
    for name, factor in factors.items():
        out[name] = (out[name] * factor).astype(out[name].dtype)
    return out
```

```python
from contextlib import ExitStack

import numpy as np

import concourse.bass as bass
from concourse import mybir

F32 = mybir.dt.float32
F32R = mybir.dt.float32r
ALU = mybir.AluOpType
ACT = mybir.ActivationFunctionType
AX = mybir.AxisListType

B, C, SIDE = 8, 128, 32
N = SIDE * SIDE
P = 128
HALF = 512
TILES = N // P
GROUPS = 16
GN_EPS = 1e-6
SCALE = float(C) ** -0.5
TAPS = 7
NK = TAPS * TAPS
KEPS = 1e-8
NZ = 7
CH = 16 * NZ
NF = (NK + 1) // 2
UA = 2 * CH + 2 * NF
UB = 4 * NZ
UR = UA + TILES * UB
UW = TILES * UA + UB
HID = 32
T_U1, T_U2, T_PR, T_EX, T_COS = 0, HALF, 2 * HALF, 2 * HALF + 2 * P, 2 * HALF + 2 * P + 2 * CH
T_END = T_COS + N


def shape_tables():
    h = np.arange(SIDE)
    z = np.stack([f(2 * np.pi * u * h / SIDE) for u in (13, 14, 15) for f in (np.cos, np.sin)]
                 + [np.cos(np.pi * h)], 1)
    z /= np.linalg.norm(z, axis=0)
    u = np.arange(-SIDE // 2, SIDE // 2)
    dft = np.exp(-2j * np.pi * np.outer(u, h) / SIDE) / np.sqrt(SIDE)
    r = TAPS // 2
    d = np.stack([np.exp(-2j * np.pi * a * h / SIDE) for a in range(-r, r + 1)])
    o = []
    for a in range(-r, r + 1):
        wrapped = np.zeros((SIDE, SIDE))
        for row in range(SIDE):
            if not 0 <= row + a < SIDE:
                wrapped[row, (row + a) % SIDE] = 1
        o.append(z.T @ (dft.conj().T @ wrapped @ dft) @ z)
    o = np.stack(o)
    taps = [(a, b) for a in range(TAPS) for b in range(TAPS)]
    eye = np.eye(P)

    ana = np.zeros((P, UW))
    centre = taps[:NF]
    for t in range(TILES):
        for hl in range(4):
            hh = 4 * t + hl
            for w in range(SIDE):
                row = hl * SIDE + w
                ana[row, t * UA + w * NZ:t * UA + (w + 1) * NZ] = z[hh]
                ph = np.array([2 * np.pi * ((a - r) * hh + (b - r) * w) / SIDE for a, b in centre])
                ana[row, t * UA + 2 * CH:t * UA + 2 * CH + NF] = np.cos(ph) / SIDE
                ana[row, t * UA + 2 * CH + NF:(t + 1) * UA] = -np.sin(ph) / SIDE
    for hl in range(4):
        for w in range(SIDE):
            ana[hl * SIDE + w, TILES * UA + hl * NZ:TILES * UA + (hl + 1) * NZ] = z[w]

    syn = np.zeros((P, T_END))
    for w in range(16):
        for q in range(NZ):
            syn[w * NZ + q, T_U1 + w:T_U1 + HALF:16] = -z[:, q]
            syn[w * NZ + q, T_U2 + w * SIDE:T_U2 + (w + 1) * SIDE] = -z[:, q]
    for c in range(2):
        for hl in range(16):
            for a in range(NZ):
                for q in range(NZ):
                    v = z[16 * c + hl, a]
                    syn[hl * NZ + q, T_PR + c * P + a * NZ + q] = v
                    syn[a * NZ + q, T_EX + c * CH + hl * NZ + q] = -v
    syn[:NK, T_COS:T_COS + N] = np.stack([np.outer(d[a], d[b]).real.ravel() for a, b in taps])

    g1 = np.stack([np.einsum("rs,w->swr", o[a], d[b]).real.reshape(NZ, -1) for a, b in taps])
    gam = g1.reshape(NK, NZ, 2, CH).transpose(0, 2, 1, 3).reshape(NK, -1)
    gam3 = np.stack([np.kron(o[a], o[b]).real for a, b in taps]).reshape(NK, -1)

    misc = np.zeros((P, M_END))
    c0 = 0
    misc[:, :P] = eye
    misc[:, P:2 * P] = np.kron(np.eye(GROUPS), np.full((C // GROUPS,) * 2, GROUPS / C))
    c0 = 2 * P
    for row in range(CH):
        misc[row, c0 + row // NZ] = 1
    c0 += 16
    for i in range(NK):
        misc[min(i, NK - 1 - i), c0 + i] = 1
    c0 += NK
    for i, (a, b) in enumerate(taps):
        misc[i, c0:c0 + 2] = (b - r, a - r)
    c0 += 2
    misc[:, c0:c0 + NK] = 1
    c0 += NK
    misc[:, c0] = 1.0 / C
    c0 += 1
    for i, (a, b) in enumerate(taps):
        misc[b * TAPS + a, c0 + i] = 1
    f = np.float32
    return {"ana": ana.astype(f), "syn": syn.astype(f), "gam": gam.astype(f),
            "gam3": gam3.astype(f), "misc": misc.astype(f)}


M_EYE, M_AVG, M_MASK, M_SEL = 0, P, 2 * P, 2 * P + 16
M_XY = M_SEL + NK
M_ONES = M_XY + 2
M_MEAN = M_ONES + NK
M_TR = M_MEAN + 1
M_END = M_TR + NK
GAM = 2 * NZ * CH


def attention_filter_kernel(nc, x, norm_w, norm_b, wq, bq, wk, bk, wv, bv, wp, bp, w1, b1, w2, b2,
                            wr, ana, syn, gam, gam3, misc, out):
    x_v = x.rearrange("b c h w -> b c (h w)")
    out_v = out.rearrange("b c h w -> c b (h w)")

    with ExitStack() as ctx:
        def sb(name, shape, dt=F32):
            return ctx.enter_context(nc.sbuf_tensor(name, shape, dt))

        def sem(name):
            return ctx.enter_context(nc.semaphore(name))

        X = sb("X", [P, B * N])
        T = sb("T", [P, N])
        HNH, HNL = sb("HNH", [P, N], F32R), sb("HNL", [P, N], F32R)
        QH, QL = sb("QH", [P, N], F32R), sb("QL", [P, N], F32R)
        KH, KL = sb("KH", [P, N], F32R), sb("KL", [P, N], F32R)
        VH, VL = sb("VH", [P, TILES, P], F32R), sb("VL", [P, TILES, P], F32R)
        E = sb("E", [P, 4 * N])
        ETH = sb("ETH", [P, 2 * TILES * HALF], F32R)
        ETL = sb("ETL", [P, 2 * TILES * HALF], F32R)
        XTH, XTL = sb("XTH", [P, TILES, P], F32R), sb("XTL", [P, TILES, P], F32R)
        R = sb("R", [P, B * UR])
        ANH, ANL = sb("ANH", [P, UW], F32R), sb("ANL", [P, UW], F32R)
        SYN = sb("SYN", [P, T_END])
        MISC = sb("MISC", [P, M_END])
        WRAW = E[:, 0:5 * P].rearrange("p (i c) -> p i c", i=5)
        WT = E[:, 5 * P:9 * P].rearrange("p (i c) -> p i c", i=4)
        WPT = E[:, 9 * P:10 * P]
        WH, WL = sb("WH", [P, 4, P], F32R), sb("WL", [P, 4, P], F32R)
        VEC = sb("VEC", [P, 6])
        BQS, BVP = sb("BQS", [P, 1]), sb("BVP", [P, 1])
        STAT = sb("STAT", [P, B, 12])
        MV = sb("MV", [P, B, 2])
        GM, GD, GS = sb("GM", [P, B]), sb("GD", [P, B]), sb("GS", [P, B])
        GA, GB, GP = sb("GA", [P, B]), sb("GB", [P, B]), sb("GP", [P, 1])
        NMX, RS, RI = sb("NMX", [P, 2]), sb("RS", [P, 4]), sb("RI", [P, 4])
        W1, B1, W2 = sb("W1", [NK, HID]), sb("B1", [HID, 1]), sb("W2", [HID, 3])
        W2R, B2 = sb("W2R", [HID, 3, NK]), sb("B2", [NK, 3])
        C25, CEN, HIDV = sb("C25", [NF, B]), sb("CEN", [NK, B]), sb("HIDV", [HID, B])
        ML = sb("ML", [NK, 30, B])
        K = sb("K", [NK, 2 * B])
        G3S = sb("G3S", [NK, P])
        PS = ctx.enter_context(nc.psum_tensor("PS", [P, 8 * HALF], F32))

        eye = MISC[:, M_EYE:M_EYE + P]
        avg = MISC[:, M_AVG:M_AVG + P]
        QI, KI, VI, RI_ = 0, 1, 2, 3

        def s_bank(t):
            return PS[:, (t % 2) * N:(t % 2 + 1) * N]

        def bank(i, n=HALF, parts=P):
            return PS[0:parts, i * HALF:i * HALF + n]
        ET_BANK, PV_BANK, MISC_BANK = 4, 6, 7

        at = [0]

        def carve(n):
            a = at[0]
            at[0] += n
            return ETH[:, a:a + n], ETL[:, a:a + n]
        SYH, SYL = carve(T_END)
        RTH, RTL = carve(4 * P)
        V3H, V3L = carve(P)
        VTH, VTL = carve(4 * P)
        GH, GL = carve(4 * CH)
        ZH, ZL = carve(N)
        KBH, KBL = carve(P)
        GAMS, GAM3S = E[0:NK, 0:GAM], E[0:NK, GAM:GAM + NK * NK]
        KHAT, KX, ZF, GF = E[:, 0:N], E[:, N:2 * N], E[:, 2 * N:3 * N], E[:, 3 * N:3 * N + 4 * CH]
        RST = T[:, 0:4 * P]
        R3S = T[0:NK, 4 * P:5 * P]
        GC = T[0:CH, 5 * P:5 * P + B * 4 * NZ]
        G3C = E[0:NK, 3 * N + 4 * CH:3 * N + 4 * CH + B * NK]

        names = """d_x0 d_xs d_w d_vec d_misc d_ana d_syn d_mlp d_gam d_out
            p_wt p_bvp p_gn1 p_gn2 v_wt v_wpt v_wpv v_bvp v_bqs v_wl a_wh v_st v_gn g_gn a_ah g_al v_w2r
            v_t a_hh g_hl p_q a_qh v_ql p_k a_kh v_kl p_s v_mx a_exp v_ri g_scl p_tr a_hi v_lo
            p_pv v_x1 g_x1 p_xt a_xh v_xl p_v a_vh v_vl p_u a_ur
            v_m2 a_mag p_c25 v_c25 p_cen v_cen p_hid v_hid p_par v_ml a_ml p_sum v_k p_kt p_g g_one v_g g_sl a_sh
            g_rst p_rt a_rth v_rtl p_r3 a_r3 v_g3s p_v3 a_v3h v_v3l v_gf a_gh v_gl p_vt a_vth v_vtl
            a_kbh v_kbl p_kh a_kh2 g_kx p_z v_z a_zh g_zl p_o v_o""".split()
        s = {n: sem(n) for n in names}

        block = ctx.enter_context(nc.Block())

        def passes(hi1, lo1, hi2, lo2):
            return ((hi1, hi2), (hi1, lo2), (lo1, hi2))

        def attention(run, eng):
            run(0, True, False, True)
            with eng.Fori(1, B - 1) as b:
                run(b, True, True, True)
            run(B - 1, True, True, False)
            run(B, False, True, False)

        def synthesis(front, both, eng):
            front(0)
            both(0, True)
            with eng.Fori(1, B - 1) as b:
                both(b, True)
            both(B - 1, False)

        @block.sync
        def _(sp):
            sp.dma_start(X[:, 0:N], x_v[0]).then_inc(s["d_x0"], 16)
            sp.dma_start(MISC[:], misc).then_inc(s["d_misc"], 16)
            for i, w in enumerate((wq, wk, wv, wp, wr)):
                sp.dma_start(WRAW[:, i, :], w).then_inc(s["d_w"], 16)
            for b in range(1, B):
                sp.dma_start(X[:, b * N:(b + 1) * N], x_v[b]).then_inc(s["d_xs"], 16)
            sp.dma_start(SYN[:], syn).then_inc(s["d_syn"], 16)
            sp.wait_ge(s["p_tr"], 2 * TILES * B)
            sp.dma_start(GAMS, gam).then_inc(s["d_gam"], 16)
            sp.dma_start(GAM3S, gam3).then_inc(s["d_gam"], 16)
            with sp.Fori(0, B) as b:
                sp.wait_ge(s["v_o"], 2 * b + 2)
                sp.dma_start(out_v[:, bass.ds(b, 1), :], X[:, bass.ds(b * N, N)])\
                    .then_inc(s["d_out"], 16)
            sp.wait_ge(s["d_out"], 16 * B)

        @block.tensor
        def _(pe):
            def mm(o, a, b_, start, stop):
                return pe.matmul(o, a, b_, start=start, stop=stop)

            pe.wait_ge(s["d_misc"], 16)
            pe.wait_ge(s["d_w"], 16 * 5)
            for slot, i in enumerate((0, 1, 3, 4)):
                ins = pe.transpose(bank(MISC_BANK)[:, slot * P:(slot + 1) * P], WRAW[:, i, :], eye)
            ins.then_inc(s["p_wt"], 1)
            pe.wait_ge(s["v_wpt"], 1)
            pe.wait_ge(s["d_vec"], 16 * 6)
            mm(bank(PV_BANK)[:, 0:P], WRAW[:, 2, :], WPT, True, True)
            mm(bank(PV_BANK)[:, P:P + 1], WPT, VEC[:, 4:5], True, True).then_inc(s["p_bvp"], 1)

            def group_norm(cols, n):
                lo, hi = cols
                pe.wait_ge(s["v_gn"], 6 * n + 1)
                mm(bank(PV_BANK)[:, 256:256 + hi - lo], avg, MV[:, lo:hi, 0], True, True)\
                    .then_inc(s["p_gn1"], 1)
                pe.wait_ge(s["v_gn"], 6 * n + 3)
                mm(bank(PV_BANK)[:, 288:288 + hi - lo], avg, GD[:, lo:hi], True, True)\
                    .then_inc(s["p_gn2"], 1)

            pe.wait_ge(s["v_bvp"], 1)
            group_norm((0, 1), 0)

            def project(w, bias_sem, base):
                for h in range(2):
                    o = PS[:, base + h * HALF:base + (h + 1) * HALF]
                    for n, (a, r) in enumerate(passes(WH[:, w, :], WL[:, w, :],
                                                      HNH[:, h * HALF:(h + 1) * HALF],
                                                      HNL[:, h * HALF:(h + 1) * HALF])):
                        ins = mm(o, a, r, n == 0, n == 2)
                    ins.then_inc(s[bias_sem], 1)

            def scores(b, t):
                q0 = slice(t * P, (t + 1) * P)
                for n, (a, r) in enumerate(passes(QH[:, q0], QL[:, q0], KH, KL)):
                    for h in range(2):
                        ins = mm(s_bank(t)[:, h * HALF:(h + 1) * HALF], a,
                                 r[:, h * HALF:(h + 1) * HALF], n == 0, n == 2)
                ins.then_inc(s["p_s"], 1)

            def transposes(b, t, after_first=True):
                pe.wait_ge(s["g_scl"], TILES * b + t + 1)
                for k in range(2):
                    if after_first:
                        pe.wait_ge(s["v_lo"], 2 * (TILES * b + t) + k - 1)
                    for j in range(4):
                        c0 = (t % 4) * N + (4 * k + j) * P
                        ins = pe.transpose(bank(ET_BANK + k)[:, j * P:(j + 1) * P],
                                           E[:, c0:c0 + P], eye)
                    ins.then_inc(s["p_tr"], 1)

            def values(b, h, c, first=False):
                if c == 0:
                    pe.wait_ge(s["v_lo"], 16 * b + 8 * h + 8)
                    if not first:
                        pe.wait_ge(s["v_x1"], 2 * b + h)
                if h == 0 and c == 0:
                    pe.wait_ge(s["v_vl"], 2 * b + 1)
                if h == 0 and c == 2:
                    pe.wait_ge(s["v_vl"], 2 * b + 2)
                for j in (2 * c, 2 * c + 1):
                    e0 = (h * TILES + j) * HALF
                    for n, (a, r) in enumerate(passes(VH[:, j, :], VL[:, j, :],
                                                      ETH[:, e0:e0 + HALF], ETL[:, e0:e0 + HALF])):
                        ins = mm(bank(PV_BANK), a, r, j == 0 and n == 0, j == TILES - 1 and n == 2)
                if c == 3:
                    ins.then_inc(s["p_pv"], 1)

            def x1_transposes(p, h):
                pe.wait_ge(s["v_x1"], 2 * p + h + 1)
                for j in range(4):
                    c0 = h * HALF + j * P
                    ins = pe.transpose(bank(MISC_BANK)[:, j * P:(j + 1) * P], T[:, c0:c0 + P], eye)
                ins.then_inc(s["p_xt"], 1)

            def project_v(b, h):
                for j in range(4):
                    t0 = (4 * h + j) * P
                    for n, (a, r) in enumerate(passes(HNH[:, t0:t0 + P], HNL[:, t0:t0 + P],
                                                      WH[:, VI, :], WL[:, VI, :])):
                        ins = mm(bank(MISC_BANK)[:, j * P:(j + 1) * P], a, r, n == 0, n == 2)
                ins.then_inc(s["p_v"], 1)

            def analysis(p):
                pe.wait_ge(s["v_xl"], 2 * p + 2)
                pe.wait_ge(s["g_al"], 1)
                for t in range(TILES):
                    u = slice(t * UA, (t + 1) * UA)
                    for n, (a, r) in enumerate(passes(XTH[:, t, :], XTL[:, t, :],
                                                      ANH[:, u], ANL[:, u])):
                        mm(bank(MISC_BANK)[:, 0:UA], a, r, t == 0 and n == 0,
                           t == TILES - 1 and n == 2)
                u = slice(TILES * UA, UW)
                for t in range(TILES):
                    o = bank(MISC_BANK)[:, UA + t * UB:UA + (t + 1) * UB]
                    for n, (a, r) in enumerate(passes(XTH[:, t, :], XTL[:, t, :],
                                                      ANH[:, u], ANL[:, u])):
                        ins = mm(o, a, r, n == 0, n == 2)
                ins.then_inc(s["p_u"], 1)

            def image(b, cur, prev, nxt):
                p = b - 1
                if cur:
                    pe.wait_ge(s["g_hl"], b + 1)
                    if prev:
                        pe.wait_ge(s["a_exp"], TILES * b - 1)
                    else:
                        pe.wait_ge(s["v_wl"], 1)
                    project(QI, "p_q", 0)
                    if prev:
                        pe.wait_ge(s["a_exp"], TILES * b)
                    project(KI, "p_k", N)
                for t in range(TILES):
                    if cur:
                        if t == 0:
                            if prev:
                                transposes(p, 6)
                                values(p, 0, 2)
                            pe.wait_ge(s["v_kl"], 2 * b + 2)
                        if t >= 2:
                            pe.wait_ge(s["a_exp"], TILES * b + t - 1)
                        scores(b, t)
                        if t >= 2:
                            transposes(b, t - 2, after_first=prev or t > 2)
                    if prev:
                        if t == 0 and not cur:
                            transposes(p, 6)
                            values(p, 0, 2)
                        if t == 1:
                            transposes(p, 7)
                            values(p, 0, 3)
                        if t == 2:
                            values(p, 1, 0)
                            if cur:
                                pe.wait_ge(s["a_ur"], b)
                            else:
                                pe.wait_ge(s["a_ur"], b)
                            x1_transposes(p, 0)
                        if t == 3:
                            values(p, 1, 1)
                        if t == 4:
                            values(p, 1, 2)
                        if t == 5:
                            values(p, 1, 3)
                    if cur:
                        if t == 4:
                            if prev:
                                pe.wait_ge(s["v_xl"], 2 * p + 1)
                            project_v(b, 0)
                        if t == 5:
                            pe.wait_ge(s["v_vl"], 2 * b + 1)
                            project_v(b, 1)
                            if not prev:
                                group_norm((1, B), 1)
                    if t == 6:
                        if prev:
                            if cur:
                                pe.wait_ge(s["v_vl"], 2 * b + 2)
                            else:
                                pe.wait_ge(s["v_xl"], 2 * p + 1)
                            x1_transposes(p, 1)
                        if cur:
                            if not prev:
                                pe.wait_ge(s["v_gn"], 12)
                            values(b, 0, 0, first=not prev)
                    if t == 7:
                        if prev:
                            analysis(p)
                        if cur:
                            values(b, 0, 1)

            attention(image, pe)

            A, D = bank(6), bank(7)
            pe.wait_ge(s["a_mag"], 1)
            mag = T[:, 600:600 + B * NF]
            for b in range(B):
                ins = mm(A[0:NF, b:b + 1], mag[:, b * NF:(b + 1) * NF],
                         MISC[:, M_MEAN:M_MEAN + 1], True, True)
            ins.then_inc(s["p_c25"], 1)
            pe.wait_ge(s["v_c25"], 1)
            mm(D[0:NK, 0:B], MISC[0:NF, M_SEL:M_SEL + NK], C25[:], True, True)\
                .then_inc(s["p_cen"], 1)
            pe.wait_ge(s["v_cen"], 1)
            pe.wait_ge(s["d_mlp"], 16 * 4)
            mm(A[0:HID, 32:32 + B], W1[:], CEN[:], True, True).then_inc(s["p_hid"], 1)
            pe.wait_ge(s["v_hid"], 1)
            for j in range(3):
                ins = mm(D[0:NK, 32 + j * B:32 + (j + 1) * B], W2R[:, j, :], HIDV[:], True, True)
            ins.then_inc(s["p_par"], 1)
            pe.wait_ge(s["a_ml"], 4)
            mm(A[0:NK, 64:64 + B], MISC[0:NK, M_ONES:M_ONES + NK], ML[:, 28, :], True, True)\
                .then_inc(s["p_sum"], 1)
            pe.wait_ge(s["v_k"], 1)
            pe.wait_ge(s["d_gam"], 32)
            mm(D[0:NK, 128:128 + B], MISC[0:NK, M_TR:M_TR + NK], K[:, 0:B], True, True)\
                .then_inc(s["p_kt"], 1)
            pe.wait_ge(s["v_k"], 2)
            for i in range(2 * NZ):
                mm(bank(5)[0:CH, i * 2 * B:(i + 1) * 2 * B], GAMS[:, i * CH:(i + 1) * CH], K[:],
                   True, True)
            for i in range(NK):
                ins = mm(bank(4)[0:NK, i * B:(i + 1) * B], GAM3S[:, i * NK:(i + 1) * NK],
                         K[:, 0:B],
                         True, True)
            ins.then_inc(s["p_g"], 1)
            pe.wait_ge(s["v_g"], 3)
            pe.wait_ge(s["g_sl"], 1)

            def rt(n, again):
                pe.wait_ge(s["g_rst"], 2 * n + 2)
                if again:
                    pe.wait_ge(s["v_rtl"], n)
                for i in range(4):
                    ins = pe.transpose(bank(4)[0:CH, i * P:(i + 1) * P],
                                       RST[:, i * CH:(i + 1) * CH], eye)
                ins.then_inc(s["p_rt"], 1)

            def r3(n):
                pe.wait_ge(s["v_rtl"], n + 1)
                m = 0
                for c in range(2):
                    w = slice(T_PR + c * P, T_PR + (c + 1) * P)
                    d_ = slice((2 + c) * P, (3 + c) * P)
                    for a, r in passes(SYH[0:CH, w], SYL[0:CH, w], RTH[0:CH, d_], RTL[0:CH, d_]):
                        ins = mm(bank(5)[:, 0:P], a, r, m == 0, m == 5)
                        m += 1
                ins.then_inc(s["p_r3"], 1)

            def v3(n):
                pe.wait_ge(s["a_r3"], n + 1)
                pe.wait_ge(s["v_g3s"], n + 1)
                mm(bank(5)[:, P:2 * P], G3S[:], R3S, True, True).then_inc(s["p_v3"], 1)

            def vt(n):
                pe.wait_ge(s["v_v3l"], n + 1)
                pe.wait_ge(s["v_gl"], n + 1)
                for i in range(4):
                    d_ = slice(i * P, (i + 1) * P)
                    g = slice(i * CH, (i + 1) * CH)
                    jobs = list(passes(GH[0:CH, g], GL[0:CH, g], RTH[0:CH, d_], RTL[0:CH, d_]))
                    if i >= 2:
                        w = slice(T_EX + (i - 2) * CH, T_EX + (i - 1) * CH)
                        jobs += passes(SYH[0:NK, w], SYL[0:NK, w], V3H[0:NK, :], V3L[0:NK, :])
                    for m, (a, r) in enumerate(jobs):
                        ins = mm(bank(6)[0:CH, d_], a, r, m == 0, m == len(jobs) - 1)
                ins.then_inc(s["p_vt"], 1)

            def khat(n, h, again):
                if h == 0:
                    pe.wait_ge(s["v_kbl"], n + 1)
                if again:
                    pe.wait_ge(s["a_kh2"], 2 * n + h - 1)
                w = slice(T_COS + h * HALF, T_COS + (h + 1) * HALF)
                for m, (a, r) in enumerate(passes(KBH[0:NK, :], KBL[0:NK, :],
                                                  SYH[0:NK, w], SYL[0:NK, w])):
                    ins = mm(bank(2 + h), a, r, m == 0, m == 2)
                ins.then_inc(s["p_kh"], 1)

            def z(b, h):
                pe.wait_ge(s["v_vtl"], b + 1)
                jobs = []
                d_ = slice((2 + h) * P, (3 + h) * P)
                for a, r in passes(VTH[0:CH, d_], VTL[0:CH, d_], SYH[0:CH, T_U2:T_U2 + HALF],
                                   SYL[0:CH, T_U2:T_U2 + HALF]):
                    jobs.append((bank(h), a, r))
                w = slice(T_U1 + h * 256, T_U1 + (h + 1) * 256)
                grid = bank(h).rearrange("c (h w) -> c h w", w=SIDE)
                for i in range(2):
                    d_ = slice(i * P, (i + 1) * P)
                    for a, r in passes(VTH[0:CH, d_], VTL[0:CH, d_], SYH[0:CH, w], SYL[0:CH, w]):
                        jobs.append((grid[:, :, 16 * i:16 * (i + 1)], a,
                                     r.rearrange("c (h w) -> c h w", w=16)))
                for m, (o, a, r) in enumerate(jobs):
                    ins = mm(o, a, r, m == 0, m == len(jobs) - 1)
                ins.then_inc(s["p_z"], 1)

            def mix(b, h):
                pe.wait_ge(s["g_zl"], 2 * b + h + 1)
                if h == 1 or not isinstance(b, int) or b:
                    pe.wait_ge(s["v_o"], 2 * b + h)
                d_ = slice(h * HALF, (h + 1) * HALF)
                for m, (a, r) in enumerate(passes(WH[:, RI_, :], WL[:, RI_, :], ZH[:, d_], ZL[:, d_])):
                    ins = mm(bank(7), a, r, m == 0, m == 2)
                ins.then_inc(s["p_o"], 1)

            def front(n):
                rt(n, False)
                r3(n)
                v3(n)
                khat(n, 0, False)
                vt(n)
                khat(n, 1, False)

            def both(b, more):
                if more:
                    rt(b + 1, True)
                z(b, 0)
                if more:
                    r3(b + 1)
                z(b, 1)
                if more:
                    v3(b + 1)
                    khat(b + 1, 0, True)
                mix(b, 0)
                if more:
                    vt(b + 1)
                    khat(b + 1, 1, True)
                mix(b, 1)

            synthesis(front, both, pe)

        @block.scalar
        def _(act):
            for i, v in enumerate((norm_w, norm_b, bq, bk, bv, bp)):
                act.dma_start(VEC[:, i:i + 1], v.rearrange("(c a) -> c a", a=1))\
                    .then_inc(s["d_vec"], 16)
            act.dma_start(R[:, 0:UW], ana).then_inc(s["d_ana"], 16)
            act.dma_start(W1[:], w1).then_inc(s["d_mlp"], 16)
            act.dma_start(B1[:], b1.rearrange("(c a) -> c a", a=1)).then_inc(s["d_mlp"], 16)
            act.dma_start(W2[:], w2).then_inc(s["d_mlp"], 16)
            act.dma_start(B2[:], b2.rearrange("(a c) -> a c", a=1).broadcast_to([NK, 3]))\
                .then_inc(s["d_mlp"], 16)

            act.wait_ge(s["v_wpv"], 1)
            act.activation(WH[:], WT, ACT.Copy).then_inc(s["a_wh"], 1)

            def hn_hi(b):
                act.wait_ge(s["v_t"], b + 1)
                act.activation(HNH[:], T[:], ACT.Copy).then_inc(s["a_hh"], 1)

            hn_hi(0)
            act.wait_ge(s["d_ana"], 16)
            act.activation(ANH[:, 0:UA], R[:, 0:UA], ACT.Copy).then_inc(s["a_ur"], 1)
            act.activation(ANH[:, UA:UW], R[:, UA:UW], ACT.Copy).then_inc(s["a_ah"], 1)

            def project_hi(dst, base, bias, done, out_sem, b):
                for h in range(2):
                    act.wait_ge(s[done], 2 * b + h + 1)
                    act.activation(dst[:, h * HALF:(h + 1) * HALF],
                                   PS[:, base + h * HALF:base + (h + 1) * HALF], ACT.Identity,
                                   bias=bias).then_inc(s[out_sem], 1)

            def exp(b, t):
                act.wait_ge(s["v_mx"], TILES * b + t + 1)
                act.activation(E[:, (t % 4) * N:(t % 4 + 1) * N], s_bank(t), ACT.Exp,
                               bias=NMX[:, t % 2:t % 2 + 1],
                               accum_out=RS[:, t % 4:t % 4 + 1]).then_inc(s["a_exp"], 1)

            def et_hi(b, t):
                h, i = t // 4, t % 4
                et = ETH[:, :].rearrange("p (h j n) -> p h j n", h=2, j=TILES)
                for k in range(2):
                    act.wait_ge(s["p_tr"], 2 * (TILES * b + t) + k + 1)
                    act.activation(et[:, h, 4 * k:4 * k + 4, i * P:(i + 1) * P],
                                   bank(ET_BANK + k).rearrange("p (j n) -> p j n", j=4),
                                   ACT.Copy).then_inc(s["a_hi"], 1)

            def misc_hi(dst, done, n, out_sem):
                act.wait_ge(s[done], n)
                act.activation(dst, bank(MISC_BANK).rearrange("p (j n) -> p j n", j=4), ACT.Copy)\
                    .then_inc(s[out_sem], 1)

            def image(b, cur, prev, nxt):
                p = b - 1
                if cur:
                    if not prev:
                        act.wait_ge(s["v_bqs"], 1)
                    project_hi(QH, 0, BQS[:, 0:1], "p_q", "a_qh", b)
                    project_hi(KH, N, VEC[:, 3:4], "p_k", "a_kh", b)
                for t in range(TILES):
                    if prev and t == 0:
                        et_hi(p, 6)
                    if cur and t >= 2:
                        et_hi(b, t - 2)
                    if prev and t == 1:
                        et_hi(p, 7)
                    if cur:
                        exp(b, t)
                    if nxt and t == TILES - 1:
                        hn_hi(b + 1)
                    if prev:
                        if t == 2:
                            misc_hi(XTH[:, 0:4, :], "p_xt", 2 * p + 1, "a_xh")
                    if cur:
                        if t == 4:
                            misc_hi(VH[:, 0:4, :], "p_v", 2 * b + 1, "a_vh")
                        if t == 5:
                            misc_hi(VH[:, 4:8, :], "p_v", 2 * b + 2, "a_vh")
                    if prev:
                        if t == 6:
                            misc_hi(XTH[:, 4:8, :], "p_xt", 2 * p + 2, "a_xh")
                        if t == 7:
                            act.wait_ge(s["p_u"], p + 1)
                            act.activation(R[:, bass.ds(p * UR, UR)], bank(MISC_BANK, UR), ACT.Copy)\
                                .then_inc(s["a_ur"], 1)

            attention(image, act)

            act.wait_ge(s["v_m2"], 2)
            act.activation(T[:, 600:600 + B * NF], T[:, 400:400 + B * NF], ACT.Sqrt).then_inc(s["a_mag"], 1)
            act.wait_ge(s["v_ml"], 9)
            act.activation(ML[:, 10, :], ML[:, 9, :], ACT.Sqrt).then_inc(s["a_ml"], 1)
            act.wait_ge(s["v_ml"], 14)
            act.activation(ML[:, 15, :], ML[:, 14, :], ACT.Sqrt, scale=0.5, bias=0.5)\
                .then_inc(s["a_ml"], 1)
            act.activation(ML[:, 24, :], ML[:, 2, :], ACT.Exp).then_inc(s["a_ml"], 1)
            act.wait_ge(s["v_ml"], 34)
            act.activation(ML[:, 28, :], ML[:, 27, :], ACT.Exp, scale=-1.0).then_inc(s["a_ml"], 1)
            act.wait_ge(s["d_syn"], 16)
            act.activation(SYH, SYN[:], ACT.Copy).then_inc(s["a_sh"], 1)

            def kernel_hi(n):
                act.wait_ge(s["v_k"], 1)
                if isinstance(n, int) is False or n:
                    act.wait_ge(s["p_kh"], 2 * n)
                act.activation(KBH[0:NK, :], K[:, bass.ds(n, 1)].broadcast_to([NK, P]), ACT.Copy)\
                    .then_inc(s["a_kbh"], 1)
                act.wait_ge(s["v_gf"], n + 1)
                if isinstance(n, int) is False or n:
                    act.wait_ge(s["p_vt"], n)
                act.activation(GH[0:CH, :], GF[0:CH, :], ACT.Copy).then_inc(s["a_gh"], 1)

            def khat_copy(n, h):
                act.wait_ge(s["p_kh"], 2 * n + h + 1)
                if isinstance(n, int) is False or n:
                    act.wait_ge(s["g_kx"], 2 * n + h - 1)
                act.activation(KHAT[:, h * HALF:(h + 1) * HALF], bank(2 + h), ACT.Copy)\
                    .then_inc(s["a_kh2"], 1)

            def copy(dst, src, done, n, out_sem):
                act.wait_ge(s[done], n)
                act.activation(dst, src, ACT.Copy).then_inc(s[out_sem], 1)

            def z_hi(b, h):
                d_ = slice(h * HALF, (h + 1) * HALF)
                copy(ZH[:, d_], ZF[:, d_], "v_z", 2 * b + h + 1, "a_zh")

            def rt_hi(n):
                copy(RTH[0:CH, :], bank(4, HALF, CH), "p_rt", n + 1, "a_rth")

            def r3_copy(n):
                copy(R3S, bank(5, P, NK), "p_r3", n + 1, "a_r3")

            def v3_hi(n):
                copy(V3H[0:NK, :], PS[0:NK, 5 * HALF + P:5 * HALF + 2 * P], "p_v3", n + 1, "a_v3h")

            def vt_hi(n):
                copy(VTH[0:CH, :], bank(6, HALF, CH), "p_vt", n + 1, "a_vth")

            def front(n):
                kernel_hi(n)
                rt_hi(n)
                r3_copy(n)
                v3_hi(n)
                khat_copy(n, 0)
                vt_hi(n)
                khat_copy(n, 1)

            def both(b, more):
                n = b + 1
                if more:
                    kernel_hi(n)
                    rt_hi(n)
                z_hi(b, 0)
                if more:
                    r3_copy(n)
                z_hi(b, 1)
                if more:
                    v3_hi(n)
                    khat_copy(n, 0)
                    vt_hi(n)
                    khat_copy(n, 1)

            synthesis(front, both, act)

        @block.vector
        def _(dve):
            TT, TS, STT = dve.tensor_tensor, dve.tensor_scalar, dve.scalar_tensor_tensor

            def stats(b):
                for h in range(2):
                    dve.bn_stats(STAT[:, b, 6 * h:6 * h + 6],
                                 X[:, b * N + h * HALF:b * N + (h + 1) * HALF]).then_inc(s["v_st"], 1)
                dve.wait_ge(s["v_st"], 3 * b + 2)
                dve.bn_aggr(MV[:, b, :], STAT[:, b, :]).then_inc(s["v_st"], 1)
                dve.wait_ge(s["v_st"], 3 * b + 3)

            gn = [0]

            def gn_step(ins):
                gn[0] += 1
                ins.then_inc(s["v_gn"], 1)
                dve.wait_ge(s["v_gn"], gn[0])

            def group_norm_means(cols):
                lo, hi = cols
                gn_step(dve.tensor_copy(GM[:, lo:hi], MV[:, lo:hi, 0]))

            def group_norm(cols, n):
                lo, hi = cols
                w = hi - lo
                gm, gv = bank(PV_BANK)[:, 256:256 + w], bank(PV_BANK)[:, 288:288 + w]
                dve.wait_ge(s["p_gn1"], n + 1)
                gn_step(TT(GM[:, lo:hi], gm, MV[:, lo:hi, 0], ALU.subtract))
                TT(GS[:, lo:hi], GM[:, lo:hi], GM[:, lo:hi], ALU.mult).then_inc(s["v_st"], 1)
                dve.wait_ge(s["v_st"], 3 * B + 2 if n else 4)
                gn_step(TT(GD[:, lo:hi], GS[:, lo:hi], MV[:, lo:hi, 1], ALU.add))
                dve.wait_ge(s["p_gn2"], n + 1)
                gn_step(TS(GS[:, lo:hi], gv, GN_EPS, None, ALU.add))
                dve.wait_ge(s["g_gn"], n + 1)
                gn_step(TS(GA[:, lo:hi], GD[:, lo:hi], VEC[:, 0:1], None, ALU.mult))
                TT(GS[:, lo:hi], GM[:, lo:hi], MV[:, lo:hi, 0], ALU.add).then_inc(s["v_bqs"], 1)
                dve.wait_ge(s["v_bqs"], 2 + 2 * n)
                TT(GS[:, lo:hi], GS[:, lo:hi], GA[:, lo:hi], ALU.mult).then_inc(s["v_bqs"], 1)
                dve.wait_ge(s["v_bqs"], 3 + 2 * n)
                gn_step(TS(GB[:, lo:hi], GS[:, lo:hi], -1.0, VEC[:, 1:2], ALU.mult, ALU.add))

            dve.wait_ge(s["d_x0"], 16)
            for h in range(2):
                dve.bn_stats(STAT[:, 0, 6 * h:6 * h + 6],
                             X[:, h * HALF:(h + 1) * HALF]).then_inc(s["v_st"], 1)
            dve.wait_ge(s["v_st"], 2)
            dve.bn_aggr(MV[:, 0, :], STAT[:, 0, :]).then_inc(s["v_st"], 1)
            dve.wait_ge(s["v_st"], 3)
            group_norm_means((0, 1))
            dve.wait_ge(s["p_wt"], 1)
            mb = bank(MISC_BANK)
            dve.tensor_copy(WPT, mb[:, 2 * P:3 * P]).then_inc(s["v_wpt"], 1)
            TS(WT[:, QI, :], mb[:, 0:P], SCALE, None, ALU.mult).then_inc(s["v_wt"], 1)
            dve.tensor_copy(WT[:, KI, :], mb[:, P:2 * P]).then_inc(s["v_wt"], 1)
            dve.tensor_copy(WT[:, RI_, :], mb[:, 3 * P:4 * P]).then_inc(s["v_wt"], 1)
            dve.wait_ge(s["p_bvp"], 1)
            dve.tensor_copy(WT[:, VI, :], bank(PV_BANK)[:, 0:P]).then_inc(s["v_wpv"], 1)
            dve.wait_ge(s["d_vec"], 16 * 6)
            TT(BVP[:], bank(PV_BANK)[:, P:P + 1], VEC[:, 5:6], ALU.add).then_inc(s["v_bvp"], 1)
            TS(BQS[:], VEC[:, 2:3], SCALE, None, ALU.mult).then_inc(s["v_bqs"], 1)
            group_norm((0, 1), 0)
            dve.wait_ge(s["a_wh"], 1)
            TT(WL[:], WT, WH[:].bitcast(F32), ALU.subtract).then_inc(s["v_wl"], 1)

            def hn(b):
                TS(T[:], X[:, bass.ds(b * N, N)], GA[:, bass.ds(b, 1)], GB[:, bass.ds(b, 1)],
                   ALU.mult, ALU.add).then_inc(s["v_t"], 1)

            hn(0)
            dve.wait_ge(s["v_bvp"], 1)

            def project_lo(dst, hi, base, bias, done, out_sem, b):
                for h in range(2):
                    d_ = slice(h * HALF, (h + 1) * HALF)
                    dve.wait_ge(s[done], 2 * b + h + 1)
                    STT(out=dst[:, d_], in0=PS[:, base + h * HALF:base + (h + 1) * HALF],
                        scalar=bias, in1=hi[:, d_].bitcast(F32), op0=ALU.add, op1=ALU.subtract)\
                        .then_inc(s[out_sem], 1)

            def row_max(b, t):
                dve.wait_ge(s["p_s"], TILES * b + t + 1)
                dve.tensor_reduce(NMX[:, t % 2:t % 2 + 1], s_bank(t), AX.X, ALU.max, negate=True)\
                    .then_inc(s["v_mx"], 1)

            def row_sum(b, t):
                dve.wait_ge(s["a_exp"], TILES * b + t + 1)
                dve.reciprocal(RI[:, t % 4:t % 4 + 1], RS[:, t % 4:t % 4 + 1])\
                    .then_inc(s["v_ri"], 1)

            def et_lo(b, t):
                h, i = t // 4, t % 4
                shape = dict(h=2, j=TILES)
                etl = ETL[:, :].rearrange("p (h j n) -> p h j n", **shape)
                eth = ETH[:, :].rearrange("p (h j n) -> p h j n", **shape)
                for k in range(2):
                    dve.wait_ge(s["a_hi"], 2 * (TILES * b + t) + k + 1)
                    part = (slice(None), h, slice(4 * k, 4 * k + 4), slice(i * P, (i + 1) * P))
                    TT(etl[part], bank(ET_BANK + k).rearrange("p (j n) -> p j n", j=4),
                       eth[part].bitcast(F32), ALU.subtract).then_inc(s["v_lo"], 1)

            def misc_lo(lo, hi, done, n, out_sem):
                dve.wait_ge(s[done], n)
                TT(lo, bank(MISC_BANK).rearrange("p (j n) -> p j n", j=4), hi.bitcast(F32),
                   ALU.subtract).then_inc(s[out_sem], 1)

            def residual(p, h):
                dve.wait_ge(s["p_pv"], 2 * p + h + 1)
                STT(out=T[:, h * HALF:(h + 1) * HALF], in0=bank(PV_BANK), scalar=BVP[:, 0:1],
                    in1=X[:, bass.ds(p * N + h * HALF, HALF)], op0=ALU.add, op1=ALU.add)\
                    .then_inc(s["v_x1"], 1)

            def image(b, cur, prev, nxt):
                p = b - 1
                if cur:
                    project_lo(QL, QH, 0, BQS[:, 0:1], "a_qh", "v_ql", b)
                    project_lo(KL, KH, N, VEC[:, 3:4], "a_kh", "v_kl", b)
                for t in range(TILES):
                    if prev and t == 0:
                        et_lo(p, 6)
                    if cur:
                        row_max(b, t)
                    if prev and t == 1:
                        et_lo(p, 7)
                    if cur and t >= 2:
                        et_lo(b, t - 2)
                    if cur:
                        if not prev and t in (1, 2, 3, 4):
                            if t == 1:
                                dve.wait_ge(s["d_xs"], 16 * (B - 1))
                            for i in range(2 * t - 1, min(2 * t + 1, B)):
                                stats_later(i)
                            if t == 4:
                                group_norm_means((1, B))
                        if nxt and t == TILES - 1:
                            if prev:
                                dve.wait_ge(s["g_x1"], 2 * p + 2)
                                dve.wait_ge(s["p_xt"], 2 * p + 2)
                            hn(b + 1)
                        row_sum(b, t)
                    if prev:
                        if t == 1:
                            residual(p, 0)
                        if t == 2:
                            misc_lo(XTL[:, 0:4, :], XTH[:, 0:4, :], "a_xh", 2 * p + 1, "v_xl")
                        if t == 5:
                            residual(p, 1)
                    if cur:
                        if t == 4:
                            misc_lo(VL[:, 0:4, :], VH[:, 0:4, :], "a_vh", 2 * b + 1, "v_vl")
                        if t == 5:
                            misc_lo(VL[:, 4:8, :], VH[:, 4:8, :], "a_vh", 2 * b + 2, "v_vl")
                            if not prev:
                                group_norm((1, B), 1)
                    if prev and t == 6:
                        misc_lo(XTL[:, 4:8, :], XTH[:, 4:8, :], "a_xh", 2 * p + 2, "v_xl")

            def stats_later(i):
                for h in range(2):
                    dve.bn_stats(STAT[:, i, 6 * h:6 * h + 6],
                                 X[:, i * N + h * HALF:i * N + (h + 1) * HALF])\
                        .then_inc(s["v_st"], 1)
                dve.wait_ge(s["v_st"], 3 * i + 3)
                dve.bn_aggr(MV[:, i, :], STAT[:, i, :]).then_inc(s["v_st"], 1)
                dve.wait_ge(s["v_st"], 3 * i + 4)

            attention(image, dve)

            dve.wait_ge(s["a_ur"], B + 1)
            dve.wait_ge(s["p_tr"], 2 * TILES * B)
            fr = R[:, :].rearrange("p (b u) -> p b u", b=B)[:, :, 2 * CH:2 * CH + 2 * NF]
            sq = T[:, 0:B * 2 * NF].rearrange("p (b u) -> p b u", b=B)
            dve.wait_ge(s["g_x1"], 2 * B)
            TT(sq, fr, fr, ALU.mult).then_inc(s["v_m2"], 1)
            dve.wait_ge(s["v_m2"], 1)
            TT(T[:, 400:400 + B * NF].rearrange("p (b u) -> p b u", b=B), sq[:, :, 0:NF],
               sq[:, :, NF:2 * NF], ALU.add).then_inc(s["v_m2"], 1)
            A, D = bank(6), bank(7)
            dve.wait_ge(s["d_mlp"], 16 * 4)
            dve.tensor_copy(W2R[:], W2[:, :].rearrange("p (j a) -> p j a", a=1)
                            .broadcast_to([HID, 3, NK])).then_inc(s["v_w2r"], 1)
            dve.wait_ge(s["p_c25"], 1)
            dve.tensor_copy(C25[:], A[0:NF, 0:B]).then_inc(s["v_c25"], 1)
            dve.wait_ge(s["p_cen"], 1)
            dve.tensor_copy(CEN[:], D[0:NK, 0:B]).then_inc(s["v_cen"], 1)
            dve.wait_ge(s["p_hid"], 1)
            TS(HIDV[:], A[0:HID, 32:32 + B], B1[:, 0:1], 0.0, ALU.add, ALU.max)\
                .then_inc(s["v_hid"], 1)
            ml = [0]

            def step(ins):
                ml[0] += 1
                ins.then_inc(s["v_ml"], 1)
                dve.wait_ge(s["v_ml"], ml[0])

            def m(i):
                return ML[:, i, :]

            dve.wait_ge(s["p_par"], 1)
            for j in range(3):
                step(TS(m(j), D[0:NK, 32 + j * B:32 + (j + 1) * B], B2[:, j:j + 1], None, ALU.add))
            step(STT(out=m(3), in0=m(0), scalar=-1.0, in1=m(0), op0=ALU.mult, op1=ALU.max))
            step(STT(out=m(4), in0=m(1), scalar=-1.0, in1=m(1), op0=ALU.mult, op1=ALU.max))
            step(TT(m(5), m(3), m(4), ALU.max))
            step(TS(m(6), m(5), 1e-36, None, ALU.is_lt))
            step(TS(m(5), m(5), 1e-36, None, ALU.max))
            dve.reciprocal(m(7), m(5)).then_inc(s["v_gn"], 1)
            dve.wait_ge(s["v_gn"], 13)
            TT(m(8), m(0), m(7), ALU.mult).then_inc(s["v_gn"], 1)
            TT(m(11), m(1), m(7), ALU.mult).then_inc(s["v_gn"], 1)
            dve.wait_ge(s["v_gn"], 15)
            TT(m(11), m(11), m(6), ALU.add).then_inc(s["v_gn"], 1)
            TT(m(12), m(8), m(8), ALU.mult).then_inc(s["v_gn"], 1)
            dve.wait_ge(s["v_gn"], 17)
            TT(m(13), m(11), m(11), ALU.mult).then_inc(s["v_gn"], 1)
            dve.wait_ge(s["v_gn"], 18)
            step(TT(m(9), m(12), m(13), ALU.add))
            dve.wait_ge(s["a_ml"], 1)
            step(dve.reciprocal(m(16), m(10)))
            step(TT(m(8), m(8), m(16), ALU.mult))
            step(TT(m(11), m(11), m(16), ALU.mult))
            step(TS(m(17), m(11), 0.0, None, ALU.is_ge))
            step(STT(out=m(14), in0=m(11), scalar=-1.0, in1=m(11), op0=ALU.mult, op1=ALU.max))
            dve.wait_ge(s["a_ml"], 2)
            step(dve.reciprocal(m(16), m(15)))
            step(STT(out=m(18), in0=m(8), scalar=-1.0, in1=m(8), op0=ALU.mult, op1=ALU.max))
            step(STT(out=m(18), in0=m(18), scalar=0.5, in1=m(16), op0=ALU.mult, op1=ALU.mult))
            step(TT(m(19), m(15), m(18), ALU.subtract))
            step(TT(m(20), m(19), m(17), ALU.mult))
            step(TT(m(20), m(20), m(18), ALU.add))
            step(TS(m(21), m(17), -1.0, 1.0, ALU.mult, ALU.add))
            step(TT(m(21), m(21), m(19), ALU.mult))
            step(TT(m(21), m(21), m(18), ALU.add))
            step(TS(m(22), m(8), 0.0, None, ALU.is_ge))
            step(TS(m(22), m(22), 2.0, -1.0, ALU.mult, ALU.add))
            step(TT(m(21), m(21), m(22), ALU.mult))
            x_, y_ = MISC[0:NK, M_XY:M_XY + 1], MISC[0:NK, M_XY + 1:M_XY + 2]
            step(TS(m(22), m(21), x_, None, ALU.mult))
            step(STT(out=m(22), in0=m(20), scalar=y_, in1=m(22), op0=ALU.mult, op1=ALU.subtract))
            step(TS(m(23), m(21), y_, None, ALU.mult))
            step(STT(out=m(23), in0=m(20), scalar=x_, in1=m(23), op0=ALU.mult, op1=ALU.add))
            dve.wait_ge(s["a_ml"], 3)
            lam = [0]

            def lam_step(ins):
                lam[0] += 1
                ins.then_inc(s["v_gn"], 1)
                dve.wait_ge(s["v_gn"], 18 + lam[0])

            lam_step(TS(m(25), m(24), KEPS, None, ALU.add))
            lam_step(dve.reciprocal(m(25), m(25)))
            for i in (24, 25):
                lam_step(STT(out=m(i), in0=m(i), scalar=2.0, in1=m(i), op0=ALU.mult, op1=ALU.mult))
                lam_step(dve.reciprocal(m(i), m(i)))
            step(TT(m(22), m(22), m(22), ALU.mult))
            step(TT(m(23), m(23), m(23), ALU.mult))
            lam_step(TT(m(22), m(22), m(24), ALU.mult))
            step(TT(m(23), m(23), m(25), ALU.mult))
            step(TT(m(27), m(22), m(23), ALU.add))
            dve.wait_ge(s["p_sum"], 1)
            lam_step(TS(m(29), A[0:NK, 64:64 + B], KEPS, None, ALU.add))
            lam_step(dve.reciprocal(m(29), m(29)))
            dve.wait_ge(s["a_ml"], 4)
            TT(K[:, 0:B], m(28), m(29), ALU.mult).then_inc(s["v_k"], 1)
            dve.wait_ge(s["p_kt"], 1)
            dve.tensor_copy(K[:, B:2 * B], D[0:NK, 128:128 + B]).then_inc(s["v_k"], 1)
            dve.wait_ge(s["p_g"], 1)
            for g in range(2):
                dve.tensor_copy(GC.rearrange("p (b c) -> p c b", b=B)[:, g * 2 * NZ:(g + 1) * 2 * NZ, :],
                                bank(5)[0:CH, 0:4 * NZ * B].rearrange("p (c b) -> p c b", b=2 * B)
                                [:, :, g * B:(g + 1) * B]).then_inc(s["v_g"], 1)
            dve.tensor_copy(G3C.rearrange("p (b c) -> p c b", b=B),
                            bank(4)[0:NK, 0:NK * B].rearrange("p (c b) -> p c b", b=B))\
                .then_inc(s["v_g"], 1)
            dve.wait_ge(s["v_g"], 3)
            dve.wait_ge(s["g_one"], 2)
            dve.wait_ge(s["v_k"], 1)

            def is_later(n):
                return not isinstance(n, int) or n > 0

            def lo(dst, full, hi, done, n, out_sem):
                dve.wait_ge(s[done], n)
                TT(dst, full, hi.bitcast(F32), ALU.subtract).then_inc(s[out_sem], 1)

            def kernel_prep(n):
                if is_later(n):
                    dve.wait_ge(s["v_gl"], n)
                gc = GC[:, bass.ds(n * 4 * NZ, 4 * NZ)]
                TT(GF[0:CH, :].rearrange("p (c w q) -> p c w q", c=4, w=16),
                   gc.rearrange("p (c a q) -> p c a q", c=4, a=1).broadcast_to([CH, 4, 16, NZ]),
                   MISC[0:CH, M_MASK:M_MASK + 16].rearrange("p (c w q) -> p c w q", c=1, q=1)
                   .broadcast_to([CH, 4, 16, NZ]), ALU.mult).then_inc(s["v_gf"], 1)
                if is_later(n):
                    dve.wait_ge(s["p_v3"], n)
                dve.tensor_copy(G3S[:, 0:NK], G3C[:, bass.ds(n * NK, NK)]).then_inc(s["v_g3s"], 1)
                lo(KBL[0:NK, :], K[:, bass.ds(n, 1)].broadcast_to([NK, P]), KBH[0:NK, :],
                   "a_kbh", n + 1, "v_kbl")
                dve.wait_ge(s["v_gf"], n + 1)
                lo(GL[0:CH, :], GF[0:CH, :], GH[0:CH, :], "a_gh", n + 1, "v_gl")

            def rt_lo(n):
                lo(RTL[0:CH, :], bank(4, HALF, CH), RTH[0:CH, :], "a_rth", n + 1, "v_rtl")

            def v3_lo(n):
                lo(V3L[0:NK, :], PS[0:NK, 5 * HALF + P:5 * HALF + 2 * P], V3H[0:NK, :],
                   "a_v3h", n + 1, "v_v3l")

            def vt_lo(n):
                lo(VTL[0:CH, :], bank(6, HALF, CH), VTH[0:CH, :], "a_vth", n + 1, "v_vtl")

            def z_sum(b, h):
                d_ = slice(h * HALF, (h + 1) * HALF)
                dve.wait_ge(s["p_z"], 2 * b + h + 1)
                dve.wait_ge(s["g_kx"], 2 * b + h + 1)
                if is_later(b):
                    dve.wait_ge(s["g_zl"], 2 * b + h - 1)
                TT(ZF[:, d_], bank(h), KX[:, d_], ALU.add).then_inc(s["v_z"], 1)

            def result(b, h):
                dve.wait_ge(s["p_o"], 2 * b + h + 1)
                xs = X[:, bass.ds(b * N + h * HALF, HALF)]
                TT(xs, bank(7), xs, ALU.add).then_inc(s["v_o"], 1)

            def front(n):
                kernel_prep(n)
                rt_lo(n)
                v3_lo(n)
                vt_lo(n)

            def both(b, more):
                n = b + 1
                if more:
                    kernel_prep(n)
                    rt_lo(n)
                z_sum(b, 0)
                z_sum(b, 1)
                if more:
                    v3_lo(n)
                result(b, 0)
                if more:
                    vt_lo(n)
                result(b, 1)

            synthesis(front, both, dve)

        @block.gpsimd
        def _(pool):
            TT = pool.tensor_tensor
            pool.memset(GP[:], -0.5).then_inc(s["g_one"], 1)
            pool.memset(G3S[:], 0.0).then_inc(s["g_one"], 1)
            pool.wait_ge(s["g_one"], 1)

            def rstd(cols, n):
                lo, hi = cols
                pool.wait_ge(s["v_gn"], 6 * n + 4)
                TT(GD[:, lo:hi], GS[:, lo:hi], GP[:, 0:1].broadcast_to([P, hi - lo]), ALU.pow)\
                    .then_inc(s["g_gn"], 1)

            def hn_lo(b):
                pool.wait_ge(s["a_hh"], b + 1)
                TT(HNL[:], T[:], HNH[:].bitcast(F32), ALU.subtract).then_inc(s["g_hl"], 1)

            rstd((0, 1), 0)
            hn_lo(0)
            pool.wait_ge(s["a_ah"], 1)
            TT(ANL[:], R[:, 0:UW], ANH[:].bitcast(F32), ALU.subtract).then_inc(s["g_al"], 1)

            def scale(b, t):
                pool.wait_ge(s["v_ri"], TILES * b + t + 1)
                e = E[:, (t % 4) * N:(t % 4 + 1) * N]
                TT(e, e, RI[:, t % 4:t % 4 + 1].broadcast_to([P, N]), ALU.mult)\
                    .then_inc(s["g_scl"], 1)

            def keep_x1(p, h):
                pool.wait_ge(s["v_x1"], 2 * p + h + 1)
                pool.tensor_copy(X[:, bass.ds(p * N + h * HALF, HALF)],
                                 T[:, h * HALF:(h + 1) * HALF]).then_inc(s["g_x1"], 1)

            def image(b, cur, prev, nxt):
                p = b - 1
                for t in range(TILES):
                    if cur:
                        scale(b, t)
                    if prev and t == 1:
                        keep_x1(p, 0)
                    if prev and t == 5:
                        keep_x1(p, 1)
                    if cur and not prev and t == 5:
                        rstd((1, B), 1)
                if nxt:
                    hn_lo(b + 1)

            attention(image, pool)
            pool.wait_ge(s["a_sh"], 1)
            TT(SYL, SYN[:], SYH.bitcast(F32), ALU.subtract).then_inc(s["g_sl"], 1)


            def rst(n):
                if isinstance(n, int) and n == 0:
                    pool.wait_ge(s["p_c25"], 1)
                else:
                    pool.wait_ge(s["p_rt"], n)
                pool.tensor_copy(RST[:, 0:2 * CH], R[:, bass.ds(n * UR, 2 * CH)])\
                    .then_inc(s["g_rst"], 1)
                pool.tensor_copy(RST[:, 2 * CH:4 * CH], R[:, bass.ds(n * UR + UA, 2 * CH)])\
                    .then_inc(s["g_rst"], 1)

            def k_x1(n, h):
                d_ = slice(h * HALF, (h + 1) * HALF)
                pool.wait_ge(s["a_kh2"], 2 * n + h + 1)
                if not isinstance(n, int) or n:
                    pool.wait_ge(s["v_z"], 2 * n + h - 1)
                TT(KX[:, d_], KHAT[:, d_], X[:, bass.ds(n * N + h * HALF, HALF)], ALU.mult)\
                    .then_inc(s["g_kx"], 1)

            def z_lo(b, h):
                d_ = slice(h * HALF, (h + 1) * HALF)
                pool.wait_ge(s["a_zh"], 2 * b + h + 1)
                TT(ZL[:, d_], ZF[:, d_], ZH[:, d_].bitcast(F32), ALU.subtract)\
                    .then_inc(s["g_zl"], 1)

            def front(n):
                rst(n)
                k_x1(n, 0)
                k_x1(n, 1)

            def both(b, more):
                n = b + 1
                if more:
                    rst(n)
                z_lo(b, 0)
                z_lo(b, 1)
                if more:
                    k_x1(n, 0)
                    k_x1(n, 1)

            synthesis(front, both, pool)


_ORDER = ["x", "L0_conv_norm_w", "L0_conv_norm_b", "L0_conv_wq", "L0_conv_bq", "L0_conv_wk",
          "L0_conv_bk", "L0_conv_wv", "L0_conv_bv", "L0_conv_wp", "L0_conv_bp", "L1_conv_w1",
          "L1_conv_b1", "L1_conv_w2", "L1_conv_b2", "L1_conv_wr"]


def kernel(**inputs):
    import concourse.bacc as bacc
    from concourse.bass_utils import run_bass_kernel_spmd

    nc = bacc.Bacc("TRN2", target_bir_lowering=False, num_devices=1)
    arrays, args = {}, []
    tables = shape_tables()
    named = [(n, np.ascontiguousarray(inputs[n])) for n in _ORDER] + list(tables.items())
    for name, a in named:
        arrays[f"in_{name}"] = a
        args.append(nc.dram_tensor(f"in_{name}", a.shape, mybir.dt.from_np(a.dtype),
                                   kind="ExternalInput").ap())
    out = nc.dram_tensor("out_0", (B, C, SIDE, SIDE), F32, kind="ExternalOutput").ap()
    attention_filter_kernel(nc, *args, out)
    r = run_bass_kernel_spmd(nc, [arrays], core_ids=[0])
    return r.results[0]["out_0"]
```

```python
from contextlib import ExitStack

import numpy as np

import concourse.bass as bass
from concourse import mybir

F32 = mybir.dt.float32
F32R = mybir.dt.float32r
ALU = mybir.AluOpType
ACT = mybir.ActivationFunctionType
AX = mybir.AxisListType

B, C, SIDE = 8, 128, 32
N = SIDE * SIDE
P = 128
HALF = 512
TILES = N // P
GROUPS = 16
GN_EPS = 1e-6
SCALE = float(C) ** -0.5
TAPS = 7
NK = TAPS * TAPS
KEPS = 1e-8
NZ = 7
CH = 16 * NZ
NF = (NK + 1) // 2
UA = 2 * CH + 2 * NF
UB = 4 * NZ
UR = UA + TILES * UB
UW = TILES * UA + UB
HID = 32
T_U1, T_U2, T_PR, T_EX, T_COS = 0, HALF, 2 * HALF, 2 * HALF + 2 * P, 2 * HALF + 2 * P + 2 * CH
T_END = T_COS + N


def shape_tables():
    h = np.arange(SIDE)
    z = np.stack([f(2 * np.pi * u * h / SIDE) for u in (13, 14, 15) for f in (np.cos, np.sin)]
                 + [np.cos(np.pi * h)], 1)
    z /= np.linalg.norm(z, axis=0)
    u = np.arange(-SIDE // 2, SIDE // 2)
    dft = np.exp(-2j * np.pi * np.outer(u, h) / SIDE) / np.sqrt(SIDE)
    r = TAPS // 2
    d = np.stack([np.exp(-2j * np.pi * a * h / SIDE) for a in range(-r, r + 1)])
    o = []
    for a in range(-r, r + 1):
        wrapped = np.zeros((SIDE, SIDE))
        for row in range(SIDE):
            if not 0 <= row + a < SIDE:
                wrapped[row, (row + a) % SIDE] = 1
        o.append(z.T @ (dft.conj().T @ wrapped @ dft) @ z)
    o = np.stack(o)
    taps = [(a, b) for a in range(TAPS) for b in range(TAPS)]
    eye = np.eye(P)

    ana = np.zeros((P, UW))
    centre = taps[:NF]
    for t in range(TILES):
        for hl in range(4):
            hh = 4 * t + hl
            for w in range(SIDE):
                row = hl * SIDE + w
                ana[row, t * UA + w * NZ:t * UA + (w + 1) * NZ] = z[hh]
                ph = np.array([2 * np.pi * ((a - r) * hh + (b - r) * w) / SIDE for a, b in centre])
                ana[row, t * UA + 2 * CH:t * UA + 2 * CH + NF] = np.cos(ph) / SIDE
                ana[row, t * UA + 2 * CH + NF:(t + 1) * UA] = -np.sin(ph) / SIDE
    for hl in range(4):
        for w in range(SIDE):
            ana[hl * SIDE + w, TILES * UA + hl * NZ:TILES * UA + (hl + 1) * NZ] = z[w]

    syn = np.zeros((P, T_END))
    for w in range(16):
        for q in range(NZ):
            syn[w * NZ + q, T_U1 + w:T_U1 + HALF:16] = -z[:, q]
            syn[w * NZ + q, T_U2 + w * SIDE:T_U2 + (w + 1) * SIDE] = -z[:, q]
    for c in range(2):
        for hl in range(16):
            for a in range(NZ):
                for q in range(NZ):
                    v = z[16 * c + hl, a]
                    syn[hl * NZ + q, T_PR + c * P + a * NZ + q] = v
                    syn[a * NZ + q, T_EX + c * CH + hl * NZ + q] = -v
    syn[:NK, T_COS:T_COS + N] = np.stack([np.outer(d[a], d[b]).real.ravel() for a, b in taps])

    g1 = np.stack([np.einsum("rs,w->swr", o[a], d[b]).real.reshape(NZ, -1) for a, b in taps])
    gam = g1.reshape(NK, NZ, 2, CH).transpose(0, 2, 1, 3).reshape(NK, -1)
    gam3 = np.stack([np.kron(o[a], o[b]).real for a, b in taps]).reshape(NK, -1)

    misc = np.zeros((P, M_END))
    c0 = 0
    misc[:, :P] = eye
    misc[:, P:2 * P] = np.kron(np.eye(GROUPS), np.full((C // GROUPS,) * 2, GROUPS / C))
    c0 = 2 * P
    for row in range(CH):
        misc[row, c0 + row // NZ] = 1
    c0 += 16
    for i in range(NK):
        misc[i, c0 + min(i, NK - 1 - i)] = 1
    c0 += NF
    for i, (a, b) in enumerate(taps):
        misc[i, c0:c0 + 2] = (b - r, a - r)
    c0 += 2
    misc[:, c0:c0 + NK] = 1
    c0 += NK
    misc[:, c0] = 1.0 / C
    c0 += 1
    for i, (a, b) in enumerate(taps):
        misc[b * TAPS + a, c0 + i] = 1
    f = np.float32
    return {"ana": ana.astype(f), "syn": syn.astype(f), "gam": gam.astype(f),
            "gam3": gam3.astype(f), "misc": misc.astype(f)}


M_EYE, M_AVG, M_MASK, M_SEL = 0, P, 2 * P, 2 * P + 16
M_XY = M_SEL + NF
M_ONES = M_XY + 2
M_MEAN = M_ONES + NK
M_TR = M_MEAN + 1
M_END = M_TR + NK
ML_P2, ML_P, ML_ABS, ML_BIG, ML_TINY, ML_RB = 0, 1, 3, 5, 6, 7
ML_S, ML_A, ML_SQ, ML_N2, ML_NR = 8, 10, 12, 14, 15
ML_M, ML_D, ML_GE, ML_SC, ML_SGN, ML_NN, ML_RN = 16, 17, 18, 20, 22, 23, 24
ML_UV, ML_LAM, ML_L2, ML_E, ML_K, ML_RS = 25, 27, 28, 29, 30, 31
GAM = 2 * NZ * CH


def attention_filter_kernel(nc, x, norm_w, norm_b, wq, bq, wk, bk, wv, bv, wp, bp, w1, b1, w2, b2,
                            wr, ana, syn, gam, gam3, misc, out):
    x_v = x.rearrange("b c h w -> b c (h w)")
    out_v = out.rearrange("b c h w -> c b (h w)")

    with ExitStack() as ctx:
        def sb(name, shape, dt=F32):
            return ctx.enter_context(nc.sbuf_tensor(name, shape, dt))

        def sem(name):
            return ctx.enter_context(nc.semaphore(name))

        X = sb("X", [P, B * N])
        T = sb("T", [P, N])
        HNH, HNL = sb("HNH", [P, N], F32R), sb("HNL", [P, N], F32R)
        QH, QL = sb("QH", [P, N], F32R), sb("QL", [P, N], F32R)
        KH, KL = sb("KH", [P, N], F32R), sb("KL", [P, N], F32R)
        VH, VL = sb("VH", [P, TILES, P], F32R), sb("VL", [P, TILES, P], F32R)
        E = sb("E", [P, 4 * N])
        ETH = sb("ETH", [P, 2 * TILES * HALF], F32R)
        ETL = sb("ETL", [P, 2 * TILES * HALF], F32R)
        XTH, XTL = sb("XTH", [P, TILES, P], F32R), sb("XTL", [P, TILES, P], F32R)
        R = sb("R", [P, B * UR])
        ANH, ANL = sb("ANH", [P, UW], F32R), sb("ANL", [P, UW], F32R)
        SYN = sb("SYN", [P, T_END])
        MISC = sb("MISC", [P, M_END])
        WRAW = E[:, 0:5 * P].rearrange("p (i c) -> p i c", i=5)
        WT = E[:, 5 * P:9 * P].rearrange("p (i c) -> p i c", i=4)
        WPT = E[:, 9 * P:10 * P]
        WH, WL = sb("WH", [P, 4, P], F32R), sb("WL", [P, 4, P], F32R)
        VEC = sb("VEC", [P, 6])
        BQS, BVP = sb("BQS", [P, 1]), sb("BVP", [P, 1])
        STAT = sb("STAT", [P, 12])
        MV = sb("MV", [P, 2])
        GM, GD, GS = sb("GM", [P, 1]), sb("GD", [P, 1]), sb("GS", [P, 1])
        GA, GB, GP = sb("GA", [P, 1]), sb("GB", [P, 1]), sb("GP", [P, 1])
        GP2, NR0 = sb("GP2", [P, 1]), sb("NR0", [P, 1])
        NMX, RS, RI = sb("NMX", [P, 2]), sb("RS", [P, 4]), sb("RI", [P, 4])
        W1, B1, W2 = sb("W1", [NK, HID]), sb("B1", [HID, 1]), sb("W2", [HID, 3])
        W2R, B2 = sb("W2R", [HID, 3, NK]), sb("B2", [NK, 3])
        C25, W1S, HIDV = sb("C25", [NF, B]), sb("W1S", [NF, HID]), sb("HIDV", [HID, B])
        ML = sb("ML", [NK, 33, B])
        MSQ, MS2 = T[:, 0:2 * B * NF], T[:, 2 * B * NF:3 * B * NF]
        MAB = T[:, 5 * P:5 * P + B * NF]
        K = sb("K", [NK, 2 * B])
        G3S = sb("G3S", [NK, P])
        PS = ctx.enter_context(nc.psum_tensor("PS", [P, 8 * HALF], F32))

        eye = MISC[:, M_EYE:M_EYE + P]
        avg = MISC[:, M_AVG:M_AVG + P]
        QI, KI, VI, RI_ = 0, 1, 2, 3

        def s_bank(t):
            return PS[:, (t % 2) * N:(t % 2 + 1) * N]

        def bank(i, n=HALF, parts=P):
            return PS[0:parts, i * HALF:i * HALF + n]
        ET_BANK, PV_BANK, MISC_BANK = 4, 6, 7
        MIX_BANK = (7, 5)

        at = [0]

        def carve(n):
            a = at[0]
            at[0] += n
            return ETH[:, a:a + n], ETL[:, a:a + n]
        SYH, SYL = carve(T_END)
        RTH, RTL = carve(4 * P)
        V3H, V3L = carve(P)
        VTH, VTL = carve(4 * P)
        GH, GL = carve(4 * CH)
        ZH, ZL = carve(N)
        KBH, KBL = carve(P)
        GAMS, GAM3S = E[0:NK, 0:GAM], E[0:NK, GAM:GAM + NK * NK]
        KHAT, KX, ZF, GF = E[:, 0:N], E[:, N:2 * N], E[:, 2 * N:3 * N], E[:, 3 * N:3 * N + 4 * CH]
        RST = T[:, 0:4 * P]
        R3S = T[0:NK, 4 * P:5 * P]
        GC = T[0:CH, 5 * P:5 * P + B * 4 * NZ]
        G3C = E[0:NK, 3 * N + 4 * CH:3 * N + 4 * CH + B * NK]

        names = """d_x0 d_xs d_w d_w2 d_vec d_misc d_ana d_syn d_mlp d_gam d_out
            p_wt p_bvp p_w1s v_w1s a_root p_gn1 p_gn2 v_wt v_wpt v_wpv v_bvp v_bqs v_wl a_wh v_st v_gn g_gn a_ah g_al v_w2r
            v_t a_hh v_hl g_hl p_q a_qh v_ql p_k a_kh v_kl p_s v_mx a_exp v_ri g_scl p_tr a_hi v_lo
            p_pv v_x1 g_x1 p_xt a_xh v_xl p_v a_vh v_vl p_u a_ur
            v_m2 a_mag p_c25 v_c25 p_hid v_hid p_par v_ml v_n2 a_nr a_lam v_ex a_ex p_sum v_k p_kt p_g g_one v_g g_sl a_sh
            g_rst p_rt a_rth v_rtl p_r3 a_r3 v_g3s p_v3 a_v3h v_v3l v_gf a_gh v_gl p_vt a_vth v_vtl
            a_kbh v_kbl p_kh a_kh2 g_kx p_z v_z a_zh g_zl p_o v_o""".split()
        s = {n: sem(n) for n in names}

        block = ctx.enter_context(nc.Block())

        def passes(hi1, lo1, hi2, lo2):
            return ((hi1, hi2), (hi1, lo2), (lo1, hi2))

        def attention(run, eng):
            run(0, True, False, True)
            with eng.Fori(1, B - 1) as b:
                run(b, True, True, True)
            run(B - 1, True, True, False)
            run(B, False, True, False)

        def synthesis(first, step, eng):
            first()
            step(0, 3)
            with eng.Fori(1, B - 3) as i:
                step(i, 3)
            for i in range(B - 3, B):
                step(i, B - 1 - i)

        def is_later(n):
            return not isinstance(n, int) or n > 0

        @block.sync
        def _(sp):
            sp.dma_start(MISC[:], misc).then_inc(s["d_misc"], 16)
            for i, w in ((0, wq), (1, wk), (4, wr)):
                sp.dma_start(WRAW[:, i, :], w).then_inc(s["d_w"], 16)
            sp.wait_ge(s["d_vec"], 16 * 6)
            sp.dma_start(R[:, 0:UW], ana).then_inc(s["d_ana"], 16)
            sp.dma_start(W1[:], w1).then_inc(s["d_mlp"], 16)
            sp.dma_start(B1[:], b1.rearrange("(c a) -> c a", a=1)).then_inc(s["d_mlp"], 16)
            sp.dma_start(W2[:], w2).then_inc(s["d_mlp"], 16)
            sp.dma_start(B2[:], b2.rearrange("(a c) -> a c", a=1).broadcast_to([NK, 3]))\
                .then_inc(s["d_mlp"], 16)
            for b in range(1, B):
                sp.dma_start(X[:, b * N:(b + 1) * N], x_v[b]).then_inc(s["d_xs"], 16)
            sp.dma_start(SYN[:], syn).then_inc(s["d_syn"], 16)
            sp.wait_ge(s["p_tr"], 2 * TILES * B)
            sp.dma_start(GAMS, gam).then_inc(s["d_gam"], 16)
            sp.dma_start(GAM3S, gam3).then_inc(s["d_gam"], 16)
            with sp.Fori(0, B) as b:
                sp.wait_ge(s["v_o"], 2 * b + 2)
                sp.dma_start(out_v[:, bass.ds(b, 1), :], X[:, bass.ds(b * N, N)])\
                    .then_inc(s["d_out"], 16)
            sp.wait_ge(s["d_out"], 16 * B)

        @block.tensor
        def _(pe):
            def mm(o, a, b_, start, stop):
                return pe.matmul(o, a, b_, start=start, stop=stop)

            pe.wait_ge(s["d_misc"], 16)

            def group_norm_mean(n, bk_):
                pe.wait_ge(s["v_st"], 3 * n + 3)
                mm(bank(bk_)[:, 256:257], avg, MV[:, 0:1], True, True).then_inc(s["p_gn1"], 1)

            def group_norm_variance(n, bk_):
                pe.wait_ge(s["v_gn"], 8 * n + 3)
                mm(bank(bk_)[:, 288:289], avg, GD[:], True, True).then_inc(s["p_gn2"], 1)

            group_norm_mean(0, PV_BANK)
            pe.wait_ge(s["d_w"], 16 * 3)
            pe.wait_ge(s["d_w2"], 16 * 2)
            for slot, i in enumerate((0, 1, 3, 4)):
                ins = pe.transpose(bank(MISC_BANK)[:, slot * P:(slot + 1) * P], WRAW[:, i, :], eye)
            ins.then_inc(s["p_wt"], 1)
            group_norm_variance(0, PV_BANK)
            pe.wait_ge(s["v_wpt"], 1)
            pe.wait_ge(s["v_gn"], 4)
            pe.wait_ge(s["d_vec"], 16 * 6)
            mm(bank(PV_BANK)[:, 0:P], WRAW[:, 2, :], WPT, True, True)
            mm(bank(PV_BANK)[:, P:P + 1], WPT, VEC[:, 4:5], True, True).then_inc(s["p_bvp"], 1)

            def project(w, bias_sem, base):
                for h in range(2):
                    o = PS[:, base + h * HALF:base + (h + 1) * HALF]
                    for n, (a, r) in enumerate(passes(WH[:, w, :], WL[:, w, :],
                                                      HNH[:, h * HALF:(h + 1) * HALF],
                                                      HNL[:, h * HALF:(h + 1) * HALF])):
                        ins = mm(o, a, r, n == 0, n == 2)
                    ins.then_inc(s[bias_sem], 1)

            def scores(b, t):
                q0 = slice(t * P, (t + 1) * P)
                for n, (a, r) in enumerate(passes(QH[:, q0], QL[:, q0], KH, KL)):
                    for h in range(2):
                        ins = mm(s_bank(t)[:, h * HALF:(h + 1) * HALF], a,
                                 r[:, h * HALF:(h + 1) * HALF], n == 0, n == 2)
                ins.then_inc(s["p_s"], 1)

            def transposes(b, t, after_first=True):
                pe.wait_ge(s["g_scl"], TILES * b + t + 1)
                for k in range(2):
                    if after_first:
                        pe.wait_ge(s["v_lo"], 2 * (TILES * b + t) + k - 1)
                    for j in range(4):
                        c0 = (t % 4) * N + (4 * k + j) * P
                        ins = pe.transpose(bank(ET_BANK + k)[:, j * P:(j + 1) * P],
                                           E[:, c0:c0 + P], eye)
                    ins.then_inc(s["p_tr"], 1)

            def values(b, h, c, first=False):
                if c == 0:
                    pe.wait_ge(s["v_lo"], 16 * b + 8 * h + 8)
                    if not first:
                        pe.wait_ge(s["v_x1"], 2 * b + h)
                if h == 0 and c == 0:
                    pe.wait_ge(s["v_vl"], 2 * b + 1)
                if h == 0 and c == 2:
                    pe.wait_ge(s["v_vl"], 2 * b + 2)
                for j in (2 * c, 2 * c + 1):
                    e0 = (h * TILES + j) * HALF
                    for n, (a, r) in enumerate(passes(VH[:, j, :], VL[:, j, :],
                                                      ETH[:, e0:e0 + HALF], ETL[:, e0:e0 + HALF])):
                        ins = mm(bank(PV_BANK), a, r, j == 0 and n == 0, j == TILES - 1 and n == 2)
                if c == 3:
                    ins.then_inc(s["p_pv"], 1)

            def x1_transposes(p, h):
                pe.wait_ge(s["v_x1"], 2 * p + h + 1)
                for j in range(4):
                    c0 = h * HALF + j * P
                    ins = pe.transpose(bank(MISC_BANK)[:, j * P:(j + 1) * P], T[:, c0:c0 + P], eye)
                ins.then_inc(s["p_xt"], 1)

            def project_v(b, h):
                for j in range(4):
                    t0 = (4 * h + j) * P
                    for n, (a, r) in enumerate(passes(HNH[:, t0:t0 + P], HNL[:, t0:t0 + P],
                                                      WH[:, VI, :], WL[:, VI, :])):
                        ins = mm(bank(MISC_BANK)[:, j * P:(j + 1) * P], a, r, n == 0, n == 2)
                ins.then_inc(s["p_v"], 1)

            def analysis(p):
                pe.wait_ge(s["v_xl"], 2 * p + 2)
                pe.wait_ge(s["g_al"], 1)
                rows = slice(TILES * UA, UW)

                def in_tile(t):
                    o = bank(MISC_BANK)[:, UA + t * UB:UA + (t + 1) * UB]
                    for n, (a, r) in enumerate(passes(XTH[:, t, :], XTL[:, t, :],
                                                      ANH[:, rows], ANL[:, rows])):
                        ins = mm(o, a, r, n == 0, n == 2)
                    return ins

                for t in range(TILES // 2):
                    in_tile(t)
                for t in range(TILES):
                    cols = slice(t * UA, (t + 1) * UA)
                    for n, (a, r) in enumerate(passes(XTH[:, t, :], XTL[:, t, :],
                                                      ANH[:, cols], ANL[:, cols])):
                        mm(bank(MISC_BANK)[:, 0:UA], a, r, t == 0 and n == 0,
                           t == TILES - 1 and n == 2)
                for t in range(TILES // 2, TILES):
                    ins = in_tile(t)
                ins.then_inc(s["p_u"], 1)

            def image(b, cur, prev, nxt):
                p = b - 1
                if cur:
                    if prev:
                        pe.wait_ge(s["g_hl"], b)
                    else:
                        pe.wait_ge(s["v_hl"], 1)
                    if prev:
                        pe.wait_ge(s["a_exp"], TILES * b - 1)
                    else:
                        pe.wait_ge(s["v_wl"], 1)
                    project(QI, "p_q", 0)
                    if prev:
                        pe.wait_ge(s["a_exp"], TILES * b)
                    project(KI, "p_k", N)
                for t in range(TILES):
                    if cur:
                        if t == 0:
                            if prev:
                                transposes(p, 6)
                                values(p, 0, 2)
                            pe.wait_ge(s["v_kl"], 2 * b + 2)
                        if t >= 2:
                            pe.wait_ge(s["a_exp"], TILES * b + t - 1)
                        scores(b, t)
                        if t >= 2:
                            transposes(b, t - 2, after_first=prev or t > 2)
                        if nxt and t == 4:
                            group_norm_variance(b + 1, MISC_BANK)
                    if prev:
                        if t == 0 and not cur:
                            transposes(p, 6)
                            values(p, 0, 2)
                        if t == 1:
                            transposes(p, 7)
                            values(p, 0, 3)
                        if t == 2:
                            values(p, 1, 0)
                            if cur:
                                pe.wait_ge(s["a_ur"], b)
                            else:
                                pe.wait_ge(s["a_ur"], b)
                            x1_transposes(p, 0)
                        if t == 3:
                            values(p, 1, 1)
                            if nxt:
                                pe.wait_ge(s["v_xl"], 2 * p + 1)
                                group_norm_mean(b + 1, MISC_BANK)
                        if t == 4:
                            values(p, 1, 2)
                        if t == 5:
                            values(p, 1, 3)
                    if cur:
                        if t == 3 and not prev:
                            group_norm_mean(1, MISC_BANK)
                        if t == 4:
                            if nxt:
                                pe.wait_ge(s["v_gn"], 8 * b + 12)
                            else:
                                pe.wait_ge(s["v_xl"], 2 * p + 1)
                            project_v(b, 0)
                        if t == 5:
                            pe.wait_ge(s["v_vl"], 2 * b + 1)
                            project_v(b, 1)
                    if t == 6:
                        if prev:
                            if cur:
                                pe.wait_ge(s["v_vl"], 2 * b + 2)
                            else:
                                pe.wait_ge(s["v_xl"], 2 * p + 1)
                            x1_transposes(p, 1)
                        if cur:
                            if not prev:
                                pe.wait_ge(s["d_mlp"], 16 * 4)
                                mm(bank(PV_BANK)[0:NF, 320:320 + HID],
                                   MISC[0:NK, M_SEL:M_SEL + NF], W1[:], True, True)\
                                    .then_inc(s["p_w1s"], 1)
                                pe.wait_ge(s["v_w1s"], 1)
                            values(b, 0, 0, first=not prev)
                    if t == 7:
                        if prev:
                            analysis(p)
                        if cur:
                            values(b, 0, 1)

            attention(image, pe)

            A, D = bank(6), bank(7)
            pe.wait_ge(s["a_mag"], 1)
            for b in range(B):
                ins = mm(A[0:NF, b:b + 1], MAB[:, b * NF:(b + 1) * NF],
                         MISC[:, M_MEAN:M_MEAN + 1], True, True)
            ins.then_inc(s["p_c25"], 1)
            pe.wait_ge(s["v_c25"], 1)
            mm(D[0:HID, 0:B], W1S[:], C25[:], True, True).then_inc(s["p_hid"], 1)
            pe.wait_ge(s["v_hid"], 1)
            for j in range(3):
                ins = mm(A[0:NK, 32 + j * B:32 + (j + 1) * B], W2R[:, j, :], HIDV[:], True, True)
            ins.then_inc(s["p_par"], 1)

            def rt(n, again):
                pe.wait_ge(s["g_rst"], 2 * n + 2)
                if again:
                    pe.wait_ge(s["v_rtl"], n)
                for i in range(4):
                    ins = pe.transpose(bank(4)[0:CH, i * P:(i + 1) * P],
                                       RST[:, i * CH:(i + 1) * CH], eye)
                ins.then_inc(s["p_rt"], 1)

            def r3(n, mixed=True):
                pe.wait_ge(s["v_rtl"], n + 1)
                if mixed:
                    pe.wait_ge(s["v_o"], 2 * n - 2)
                m = 0
                for c in range(2):
                    w = slice(T_PR + c * P, T_PR + (c + 1) * P)
                    d_ = slice((2 + c) * P, (3 + c) * P)
                    for a, r in passes(SYH[0:CH, w], SYL[0:CH, w], RTH[0:CH, d_], RTL[0:CH, d_]):
                        ins = mm(bank(5)[:, 0:P], a, r, m == 0, m == 5)
                        m += 1
                ins.then_inc(s["p_r3"], 1)

            def v3(n):
                pe.wait_ge(s["a_r3"], n + 1)
                pe.wait_ge(s["v_g3s"], n + 1)
                mm(bank(5)[:, P:2 * P], G3S[:], R3S, True, True).then_inc(s["p_v3"], 1)

            def vt(n):
                pe.wait_ge(s["v_v3l"], n + 1)
                pe.wait_ge(s["v_gl"], n + 1)
                for i in range(4):
                    d_ = slice(i * P, (i + 1) * P)
                    g = slice(i * CH, (i + 1) * CH)
                    jobs = list(passes(GH[0:CH, g], GL[0:CH, g], RTH[0:CH, d_], RTL[0:CH, d_]))
                    if i >= 2:
                        w = slice(T_EX + (i - 2) * CH, T_EX + (i - 1) * CH)
                        jobs += passes(SYH[0:NK, w], SYL[0:NK, w], V3H[0:NK, :], V3L[0:NK, :])
                    for m, (a, r) in enumerate(jobs):
                        ins = mm(bank(6)[0:CH, d_], a, r, m == 0, m == len(jobs) - 1)
                ins.then_inc(s["p_vt"], 1)

            def khat(n, h, again):
                if h == 0:
                    pe.wait_ge(s["v_kbl"], n + 1)
                if again:
                    pe.wait_ge(s["a_kh2"], 2 * n + h - 1)
                w = slice(T_COS + h * HALF, T_COS + (h + 1) * HALF)
                for m, (a, r) in enumerate(passes(KBH[0:NK, :], KBL[0:NK, :],
                                                  SYH[0:NK, w], SYL[0:NK, w])):
                    ins = mm(bank(2 + h), a, r, m == 0, m == 2)
                ins.then_inc(s["p_kh"], 1)

            def z(b, h):
                pe.wait_ge(s["v_vtl"], b + 1)
                jobs = []
                d_ = slice((2 + h) * P, (3 + h) * P)
                for a, r in passes(VTH[0:CH, d_], VTL[0:CH, d_], SYH[0:CH, T_U2:T_U2 + HALF],
                                   SYL[0:CH, T_U2:T_U2 + HALF]):
                    jobs.append((bank(h), a, r))
                w = slice(T_U1 + h * 256, T_U1 + (h + 1) * 256)
                grid = bank(h).rearrange("c (h w) -> c h w", w=SIDE)
                for i in range(2):
                    d_ = slice(i * P, (i + 1) * P)
                    for a, r in passes(VTH[0:CH, d_], VTL[0:CH, d_], SYH[0:CH, w], SYL[0:CH, w]):
                        jobs.append((grid[:, :, 16 * i:16 * (i + 1)], a,
                                     r.rearrange("c (h w) -> c h w", w=16)))
                for m, (o, a, r) in enumerate(jobs):
                    ins = mm(o, a, r, m == 0, m == len(jobs) - 1)
                ins.then_inc(s["p_z"], 1)

            def mix(b, h):
                pe.wait_ge(s["g_zl"], 2 * b + h + 1)
                if is_later(b):
                    pe.wait_ge(s["v_o"], 2 * b + h - 1)
                d_ = slice(h * HALF, (h + 1) * HALF)
                for m, (a, r) in enumerate(passes(WH[:, RI_, :], WL[:, RI_, :], ZH[:, d_], ZL[:, d_])):
                    ins = mm(bank(MIX_BANK[h]), a, r, m == 0, m == 2)
                ins.then_inc(s["p_o"], 1)

            def kernel_and_borders():
                pe.wait_ge(s["a_ex"], 1)
                mm(A[0:NK, 64:64 + B], MISC[0:NK, M_ONES:M_ONES + NK], ML[:, ML_K, :], True, True)\
                    .then_inc(s["p_sum"], 1)
                pe.wait_ge(s["v_k"], 1)
                pe.wait_ge(s["d_gam"], 32)
                mm(D[0:NK, 128:128 + B], MISC[0:NK, M_TR:M_TR + NK], K[:, 0:B], True, True)\
                    .then_inc(s["p_kt"], 1)
                for i in range(NK):
                    mm(bank(4)[0:NK, i * B:(i + 1) * B], GAM3S[:, i * NK:(i + 1) * NK],
                       K[:, 0:B], True, True)
                pe.wait_ge(s["v_k"], 2)
                pe.wait_ge(s["a_r3"], 1)
                for i in range(2 * NZ):
                    ins = mm(bank(5)[0:CH, i * 2 * B:(i + 1) * 2 * B],
                             GAMS[:, i * CH:(i + 1) * CH], K[:], True, True)
                ins.then_inc(s["p_g"], 1)

            def first():
                rt(0, False)
                r3(0, False)
                kernel_and_borders()
                khat(0, 0, False)
                pe.wait_ge(s["v_g"], 3)
                v3(0)
                khat(0, 1, False)
                vt(0)
                rt(1, True)

            def step(i, more):
                z(i, 0)
                if more:
                    r3(i + 1, is_later(i))
                z(i, 1)
                if more:
                    v3(i + 1)
                    khat(i + 1, 0, True)
                    khat(i + 1, 1, True)
                if more:
                    vt(i + 1)
                mix(i, 0)
                if more > 1:
                    rt(i + 2, True)
                mix(i, 1)

            synthesis(first, step, pe)

        @block.scalar
        def _(act):
            act.dma_start(X[:, 0:N], x_v[0]).then_inc(s["d_x0"], 16)
            for i, w in ((3, wp), (2, wv)):
                act.dma_start(WRAW[:, i, :], w).then_inc(s["d_w2"], 16)
            for i, v in enumerate((norm_w, norm_b, bq, bk, bv, bp)):
                act.dma_start(VEC[:, i:i + 1], v.rearrange("(c a) -> c a", a=1))\
                    .then_inc(s["d_vec"], 16)

            act.wait_ge(s["g_one"], 3)
            act.activation(NR0[:], GP2[:], ACT.Exp).then_inc(s["a_root"], 1)
            act.wait_ge(s["v_wpv"], 1)
            act.activation(WH[:], WT, ACT.Copy).then_inc(s["a_wh"], 1)

            def hn_hi(b):
                act.wait_ge(s["v_t"], b + 1)
                act.activation(HNH[:], T[:], ACT.Copy).then_inc(s["a_hh"], 1)

            hn_hi(0)
            act.wait_ge(s["d_ana"], 16)
            act.activation(ANH[:, 0:UA], R[:, 0:UA], ACT.Copy).then_inc(s["a_ur"], 1)
            act.activation(ANH[:, UA:UW], R[:, UA:UW], ACT.Copy).then_inc(s["a_ah"], 1)

            def project_hi(dst, base, bias, done, out_sem, b):
                for h in range(2):
                    act.wait_ge(s[done], 2 * b + h + 1)
                    act.activation(dst[:, h * HALF:(h + 1) * HALF],
                                   PS[:, base + h * HALF:base + (h + 1) * HALF], ACT.Identity,
                                   bias=bias).then_inc(s[out_sem], 1)

            def exp(b, t):
                act.wait_ge(s["v_mx"], TILES * b + t + 1)
                act.activation(E[:, (t % 4) * N:(t % 4 + 1) * N], s_bank(t), ACT.Exp,
                               bias=NMX[:, t % 2:t % 2 + 1],
                               accum_out=RS[:, t % 4:t % 4 + 1]).then_inc(s["a_exp"], 1)

            def et_hi(b, t):
                h, i = t // 4, t % 4
                et = ETH[:, :].rearrange("p (h j n) -> p h j n", h=2, j=TILES)
                for k in range(2):
                    act.wait_ge(s["p_tr"], 2 * (TILES * b + t) + k + 1)
                    act.activation(et[:, h, 4 * k:4 * k + 4, i * P:(i + 1) * P],
                                   bank(ET_BANK + k).rearrange("p (j n) -> p j n", j=4),
                                   ACT.Copy).then_inc(s["a_hi"], 1)

            def misc_hi(dst, done, n, out_sem):
                act.wait_ge(s[done], n)
                act.activation(dst, bank(MISC_BANK).rearrange("p (j n) -> p j n", j=4), ACT.Copy)\
                    .then_inc(s[out_sem], 1)

            def image(b, cur, prev, nxt):
                p = b - 1
                if not cur:
                    act.wait_ge(s["a_root"], 1)
                    act.activation(NR0[:], GP2[:], ACT.Sqrt).then_inc(s["a_root"], 1)
                if cur:
                    if not prev:
                        act.wait_ge(s["v_bqs"], 1)
                    project_hi(QH, 0, BQS[:, 0:1], "p_q", "a_qh", b)
                    project_hi(KH, N, VEC[:, 3:4], "p_k", "a_kh", b)
                for t in range(TILES):
                    if prev and t == 0:
                        et_hi(p, 6)
                    if cur and t >= 2:
                        et_hi(b, t - 2)
                    if prev and t == 1:
                        et_hi(p, 7)
                    if cur:
                        exp(b, t)
                    if nxt and t == (TILES - 1 if prev else TILES - 2):
                        hn_hi(b + 1)
                    if prev:
                        if t == 2:
                            misc_hi(XTH[:, 0:4, :], "p_xt", 2 * p + 1, "a_xh")
                    if cur:
                        if t == 4:
                            misc_hi(VH[:, 0:4, :], "p_v", 2 * b + 1, "a_vh")
                        if t == 5:
                            misc_hi(VH[:, 4:8, :], "p_v", 2 * b + 2, "a_vh")
                    if prev:
                        if t == 6:
                            misc_hi(XTH[:, 4:8, :], "p_xt", 2 * p + 2, "a_xh")
                            if not cur:
                                act.wait_ge(s["d_syn"], 16)
                                act.activation(SYH, SYN[:], ACT.Copy).then_inc(s["a_sh"], 1)
                        if t == 7:
                            act.wait_ge(s["p_u"], p + 1)
                            act.activation(R[:, bass.ds(p * UR, UR)], bank(MISC_BANK, UR), ACT.Copy)\
                                .then_inc(s["a_ur"], 1)

            attention(image, act)

            act.wait_ge(s["v_m2"], 2)
            act.activation(MAB, MS2, ACT.Sqrt).then_inc(s["a_mag"], 1)

            def k_hi(n):
                act.wait_ge(s["v_k"], 1)
                if is_later(n):
                    act.wait_ge(s["p_kh"], 2 * n)
                act.activation(KBH[0:NK, :], K[:, bass.ds(n, 1)].broadcast_to([NK, P]), ACT.Copy)\
                    .then_inc(s["a_kbh"], 1)

            def g_hi(n):
                act.wait_ge(s["v_gf"], n + 1)
                if is_later(n):
                    act.wait_ge(s["p_vt"], n)
                act.activation(GH[0:CH, :], GF[0:CH, :], ACT.Copy).then_inc(s["a_gh"], 1)

            def khat_copy(n, h):
                act.wait_ge(s["p_kh"], 2 * n + h + 1)
                if is_later(n):
                    act.wait_ge(s["g_kx"], 2 * n + h - 1)
                act.activation(KHAT[:, h * HALF:(h + 1) * HALF], bank(2 + h), ACT.Copy)\
                    .then_inc(s["a_kh2"], 1)

            def copy(dst, src, done, n, out_sem):
                act.wait_ge(s[done], n)
                act.activation(dst, src, ACT.Copy).then_inc(s[out_sem], 1)

            def z_hi(b, h):
                d_ = slice(h * HALF, (h + 1) * HALF)
                copy(ZH[:, d_], ZF[:, d_], "v_z", 2 * b + h + 1, "a_zh")

            def rt_hi(n):
                copy(RTH[0:CH, :], bank(4, HALF, CH), "p_rt", n + 1, "a_rth")

            def r3_copy(n):
                copy(R3S, bank(5, P, NK), "p_r3", n + 1, "a_r3")

            def v3_hi(n):
                copy(V3H[0:NK, :], PS[0:NK, 5 * HALF + P:5 * HALF + 2 * P], "p_v3", n + 1, "a_v3h")

            def vt_hi(n):
                copy(VTH[0:CH, :], bank(6, HALF, CH), "p_vt", n + 1, "a_vth")

            def roots():
                act.wait_ge(s["v_n2"], 1)
                act.activation(ML[:, ML_NR, :], ML[:, ML_N2, :], ACT.Sqrt).then_inc(s["a_nr"], 1)
                act.activation(ML[:, ML_LAM, :], ML[:, ML_P2, :], ACT.Exp).then_inc(s["a_lam"], 1)

            def first():
                rt_hi(0)
                roots()
                r3_copy(0)
                act.wait_ge(s["v_ex"], 1)
                act.activation(ML[:, ML_K, :], ML[:, ML_E, :], ACT.Exp, scale=-1.0)\
                    .then_inc(s["a_ex"], 1)
                k_hi(0)
                g_hi(0)
                khat_copy(0, 0)
                v3_hi(0)
                khat_copy(0, 1)
                k_hi(1)
                vt_hi(0)
                rt_hi(1)

            def step(i, more):
                if more:
                    g_hi(i + 1)
                if more:
                    r3_copy(i + 1)
                z_hi(i, 0)
                if more:
                    v3_hi(i + 1)
                z_hi(i, 1)
                if more:
                    khat_copy(i + 1, 0)
                    khat_copy(i + 1, 1)
                if more > 1:
                    k_hi(i + 2)
                if more:
                    vt_hi(i + 1)
                if more > 1:
                    rt_hi(i + 2)

            synthesis(first, step, act)

        @block.vector
        def _(dve):
            TT, TS, STT = dve.tensor_tensor, dve.tensor_scalar, dve.scalar_tensor_tensor

            def stats(n):
                for h in range(2):
                    dve.bn_stats(STAT[:, 6 * h:6 * h + 6], X[:, bass.ds(n * N + h * HALF, HALF)])\
                        .then_inc(s["v_st"], 1)
                dve.wait_ge(s["v_st"], 3 * n + 2)

            def stats_end():
                dve.bn_aggr(MV[:], STAT[:]).then_inc(s["v_st"], 1)

            def group_norm_a(n, bk_):
                dve.wait_ge(s["p_gn1"], n + 1)
                TT(GM[:], bank(bk_)[:, 256:257], MV[:, 0:1], ALU.subtract).then_inc(s["v_gn"], 1)
                dve.wait_ge(s["v_gn"], 8 * n + 1)
                TT(GS[:], GM[:], GM[:], ALU.mult).then_inc(s["v_gn"], 1)
                dve.wait_ge(s["v_gn"], 8 * n + 2)
                TT(GD[:], GS[:], MV[:, 1:2], ALU.add).then_inc(s["v_gn"], 1)

            def group_norm_b(n, bk_):
                dve.wait_ge(s["p_gn2"], n + 1)
                TS(GS[:], bank(bk_)[:, 288:289], GN_EPS, None, ALU.add).then_inc(s["v_gn"], 1)

            def group_norm_c(n):
                dve.wait_ge(s["g_gn"], n + 1)
                TS(GA[:], GD[:], VEC[:, 0:1], None, ALU.mult).then_inc(s["v_gn"], 1)
                TT(GS[:], GM[:], MV[:, 0:1], ALU.add).then_inc(s["v_gn"], 1)
                dve.wait_ge(s["v_gn"], 8 * n + 6)
                TT(GS[:], GS[:], GA[:], ALU.mult).then_inc(s["v_gn"], 1)
                dve.wait_ge(s["v_gn"], 8 * n + 7)
                TS(GB[:], GS[:], -1.0, VEC[:, 1:2], ALU.mult, ALU.add).then_inc(s["v_gn"], 1)
                dve.wait_ge(s["v_gn"], 8 * n + 8)

            dve.wait_ge(s["d_x0"], 16)
            stats(0)
            stats_end()
            group_norm_a(0, PV_BANK)
            dve.wait_ge(s["p_wt"], 1)
            mb = bank(MISC_BANK)
            dve.tensor_copy(WPT, mb[:, 2 * P:3 * P]).then_inc(s["v_wpt"], 1)
            TS(WT[:, QI, :], mb[:, 0:P], SCALE, None, ALU.mult).then_inc(s["v_wt"], 1)
            dve.tensor_copy(WT[:, KI, :], mb[:, P:2 * P]).then_inc(s["v_wt"], 1)
            dve.tensor_copy(WT[:, RI_, :], mb[:, 3 * P:4 * P]).then_inc(s["v_wt"], 1)
            group_norm_b(0, PV_BANK)
            dve.wait_ge(s["p_bvp"], 1)
            dve.tensor_copy(WT[:, VI, :], bank(PV_BANK)[:, 0:P]).then_inc(s["v_wpv"], 1)
            dve.wait_ge(s["d_vec"], 16 * 6)
            TT(BVP[:], bank(PV_BANK)[:, P:P + 1], VEC[:, 5:6], ALU.add).then_inc(s["v_bvp"], 1)
            TS(BQS[:], VEC[:, 2:3], SCALE, None, ALU.mult).then_inc(s["v_bqs"], 1)
            group_norm_c(0)

            def hn(b):
                TS(T[:], X[:, bass.ds(b * N, N)], GA[:], GB[:],
                   ALU.mult, ALU.add).then_inc(s["v_t"], 1)

            hn(0)
            dve.wait_ge(s["a_wh"], 1)
            TT(WL[:], WT, WH[:].bitcast(F32), ALU.subtract).then_inc(s["v_wl"], 1)
            dve.wait_ge(s["a_hh"], 1)
            TT(HNL[:], T[:], HNH[:].bitcast(F32), ALU.subtract).then_inc(s["v_hl"], 1)
            dve.wait_ge(s["v_bvp"], 1)

            def project_lo(dst, hi, base, bias, done, out_sem, b):
                for h in range(2):
                    d_ = slice(h * HALF, (h + 1) * HALF)
                    dve.wait_ge(s[done], 2 * b + h + 1)
                    STT(out=dst[:, d_], in0=PS[:, base + h * HALF:base + (h + 1) * HALF],
                        scalar=bias, in1=hi[:, d_].bitcast(F32), op0=ALU.add, op1=ALU.subtract)\
                        .then_inc(s[out_sem], 1)

            def row_max(b, t):
                dve.wait_ge(s["p_s"], TILES * b + t + 1)
                dve.tensor_reduce(NMX[:, t % 2:t % 2 + 1], s_bank(t), AX.X, ALU.max, negate=True)\
                    .then_inc(s["v_mx"], 1)

            def row_sum(b, t):
                dve.wait_ge(s["a_exp"], TILES * b + t + 1)
                dve.reciprocal(RI[:, t % 4:t % 4 + 1], RS[:, t % 4:t % 4 + 1])\
                    .then_inc(s["v_ri"], 1)

            def et_lo(b, t):
                h, i = t // 4, t % 4
                shape = dict(h=2, j=TILES)
                etl = ETL[:, :].rearrange("p (h j n) -> p h j n", **shape)
                eth = ETH[:, :].rearrange("p (h j n) -> p h j n", **shape)
                for k in range(2):
                    dve.wait_ge(s["a_hi"], 2 * (TILES * b + t) + k + 1)
                    part = (slice(None), h, slice(4 * k, 4 * k + 4), slice(i * P, (i + 1) * P))
                    TT(etl[part], bank(ET_BANK + k).rearrange("p (j n) -> p j n", j=4),
                       eth[part].bitcast(F32), ALU.subtract).then_inc(s["v_lo"], 1)

            def misc_lo(lo, hi, done, n, out_sem):
                dve.wait_ge(s[done], n)
                TT(lo, bank(MISC_BANK).rearrange("p (j n) -> p j n", j=4), hi.bitcast(F32),
                   ALU.subtract).then_inc(s[out_sem], 1)

            def residual(p, h):
                dve.wait_ge(s["p_pv"], 2 * p + h + 1)
                STT(out=T[:, h * HALF:(h + 1) * HALF], in0=bank(PV_BANK), scalar=BVP[:, 0:1],
                    in1=X[:, bass.ds(p * N + h * HALF, HALF)], op0=ALU.add, op1=ALU.add)\
                    .then_inc(s["v_x1"], 1)

            def image(b, cur, prev, nxt):
                p = b - 1
                if cur:
                    project_lo(QL, QH, 0, BQS[:, 0:1], "a_qh", "v_ql", b)
                    project_lo(KL, KH, N, VEC[:, 3:4], "a_kh", "v_kl", b)
                for t in range(TILES):
                    if prev and t == 0:
                        et_lo(p, 6)
                    if nxt and t == 4:
                        group_norm_a(b + 1, MISC_BANK)
                    if cur:
                        row_max(b, t)
                    if nxt and t == 4:
                        group_norm_b(b + 1, MISC_BANK)
                    if prev and t == 1:
                        et_lo(p, 7)
                    if cur and t >= 2:
                        et_lo(b, t - 2)
                    if cur:
                        if nxt and t == (TILES - 1 if prev else TILES - 2):
                            if prev:
                                dve.wait_ge(s["g_x1"], 2 * p + 2)
                                dve.wait_ge(s["p_xt"], 2 * p + 2)
                            hn(b + 1)
                        if nxt and t == 2:
                            dve.wait_ge(s["d_xs"], 16 * (B - 1))
                            stats(b + 1)
                        row_sum(b, t)
                        if nxt:
                            if t == 2:
                                stats_end()
                            if t == 5:
                                group_norm_c(b + 1)
                    if prev:
                        if t == 1:
                            residual(p, 0)
                        if t == 2:
                            misc_lo(XTL[:, 0:4, :], XTH[:, 0:4, :], "a_xh", 2 * p + 1, "v_xl")
                        if t == 5:
                            residual(p, 1)
                    if cur:
                        if t == 4:
                            misc_lo(VL[:, 0:4, :], VH[:, 0:4, :], "a_vh", 2 * b + 1, "v_vl")
                        if t == 5:
                            misc_lo(VL[:, 4:8, :], VH[:, 4:8, :], "a_vh", 2 * b + 2, "v_vl")
                            if not prev:
                                dve.wait_ge(s["d_mlp"], 16 * 4)
                                dve.tensor_copy(W2R[:], W2[:, :].rearrange("p (j a) -> p j a", a=1)
                                                .broadcast_to([HID, 3, NK])).then_inc(s["v_w2r"], 1)
                                dve.wait_ge(s["p_w1s"], 1)
                                dve.tensor_copy(W1S[:], bank(PV_BANK)[0:NF, 320:320 + HID])\
                                    .then_inc(s["v_w1s"], 1)
                    if prev and t == 6:
                        misc_lo(XTL[:, 4:8, :], XTH[:, 4:8, :], "a_xh", 2 * p + 2, "v_xl")

            attention(image, dve)

            A, D = bank(6), bank(7)
            dve.wait_ge(s["a_ur"], B + 1)
            dve.wait_ge(s["g_x1"], 2 * B)
            fr = R[:, :].rearrange("p (b u) -> p b u", b=B)[:, :, 2 * CH:2 * CH + 2 * NF]
            sq = MSQ.rearrange("p (b u) -> p b u", b=B)
            TT(sq, fr, fr, ALU.mult).then_inc(s["v_m2"], 1)
            dve.wait_ge(s["v_m2"], 1)
            TT(MS2.rearrange("p (b u) -> p b u", b=B), sq[:, :, 0:NF], sq[:, :, NF:2 * NF], ALU.add)\
                .then_inc(s["v_m2"], 1)
            dve.wait_ge(s["p_c25"], 1)
            dve.tensor_copy(C25[:], A[0:NF, 0:B]).then_inc(s["v_c25"], 1)
            dve.wait_ge(s["p_hid"], 1)
            TS(HIDV[:], D[0:HID, 0:B], B1[:, 0:1], 0.0, ALU.add, ALU.max).then_inc(s["v_hid"], 1)

            ml = [0]

            def small(ins):
                ml[0] += 1
                ins.then_inc(s["v_ml"], 1)

            def settle():
                dve.wait_ge(s["v_ml"], ml[0])

            def m(i, n=1):
                return ML[:, i:i + n, :]

            def wide(i, n):
                return m(i).broadcast_to([NK, n, B])

            def params():
                dve.wait_ge(s["p_par"], 1)
                for j, row in enumerate((ML_P, ML_P + 1, ML_P2)):
                    small(TS(ML[:, row, :], A[0:NK, 32 + j * B:32 + (j + 1) * B], B2[:, j:j + 1],
                             None, ALU.add))
                settle()

            def mlp_kernel():
                small(STT(out=m(ML_ABS, 2), in0=m(ML_P, 2), scalar=-1.0, in1=m(ML_P, 2),
                          op0=ALU.mult, op1=ALU.max))
                settle()
                small(TT(m(ML_BIG), m(ML_ABS), m(ML_ABS + 1), ALU.max))
                settle()
                small(TS(m(ML_TINY), m(ML_BIG), 1e-36, None, ALU.is_lt))
                small(TS(m(ML_RB), m(ML_BIG), 1e-36, None, ALU.max))
                settle()
                small(dve.reciprocal(m(ML_RB), m(ML_RB)))
                settle()
                small(TT(m(ML_S, 4), m(ML_P, 4), wide(ML_RB, 4), ALU.mult))
                settle()
                p1 = ML[:, ML_S + 1:ML_S + 4:2, :]
                small(TT(p1, p1, wide(ML_TINY, 2), ALU.add))
                settle()
                small(TT(m(ML_SQ, 2), m(ML_S, 2), m(ML_S, 2), ALU.mult))
                settle()
                TT(m(ML_N2), m(ML_SQ), m(ML_SQ + 1), ALU.add).then_inc(s["v_n2"], 1)
                small(TS(m(ML_GE), m(ML_S + 1), 0.0, None, ALU.is_lt))
                small(TS(m(ML_GE + 1), m(ML_S + 1), 0.0, None, ALU.is_ge))
                small(TS(m(ML_SGN), m(ML_S), 0.0, None, ALU.is_ge))
                settle()
                small(TS(m(ML_SGN), m(ML_SGN), 2.0, -1.0, ALU.mult, ALU.add))
                dve.wait_ge(s["a_nr"], 1)
                small(TT(m(ML_M), m(ML_A + 1), m(ML_NR), ALU.add))
                settle()
                small(TT(m(ML_D), m(ML_M), m(ML_A), ALU.subtract))
                small(TT(m(ML_NN), m(ML_M), m(ML_M), ALU.mult))
                settle()
                small(TT(m(ML_SC, 2), m(ML_GE, 2), wide(ML_D, 2), ALU.mult))
                small(TT(m(ML_NN), m(ML_NN), m(ML_SQ), ALU.add))
                settle()
                small(TT(m(ML_SC, 2), m(ML_SC, 2), wide(ML_A, 2), ALU.add))
                small(dve.reciprocal(m(ML_RN), m(ML_NN)))
                settle()
                small(TT(m(ML_SC), m(ML_SC), m(ML_SGN), ALU.mult))
                settle()
                x_, y_ = MISC[0:NK, M_XY:M_XY + 1], MISC[0:NK, M_XY + 1:M_XY + 2]
                small(TS(m(ML_UV, 2), m(ML_SC, 2), x_, None, ALU.mult))
                dve.wait_ge(s["a_lam"], 1)
                small(TS(m(ML_L2), m(ML_LAM), KEPS, None, ALU.add))
                settle()
                small(STT(out=m(ML_UV), in0=m(ML_SC + 1), scalar=y_, in1=m(ML_UV), op0=ALU.mult,
                          op1=ALU.subtract))
                small(STT(out=m(ML_UV + 1), in0=m(ML_SC), scalar=y_, in1=m(ML_UV + 1),
                          op0=ALU.mult, op1=ALU.add))
                small(dve.reciprocal(m(ML_L2), m(ML_L2)))
                settle()
                small(STT(out=m(ML_LAM, 2), in0=m(ML_LAM, 2), scalar=2.0, in1=m(ML_LAM, 2),
                          op0=ALU.mult, op1=ALU.mult))
                small(TT(m(ML_UV, 2), m(ML_UV, 2), m(ML_UV, 2), ALU.mult))
                settle()
                small(dve.reciprocal(m(ML_LAM, 2), m(ML_LAM, 2)))
                small(TT(m(ML_UV, 2), m(ML_UV, 2), wide(ML_RN, 2), ALU.mult))
                settle()
                small(TT(m(ML_UV, 2), m(ML_UV, 2), m(ML_LAM, 2), ALU.mult))
                settle()
                TT(m(ML_E), m(ML_UV), m(ML_UV + 1), ALU.add).then_inc(s["v_ex"], 1)
                dve.wait_ge(s["p_sum"], 1)
                small(TS(ML[:, ML_RS, :], A[0:NK, 64:64 + B], KEPS, None, ALU.add))
                settle()
                small(dve.reciprocal(m(ML_RS), m(ML_RS)))
                settle()
                TT(K[:, 0:B], ML[:, ML_K, :], ML[:, ML_RS, :], ALU.mult).then_inc(s["v_k"], 1)
                dve.wait_ge(s["p_kt"], 1)
                dve.tensor_copy(K[:, B:2 * B], D[0:NK, 128:128 + B]).then_inc(s["v_k"], 1)

            def borders():
                dve.wait_ge(s["g_one"], 3)
                dve.wait_ge(s["p_g"], 1)
                for g in range(2):
                    dve.tensor_copy(GC.rearrange("p (b c) -> p c b", b=B)
                                    [:, g * 2 * NZ:(g + 1) * 2 * NZ, :],
                                    bank(5)[0:CH, 0:4 * NZ * B]
                                    .rearrange("p (c b) -> p c b", b=2 * B)
                                    [:, :, g * B:(g + 1) * B]).then_inc(s["v_g"], 1)
                dve.tensor_copy(G3C.rearrange("p (b c) -> p c b", b=B),
                                bank(4)[0:NK, 0:NK * B].rearrange("p (c b) -> p c b", b=B))\
                    .then_inc(s["v_g"], 1)
                dve.wait_ge(s["v_g"], 3)

            def lo(dst, full, hi, done, n, out_sem):
                dve.wait_ge(s[done], n)
                TT(dst, full, hi.bitcast(F32), ALU.subtract).then_inc(s[out_sem], 1)

            def g_full(n):
                if is_later(n):
                    dve.wait_ge(s["v_gl"], n)
                gc = GC[:, bass.ds(n * 4 * NZ, 4 * NZ)]
                TT(GF[0:CH, :].rearrange("p (c w q) -> p c w q", c=4, w=16),
                   gc.rearrange("p (c a q) -> p c a q", c=4, a=1).broadcast_to([CH, 4, 16, NZ]),
                   MISC[0:CH, M_MASK:M_MASK + 16].rearrange("p (c w q) -> p c w q", c=1, q=1)
                   .broadcast_to([CH, 4, 16, NZ]), ALU.mult).then_inc(s["v_gf"], 1)

            def g3_copy(n):
                if is_later(n):
                    dve.wait_ge(s["p_v3"], n)
                dve.tensor_copy(G3S[:, 0:NK], G3C[:, bass.ds(n * NK, NK)]).then_inc(s["v_g3s"], 1)

            def k_lo(n):
                lo(KBL[0:NK, :], K[:, bass.ds(n, 1)].broadcast_to([NK, P]), KBH[0:NK, :],
                   "a_kbh", n + 1, "v_kbl")

            def g_lo(n):
                dve.wait_ge(s["v_gf"], n + 1)
                lo(GL[0:CH, :], GF[0:CH, :], GH[0:CH, :], "a_gh", n + 1, "v_gl")

            def rt_lo(n):
                lo(RTL[0:CH, :], bank(4, HALF, CH), RTH[0:CH, :], "a_rth", n + 1, "v_rtl")

            def v3_lo(n):
                lo(V3L[0:NK, :], PS[0:NK, 5 * HALF + P:5 * HALF + 2 * P], V3H[0:NK, :],
                   "a_v3h", n + 1, "v_v3l")

            def vt_lo(n):
                lo(VTL[0:CH, :], bank(6, HALF, CH), VTH[0:CH, :], "a_vth", n + 1, "v_vtl")

            def z_sum(b, h):
                d_ = slice(h * HALF, (h + 1) * HALF)
                dve.wait_ge(s["p_z"], 2 * b + h + 1)
                dve.wait_ge(s["g_kx"], 2 * b + h + 1)
                if is_later(b):
                    dve.wait_ge(s["g_zl"], 2 * b + h - 1)
                TT(ZF[:, d_], bank(h), KX[:, d_], ALU.add).then_inc(s["v_z"], 1)

            def result(b, h):
                dve.wait_ge(s["p_o"], 2 * b + h + 1)
                xs = X[:, bass.ds(b * N + h * HALF, HALF)]
                TT(xs, bank(MIX_BANK[h]), xs, ALU.add).then_inc(s["v_o"], 1)

            def first():
                params()
                rt_lo(0)
                mlp_kernel()
                k_lo(0)
                borders()
                g_full(0)
                g3_copy(0)
                g_lo(0)
                v3_lo(0)
                g_full(1)
                g3_copy(1)
                k_lo(1)
                vt_lo(0)
                rt_lo(1)

            def step(i, more):
                z_sum(i, 0)
                if more:
                    g_lo(i + 1)
                z_sum(i, 1)
                if more:
                    v3_lo(i + 1)
                if more > 1:
                    g_full(i + 2)
                if more > 1:
                    g3_copy(i + 2)
                    k_lo(i + 2)
                if more:
                    vt_lo(i + 1)
                result(i, 0)
                if more > 1:
                    rt_lo(i + 2)
                result(i, 1)

            synthesis(first, step, dve)

        @block.gpsimd
        def _(pool):
            TT = pool.tensor_tensor
            pool.memset(GP[:], -0.5).then_inc(s["g_one"], 1)
            pool.memset(GP2[:], 1.0).then_inc(s["g_one"], 1)
            pool.memset(G3S[:], 0.0).then_inc(s["g_one"], 1)
            pool.wait_ge(s["g_one"], 1)

            def rstd(n):
                pool.wait_ge(s["v_gn"], 8 * n + 4)
                TT(GD[:], GS[:], GP[:], ALU.pow).then_inc(s["g_gn"], 1)

            def hn_lo(b):
                pool.wait_ge(s["a_hh"], b + 1)
                TT(HNL[:], T[:], HNH[:].bitcast(F32), ALU.subtract).then_inc(s["g_hl"], 1)

            rstd(0)
            pool.wait_ge(s["a_ah"], 1)
            TT(ANL[:], R[:, 0:UW], ANH[:].bitcast(F32), ALU.subtract).then_inc(s["g_al"], 1)

            def scale(b, t):
                pool.wait_ge(s["v_ri"], TILES * b + t + 1)
                e = E[:, (t % 4) * N:(t % 4 + 1) * N]
                TT(e, e, RI[:, t % 4:t % 4 + 1].broadcast_to([P, N]), ALU.mult)\
                    .then_inc(s["g_scl"], 1)

            def keep_x1(p, h):
                pool.wait_ge(s["v_x1"], 2 * p + h + 1)
                pool.tensor_copy(X[:, bass.ds(p * N + h * HALF, HALF)],
                                 T[:, h * HALF:(h + 1) * HALF]).then_inc(s["g_x1"], 1)

            def image(b, cur, prev, nxt):
                p = b - 1
                for t in range(TILES):
                    if cur:
                        scale(b, t)
                    if prev and t == 1:
                        keep_x1(p, 0)
                    if prev and t == 5:
                        keep_x1(p, 1)
                    if nxt and t == 4:
                        rstd(b + 1)
                    if nxt and not prev and t == 6:
                        hn_lo(b + 1)
                if nxt and prev:
                    hn_lo(b + 1)

            attention(image, pool)
            pool.wait_ge(s["a_sh"], 1)
            TT(SYL, SYN[:], SYH.bitcast(F32), ALU.subtract).then_inc(s["g_sl"], 1)


            def rst(n):
                if is_later(n):
                    pool.wait_ge(s["p_rt"], n)
                else:
                    pool.wait_ge(s["a_mag"], 1)
                pool.tensor_copy(RST[:, 0:2 * CH], R[:, bass.ds(n * UR, 2 * CH)])\
                    .then_inc(s["g_rst"], 1)
                pool.tensor_copy(RST[:, 2 * CH:4 * CH], R[:, bass.ds(n * UR + UA, 2 * CH)])\
                    .then_inc(s["g_rst"], 1)

            def k_x1(n, h):
                d_ = slice(h * HALF, (h + 1) * HALF)
                pool.wait_ge(s["a_kh2"], 2 * n + h + 1)
                if is_later(n):
                    pool.wait_ge(s["v_z"], 2 * n + h - 1)
                TT(KX[:, d_], KHAT[:, d_], X[:, bass.ds(n * N + h * HALF, HALF)], ALU.mult)\
                    .then_inc(s["g_kx"], 1)

            def z_lo(b, h):
                d_ = slice(h * HALF, (h + 1) * HALF)
                pool.wait_ge(s["a_zh"], 2 * b + h + 1)
                TT(ZL[:, d_], ZF[:, d_], ZH[:, d_].bitcast(F32), ALU.subtract)\
                    .then_inc(s["g_zl"], 1)

            def first():
                rst(0)
                rst(1)
                k_x1(0, 0)
                k_x1(0, 1)
                rst(2)

            def step(i, more):
                z_lo(i, 0)
                z_lo(i, 1)
                if more:
                    k_x1(i + 1, 0)
                    k_x1(i + 1, 1)
                if more > 2:
                    rst(i + 3)

            synthesis(first, step, pool)


_ORDER = ["x", "L0_conv_norm_w", "L0_conv_norm_b", "L0_conv_wq", "L0_conv_bq", "L0_conv_wk",
          "L0_conv_bk", "L0_conv_wv", "L0_conv_bv", "L0_conv_wp", "L0_conv_bp", "L1_conv_w1",
          "L1_conv_b1", "L1_conv_w2", "L1_conv_b2", "L1_conv_wr"]


def kernel(**inputs):
    import concourse.bacc as bacc
    from concourse.bass_utils import run_bass_kernel_spmd

    nc = bacc.Bacc("TRN2", target_bir_lowering=False, num_devices=1)
    arrays, args = {}, []
    tables = shape_tables()
    named = [(n, np.ascontiguousarray(inputs[n])) for n in _ORDER] + list(tables.items())
    for name, a in named:
        arrays[f"in_{name}"] = a
        args.append(nc.dram_tensor(f"in_{name}", a.shape, mybir.dt.from_np(a.dtype),
                                   kind="ExternalInput").ap())
    out = nc.dram_tensor("out_0", (B, C, SIDE, SIDE), F32, kind="ExternalOutput").ap()
    attention_filter_kernel(nc, *args, out)
    r = run_bass_kernel_spmd(nc, [arrays], core_ids=[0])
    return r.results[0]["out_0"]
```

```python
from contextlib import ExitStack

import numpy as np

import concourse.bass as bass
from concourse import mybir

F32 = mybir.dt.float32
F32R = mybir.dt.float32r
ALU = mybir.AluOpType
ACT = mybir.ActivationFunctionType
AX = mybir.AxisListType

B, C, SIDE = 8, 128, 32
N = SIDE * SIDE
P = 128
HALF = 512
TILES = N // P
GROUPS = 16
GN_EPS = 1e-6
SCALE = float(C) ** -0.5
TAPS = 7
NK = TAPS * TAPS
KEPS = 1e-8
NZ = 7
CH = 16 * NZ
NF = (NK + 1) // 2
UA = 2 * CH + 2 * NF
UB = 4 * NZ
UR = UA + TILES * UB
UO = CH
UE = (TILES - 2) * UA
UI = UE + UB + UA
UW = UI + UB + UA + UB
HID = 32
T_U1, T_U2, T_PR, T_EX, T_COS = 0, HALF, 2 * HALF, 2 * HALF + 2 * P, 2 * HALF + 2 * P + 2 * CH
T_END = T_COS + N
K_MID, K_LO, K_ROWS = 32, 64, 96
LO = 64
M_EYE, M_AVG, M_MASK, M_SEL = 0, P, 2 * P, 2 * P + 16
M_XY = M_SEL + K_ROWS
M_ONES = M_XY + 2
M_MEAN = M_ONES + NK
M_SELT = M_MEAN + 1
M_END = M_SELT + K_ROWS
ML_P2, ML_P = 0, 1
ML_ABS, ML_BIG = 3, 5
ML_TINY, ML_RB = 6, 7
ML_S, ML_A = 8, 10
ML_SQ, ML_N2, ML_NR = 12, 14, 15
ML_M, ML_D = 16, 17
ML_GE = 18
ML_SC, ML_SGN = 20, 22
ML_NN, ML_RN = 23, 24
ML_UV = 25
ML_LAM, ML_L2 = 27, 28
ML_E, ML_K, ML_RS = 29, 30, 31
ML_END = 32
GAM = 2 * NZ * CH


def shape_tables():
    h = np.arange(SIDE)
    z = np.stack([f(2 * np.pi * u * h / SIDE) for u in (13, 14, 15) for f in (np.cos, np.sin)]
                 + [np.cos(np.pi * h)], 1)
    z /= np.linalg.norm(z, axis=0)
    u = np.arange(-SIDE // 2, SIDE // 2)
    dft = np.exp(-2j * np.pi * np.outer(u, h) / SIDE) / np.sqrt(SIDE)
    r = TAPS // 2
    d = np.stack([np.exp(-2j * np.pi * a * h / SIDE) for a in range(-r, r + 1)])
    o = []
    for a in range(-r, r + 1):
        wrapped = np.zeros((SIDE, SIDE))
        for row in range(SIDE):
            if not 0 <= row + a < SIDE:
                wrapped[row, (row + a) % SIDE] = 1
        o.append(z.T @ (dft.conj().T @ wrapped @ dft) @ z)
    o = np.stack(o)
    taps = [(a, b) for a in range(TAPS) for b in range(TAPS)]

    ana = np.zeros((P, UW))
    centre = taps[:NF]
    for t in range(TILES):
        u0 = {0: UE + UB, TILES - 1: UI + UB}.get(t, (t - 1) * UA)
        for hl in range(4):
            hh = 4 * t + hl
            for w in range(SIDE):
                row = hl * SIDE + w
                ana[row, u0 + w * NZ:u0 + (w + 1) * NZ] = z[hh]
                ph = np.array([2 * np.pi * ((a - r) * hh + (b - r) * w) / SIDE for a, b in centre])
                ana[row, u0 + 2 * CH:u0 + 2 * CH + NF] = np.cos(ph) / SIDE
                ana[row, u0 + 2 * CH + NF:u0 + UA] = -np.sin(ph) / SIDE
    for hl in range(4):
        for w in range(SIDE):
            ana[hl * SIDE + w, UI + hl * NZ:UI + (hl + 1) * NZ] = z[w]

    syn = np.zeros((P, T_END))
    for w in range(16):
        for q in range(NZ):
            syn[w * NZ + q, T_U1 + w:T_U1 + HALF:16] = -z[:, q]
            syn[w * NZ + q, T_U2 + w * SIDE:T_U2 + (w + 1) * SIDE] = -z[:, q]
    for c in range(2):
        for hl in range(16):
            for a in range(NZ):
                for q in range(NZ):
                    v = z[16 * c + hl, a]
                    syn[hl * NZ + q, T_PR + c * P + a * NZ + q] = v
                    for half in (0, LO):
                        syn[half + a * NZ + q, T_EX + c * CH + hl * NZ + q] = -v
    for third in (0, K_MID, K_LO):
        syn[third:third + NF, T_COS:T_COS + N] = \
            np.stack([np.outer(d[a], d[b]).real.ravel() for a, b in centre])

    g1 = np.stack([np.einsum("rs,w->swr", o[a], d[b]).real.reshape(NZ, -1) for a, b in taps])
    g1 = g1.reshape(NK, NZ, 2, CH).transpose(0, 2, 1, 3).reshape(NK, -1)
    g3 = np.stack([np.kron(o[a], o[b]).real for a, b in taps]).reshape(NK, -1)
    g = np.concatenate([g1, g3], 1)
    g = ((g + g[::-1]) / 2)[:NF]
    gam = np.zeros((K_ROWS, GAM + NK * NK))
    for third in (0, K_MID, K_LO):
        gam[third:third + NF] = g

    misc = np.zeros((P, M_END))
    misc[:, M_EYE:M_EYE + P] = np.eye(P)
    misc[:, M_AVG:M_AVG + P] = np.kron(np.eye(GROUPS), np.full((C // GROUPS,) * 2, GROUPS / C))
    for row in range(CH):
        misc[row, M_MASK + row // NZ] = 1
    for i, (a, b) in enumerate(taps):
        for third in (0, K_MID, K_LO):
            misc[i, M_SEL + third + min(i, NK - 1 - i)] = 1
            t = b * TAPS + a
            misc[i, M_SELT + third + min(t, NK - 1 - t)] = 1
        misc[i, M_XY:M_XY + 2] = (b - r, a - r)
    misc[:, M_ONES:M_ONES + NK] = 1
    misc[:, M_MEAN] = 1.0 / C
    f = np.float32
    return {"ana": ana.astype(f), "syn": syn.astype(f), "gam": gam.astype(f),
            "misc": misc.astype(f)}


def attention_filter_kernel(nc, x, norm_w, norm_b, wq, bq, wk, bk, wv, bv, wp, bp, w1, b1, w2, b2,
                            wr, ana, syn, gam, misc, out):
    x_v = x.rearrange("b c h w -> b c (h w)")
    out_v = out.rearrange("b c h w -> c b (h w)")

    with ExitStack() as ctx:
        def sb(name, shape, dt=F32):
            return ctx.enter_context(nc.sbuf_tensor(name, shape, dt))

        def sem(name):
            return ctx.enter_context(nc.semaphore(name))

        X = sb("X", [P, B * N])
        T = sb("T", [P, N])
        HNH, HNL = sb("HNH", [P, N], F32R), sb("HNL", [P, N], F32R)
        QH, QL = sb("QH", [P, N], F32R), sb("QL", [P, N], F32R)
        KH, KL = sb("KH", [P, N], F32R), sb("KL", [P, N], F32R)
        VH, VL = sb("VH", [P, TILES, P], F32R), sb("VL", [P, TILES, P], F32R)
        E = sb("E", [P, 4 * N])
        ETH = sb("ETH", [P, 2 * TILES * HALF], F32R)
        ETL = sb("ETL", [P, 2 * TILES * HALF], F32R)
        XTH, XTL = sb("XTH", [P, TILES, P], F32R), sb("XTL", [P, TILES, P], F32R)
        R = sb("R", [P, B * UR])
        ANH, ANL = sb("ANH", [P, UW], F32R), sb("ANL", [P, UW], F32R)
        SYN = sb("SYN", [P, T_END])
        MISC = sb("MISC", [P, M_END])
        WRAW = E[:, 0:5 * P].rearrange("p (i c) -> p i c", i=5)
        WT = E[:, 5 * P:9 * P].rearrange("p (i c) -> p i c", i=4)
        WPT = E[:, 9 * P:10 * P]
        WH, WL = sb("WH", [P, 4, P], F32R), sb("WL", [P, 4, P], F32R)
        VEC = sb("VEC", [P, 6])
        BQS, BVP = sb("BQS", [P, 1]), sb("BVP", [P, 1])
        STAT = sb("STAT", [P, 12])
        MV = sb("MV", [P, 2])
        GM, GD, GS = sb("GM", [P, 1]), sb("GD", [P, 1]), sb("GS", [P, 1])
        GA, GB = sb("GA", [P, 1]), sb("GB", [P, 1])
        MINUS_HALF, ONE = sb("MINUS_HALF", [P, 1]), sb("ONE", [P, 1])
        UNUSED = sb("UNUSED", [P, 1])
        NMX, RS, RI = sb("NMX", [P, 2]), sb("RS", [P, 4]), sb("RI", [P, 4])
        W1, B1, W2 = sb("W1", [NK, HID]), sb("B1", [HID, 1]), sb("W2", [HID, 3])
        B2 = sb("B2", [NK, 3])
        C25, W1S, HIDV = sb("C25", [NF, B]), sb("W1S", [NF, HID]), sb("HIDV", [HID, B])
        ML = sb("ML", [NK, ML_END, B])
        FR = R[:, :].rearrange("p (b u) -> p b u", b=B)[:, :, UO + 2 * CH:UO + UA]
        K = sb("K", [NK, B])
        K3 = sb("K3", [K_ROWS, 2 * B], F32R)
        PS = ctx.enter_context(nc.psum_tensor("PS", [P, 8 * HALF], F32))

        eye = MISC[:, M_EYE:M_EYE + P]
        avg = MISC[:, M_AVG:M_AVG + P]
        QI, KI, VI, RI_ = 0, 1, 2, 3

        def s_bank(t):
            return PS[:, (t % 2) * N:(t % 2 + 1) * N]

        def bank(i, n=HALF, parts=P):
            return PS[0:parts, i * HALF:i * HALF + n]
        ET_BANK, PV_BANK, MISC_BANK = 4, 6, 7
        K3_AT = 96
        GN1_AT, GN2_AT, W1S_AT = 256, 288, 320
        LAST_PV_BANK, LAST_U_BANK = 0, 1
        MIX_BANK = (5, 7)

        at = [0]

        def carve(n):
            a = at[0]
            at[0] += n
            return ETH[:, a:a + n], ETL[:, a:a + n]
        SYH, SYL = carve(T_END)
        RTH, RTL = carve(4 * P)
        V3 = carve(P)[0]
        VTH, VTL = carve(4 * P)
        GH, GL = carve(4 * CH)
        ZH, ZL = carve(N)
        KB = carve(P)[0]
        GAM3R, GAMR = carve(NK * NK)
        GAM3R, GAMR = GAM3R[0:K_ROWS, :], GAMR[0:K_ROWS, 0:GAM]
        GAMS, GAM3S = E[0:K_ROWS, 0:GAM], E[0:K_ROWS, GAM:GAM + NK * NK]
        KHAT, KX, ZF, GF = E[:, 0:N], E[:, N:2 * N], E[:, 2 * N:3 * N], E[:, 3 * N:3 * N + 4 * CH]
        RST = T[:, 0:4 * P]
        R3S = T[0:NK, 4 * P:5 * P]
        G3S = T[0:NK, 7 * P:8 * P]
        GC = T[0:CH, 5 * P:5 * P + B * 4 * NZ]
        G3C = E[0:NK, 3 * N + 4 * CH:3 * N + 4 * CH + B * NK]

        names = """
            d_x0 d_xs d_w d_w2 d_vec d_misc d_ana d_syn d_mlp d_gam d_out
            g_one p_wt v_wpt v_wt p_bvp v_bvp v_bqs a_wh v_wl a_ah g_al p_w1s v_w1s a_root
            v_st p_gn1 p_gn2 v_gn g_gn v_t a_hh v_hl g_hl
            p_q a_qh v_ql p_k a_kh v_kl p_v a_vh v_vl
            p_s v_mx a_exp v_ri g_scl p_tr a_hi v_lo
            p_pv v_x1 g_x1 p_xt a_xh v_xl p_u a_ur
            v_m2 a_mag p_c25 v_c25 p_hid v_hid p_par v_ml v_n2 a_nr a_lam v_ex a_ex p_sum v_k
            p_k3 a_k3 v_k3 g_g3z a_gam g_gam p_g v_g a_sh v_syl
            g_rst p_rt a_rth v_rtl p_r3 a_r3 v_g3s p_v3 a_v3h v_v3l v_gf a_gh v_gl p_vt a_vth v_vtl
            a_kbh p_kh a_kh2 g_kx p_z v_z a_zh g_zl v_zl p_o v_o""".split()
        s = {n: sem(n) for n in names}

        block = ctx.enter_context(nc.Block())

        def passes(hi1, lo1, hi2, lo2):
            return ((hi1, hi2), (hi1, lo2), (lo1, hi2))

        def attention(run, eng):
            run(0, True, False, True)
            with eng.Fori(1, B - 1) as b:
                run(b, True, True, True)
            run(B - 1, True, True, False)
            run(B, False, True, False)

        def synthesis(first, step, eng):
            first()
            step(0, 3)
            with eng.Fori(1, B - 3) as i:
                step(i, 3)
            for i in range(B - 3, B):
                step(i, B - 1 - i)

        def is_later(n):
            return not isinstance(n, int) or n > 0

        @block.sync
        def _(sp):
            sp.dma_start(MISC[:], misc).then_inc(s["d_misc"], 16)
            for i, w in ((0, wq), (1, wk), (4, wr)):
                sp.dma_start(WRAW[:, i, :], w).then_inc(s["d_w"], 16)
            sp.wait_ge(s["d_vec"], 16 * 6)
            sp.dma_start(R[:, 0:UW], ana).then_inc(s["d_ana"], 16)
            sp.dma_start(W1[:], w1).then_inc(s["d_mlp"], 16)
            sp.dma_start(B1[:], b1.rearrange("(c a) -> c a", a=1)).then_inc(s["d_mlp"], 16)
            sp.dma_start(W2[:], w2).then_inc(s["d_mlp"], 16)
            sp.dma_start(B2[:], b2.rearrange("(a c) -> a c", a=1).broadcast_to([NK, 3]))\
                .then_inc(s["d_mlp"], 16)
            for b in range(1, B):
                sp.dma_start(X[:, b * N:(b + 1) * N], x_v[b]).then_inc(s["d_xs"], 16)
            sp.dma_start(SYN[:], syn).then_inc(s["d_syn"], 16)
            sp.wait_ge(s["p_tr"], 2 * TILES * B)
            sp.dma_start(E[0:K_ROWS, 0:GAM + NK * NK], gam).then_inc(s["d_gam"], 16)
            with sp.Fori(0, B - 1) as b:
                sp.wait_ge(s["v_o"], 2 * b + 2)
                sp.dma_start(out_v[:, bass.ds(b, 1), :], X[:, bass.ds(b * N, N)])\
                    .then_inc(s["d_out"], 16)
            for h in range(2):
                half = slice(h * HALF, (h + 1) * HALF)
                sp.wait_ge(s["v_o"], 2 * (B - 1) + h + 1)
                sp.dma_start(out_v[:, B - 1, half], X[:, (B - 1) * N + h * HALF:][:, 0:HALF])\
                    .then_inc(s["d_out"], 16)
            sp.wait_ge(s["d_out"], 16 * (B + 1))

        @block.tensor
        def _(pe):
            def mm(o, a, b_, start, stop):
                return pe.matmul(o, a, b_, start=start, stop=stop)

            pe.wait_ge(s["d_misc"], 16)

            def group_norm_mean(n, bk_):
                pe.wait_ge(s["v_st"], 3 * n + 3)
                mm(bank(bk_)[:, GN1_AT:GN1_AT + 1], avg, MV[:, 0:1], True, True)\
                    .then_inc(s["p_gn1"], 1)

            def group_norm_variance(n, bk_):
                pe.wait_ge(s["v_gn"], 8 * n + 3)
                mm(bank(bk_)[:, GN2_AT:GN2_AT + 1], avg, GD[:], True, True).then_inc(s["p_gn2"], 1)

            group_norm_mean(0, PV_BANK)
            pe.wait_ge(s["d_w"], 16 * 3)
            pe.wait_ge(s["d_w2"], 16 * 2)
            for slot, i in enumerate((0, 1, 3, 4)):
                ins = pe.transpose(bank(MISC_BANK)[:, slot * P:(slot + 1) * P], WRAW[:, i, :], eye)
            ins.then_inc(s["p_wt"], 1)
            group_norm_variance(0, PV_BANK)
            pe.wait_ge(s["v_wpt"], 1)
            pe.wait_ge(s["v_gn"], 4)
            pe.wait_ge(s["d_vec"], 16 * 6)
            mm(bank(PV_BANK)[:, 0:P], WRAW[:, 2, :], WPT, True, True)
            mm(bank(PV_BANK)[:, P:P + 1], WPT, VEC[:, 4:5], True, True).then_inc(s["p_bvp"], 1)

            def project(w, done, base, first=False):
                for h in range(2):
                    if base == 0 and first:
                        pe.wait_ge(s["v_hl"], h + 1)
                    o = PS[:, base + h * HALF:base + (h + 1) * HALF]
                    for n, (a, r) in enumerate(passes(WH[:, w, :], WL[:, w, :],
                                                      HNH[:, h * HALF:(h + 1) * HALF],
                                                      HNL[:, h * HALF:(h + 1) * HALF])):
                        ins = mm(o, a, r, n == 0, n == 2)
                    ins.then_inc(s[done], 1)

            def scores(b, t):
                q0 = slice(t * P, (t + 1) * P)
                for n, (a, r) in enumerate(passes(QH[:, q0], QL[:, q0], KH, KL)):
                    if t == 0 and n == 0:
                        pe.wait_ge(s["v_ql"], 2 * b + 2)
                        pe.wait_ge(s["a_kh"], 2 * b + 2)
                    if t == 0 and n == 1:
                        pe.wait_ge(s["v_kl"], 2 * b + 2)
                    for h in range(2):
                        ins = mm(s_bank(t)[:, h * HALF:(h + 1) * HALF], a,
                                 r[:, h * HALF:(h + 1) * HALF], n == 0, n == 2)
                ins.then_inc(s["p_s"], 1)

            def transposes(b, t):
                pe.wait_ge(s["g_scl"], TILES * b + t + 1)
                for k in range(2):
                    if is_later(b) or t > 0:
                        pe.wait_ge(s["v_lo"], 2 * (TILES * b + t) + k - 1)
                    for j in range(4):
                        c0 = (t % 4) * N + (4 * k + j) * P
                        ins = pe.transpose(bank(ET_BANK + k)[:, j * P:(j + 1) * P],
                                           E[:, c0:c0 + P], eye)
                    ins.then_inc(s["p_tr"], 1)

            def values(b, h, c, pv=PV_BANK):
                if c == 0:
                    pe.wait_ge(s["v_lo"], 16 * b + 8 * h + 8)
                    if pv == PV_BANK and (is_later(b) or h > 0):
                        pe.wait_ge(s["v_x1"], 2 * b + h)
                if h == 0 and c == 0:
                    pe.wait_ge(s["v_vl"], 2 * b + 1)
                if h == 0 and c == 2:
                    pe.wait_ge(s["v_vl"], 2 * b + 2)
                for j in (2 * c, 2 * c + 1):
                    e0 = (h * TILES + j) * HALF
                    for n, (a, r) in enumerate(passes(VH[:, j, :], VL[:, j, :],
                                                      ETH[:, e0:e0 + HALF], ETL[:, e0:e0 + HALF])):
                        ins = mm(bank(pv), a, r, j == 0 and n == 0, j == TILES - 1 and n == 2)
                if c == 3:
                    ins.then_inc(s["p_pv"], 1)

            def x1_transposes(p, h):
                pe.wait_ge(s["v_x1"], 2 * p + h + 1)
                for j in range(4):
                    c0 = h * HALF + j * P
                    ins = pe.transpose(bank(MISC_BANK)[:, j * P:(j + 1) * P], T[:, c0:c0 + P], eye)
                ins.then_inc(s["p_xt"], 1)

            def project_v(b, h):
                for j in range(4):
                    t0 = (4 * h + j) * P
                    for n, (a, r) in enumerate(passes(HNH[:, t0:t0 + P], HNL[:, t0:t0 + P],
                                                      WH[:, VI, :], WL[:, VI, :])):
                        ins = mm(bank(MISC_BANK)[:, j * P:(j + 1) * P], a, r, n == 0, n == 2)
                ins.then_inc(s["p_v"], 1)

            def in_tile(t, o):
                cols = slice(UI, UI + UB)
                at = t * UB + (UO + UA if t < TILES // 2 else -CH)
                for n, (a, r) in enumerate(passes(XTH[:, t, :], XTL[:, t, :],
                                                  ANH[:, cols], ANL[:, cols])):
                    ins = mm(o[:, at:at + UB], a, r, n == 0, n == 2)
                return ins

            def over_tiles(t, o):
                if 0 < t < TILES - 1:
                    cols, at, n_cols = slice((t - 1) * UA, t * UA), UO, UA
                else:
                    at, n_cols = UO - UB, UA + 2 * UB
                    cols = slice(UE, UE + n_cols) if t == 0 else slice(UI, UW)
                for n, (a, r) in enumerate(passes(XTH[:, t, :], XTL[:, t, :],
                                                  ANH[:, cols], ANL[:, cols])):
                    mm(o[:, at:at + n_cols], a, r, t == 0 and n == 0, t == TILES - 1 and n == 2)

            def analysis(p):
                pe.wait_ge(s["v_xl"], 2 * p + 2)
                pe.wait_ge(s["g_al"], 1)
                for t in range(1, TILES // 2):
                    in_tile(t, bank(MISC_BANK))
                for t in range(TILES):
                    over_tiles(t, bank(MISC_BANK))
                for t in range(TILES // 2, TILES - 1):
                    ins = in_tile(t, bank(MISC_BANK))
                ins.then_inc(s["p_u"], 1)

            def rt(n):
                pe.wait_ge(s["g_rst"], 2 * n + 2)
                if is_later(n):
                    pe.wait_ge(s["v_rtl"], n)
                else:
                    pe.wait_ge(s["v_lo"], 2 * TILES * B)
                for i, c in enumerate((1, 2, 3, 0)):
                    ins = pe.transpose(bank(4)[0:CH, i * P:(i + 1) * P],
                                       RST[:, c * CH:(c + 1) * CH], eye)
                ins.then_inc(s["p_rt"], 1)

            def r3(n, after_mix=True):
                pe.wait_ge(s["v_rtl"], n + 1)
                pe.wait_ge(s["v_syl"], 1)
                if after_mix:
                    pe.wait_ge(s["v_o"], 2 * n - 3)
                m = 0
                for c in range(2):
                    w = slice(T_PR + c * P, T_PR + (c + 1) * P)
                    d_ = slice((2 + c) * P, (3 + c) * P)
                    for a, r in passes(SYH[0:CH, w], SYL[0:CH, w], RTH[0:CH, d_], RTL[0:CH, d_]):
                        ins = mm(bank(5)[:, 0:P], a, r, m == 0, m == 5)
                        m += 1
                ins.then_inc(s["p_r3"], 1)

            def v3(n):
                pe.wait_ge(s["a_r3"], n + 1)
                pe.wait_ge(s["v_g3s"], n + 1)
                mm(bank(5)[:, P:2 * P], G3S, R3S, True, True).then_inc(s["p_v3"], 1)

            def vt(n):
                pe.wait_ge(s["v_gl"], n + 1)
                for i in range(4):
                    d_ = slice(i * P, (i + 1) * P)
                    g = slice(i * CH, (i + 1) * CH)
                    jobs = list(passes(GH[0:CH, g], GL[0:CH, g], RTH[0:CH, d_], RTL[0:CH, d_]))
                    if i >= 2:
                        if i == 2:
                            pe.wait_ge(s["v_v3l"], n + 1)
                        w = slice(T_EX + (i - 2) * CH, T_EX + (i - 1) * CH)
                        jobs += [(SYH[:, w], V3), (SYL[0:NK, w], V3[0:NK, :])]
                    for m, (a, r) in enumerate(jobs):
                        ins = mm(bank(6)[0:CH, d_], a, r, m == 0, m == len(jobs) - 1)
                ins.then_inc(s["p_vt"], 1)

            def khat(n, h):
                if h == 0:
                    pe.wait_ge(s["v_syl"], 2)
                    pe.wait_ge(s["a_kbh"], n + 1)
                if is_later(n):
                    pe.wait_ge(s["a_kh2"], 2 * n + h - 1)
                w = slice(T_COS + h * HALF, T_COS + (h + 1) * HALF)
                mm(bank(2 + h), KB[0:K_ROWS, :], SYH[0:K_ROWS, w], True, True)\
                    .then_inc(s["p_kh"], 1)

            def z(b, h):
                pe.wait_ge(s["v_vtl"], b + 1)
                jobs = []
                d_ = slice((2 + h) * P, (3 + h) * P)
                for a, r in passes(VTH[0:CH, d_], VTL[0:CH, d_], SYH[0:CH, T_U2:T_U2 + HALF],
                                   SYL[0:CH, T_U2:T_U2 + HALF]):
                    jobs.append((bank(h), a, r))
                w = slice(T_U1 + h * 256, T_U1 + (h + 1) * 256)
                grid = bank(h).rearrange("c (h w) -> c h w", w=SIDE)
                for i in range(2):
                    d_ = slice(i * P, (i + 1) * P)
                    for a, r in passes(VTH[0:CH, d_], VTL[0:CH, d_], SYH[0:CH, w], SYL[0:CH, w]):
                        jobs.append((grid[:, :, 16 * i:16 * (i + 1)], a,
                                     r.rearrange("c (h w) -> c h w", w=16)))
                for m, (o, a, r) in enumerate(jobs):
                    ins = mm(o, a, r, m == 0, m == len(jobs) - 1)
                ins.then_inc(s["p_z"], 1)

            def mix(b, h, last=False):
                if last:
                    pe.wait_ge(s["v_zl"], h + 1)
                else:
                    pe.wait_ge(s["g_zl"], 2 * b + h + 1)
                if is_later(b):
                    pe.wait_ge(s["v_o"], 2 * b + h - 1)
                d_ = slice(h * HALF, (h + 1) * HALF)
                for m, (a, r) in enumerate(passes(WH[:, RI_, :], WL[:, RI_, :],
                                                  ZH[:, d_], ZL[:, d_])):
                    ins = mm(bank(MIX_BANK[h]), a, r, m == 0, m == 2)
                ins.then_inc(s["p_o"], 1)

            def image(b, cur, prev, nxt):
                p = b - 1
                if prev:
                    transposes(p, 6)
                if cur:
                    if prev:
                        pe.wait_ge(s["v_hl"], 3)
                        pe.wait_ge(s["g_hl"], b)
                        pe.wait_ge(s["a_exp"], TILES * b - 1)
                    else:
                        pe.wait_ge(s["v_wl"], 1)
                    project(QI, "p_q", 0, first=not prev)
                    if prev:
                        pe.wait_ge(s["a_exp"], TILES * b)
                    project(KI, "p_k", N)
                for t in range(TILES):
                    if cur:
                        if t == 0:
                            if prev:
                                values(p, 0, 2)
                            else:
                                project_v(0, 0)
                        if t >= 2:
                            pe.wait_ge(s["a_exp"], TILES * b + t - 1)
                        scores(b, t)
                        if t >= 2:
                            transposes(b, t - 2)
                        if nxt and t == 4:
                            group_norm_variance(b + 1, MISC_BANK)
                    if prev:
                        if t == 0 and not cur:
                            values(p, 0, 2)
                        if t == 1:
                            transposes(p, 7)
                            values(p, 0, 3)
                        pv = PV_BANK if cur else LAST_PV_BANK
                        if t == 2:
                            values(p, 1, 0, pv=pv)
                            pe.wait_ge(s["a_ur"], b)
                            x1_transposes(p, 0)
                        if t == 3:
                            values(p, 1, 1, pv=pv)
                            if nxt:
                                pe.wait_ge(s["v_xl"], 2 * p + 1)
                                group_norm_mean(b + 1, MISC_BANK)
                        if t == 4:
                            values(p, 1, 2, pv=pv)
                        if t == 5:
                            if not cur:
                                rt(0)
                            values(p, 1, 3, pv=pv)
                    if cur:
                        if not prev and t == 1:
                            pe.wait_ge(s["v_vl"], 1)
                            project_v(0, 1)
                        if not prev and t == 3:
                            pe.wait_ge(s["v_vl"], 2)
                            group_norm_mean(1, MISC_BANK)
                            pe.wait_ge(s["d_mlp"], 16 * 4)
                            mm(bank(PV_BANK)[0:NF, W1S_AT:W1S_AT + HID],
                               MISC[0:NK, M_SEL:M_SEL + NF], W1[:], True, True)\
                                .then_inc(s["p_w1s"], 1)
                        if prev and t == 4:
                            if nxt:
                                pe.wait_ge(s["v_gn"], 8 * b + 12)
                            else:
                                pe.wait_ge(s["v_xl"], 2 * p + 1)
                            project_v(b, 0)
                        if prev and t == 5:
                            pe.wait_ge(s["v_vl"], 2 * b + 1)
                            project_v(b, 1)
                    if t == 6 and not cur:
                        o = bank(LAST_U_BANK)
                        pe.wait_ge(s["v_xl"], 2 * p + 1)
                        for k in range(1, TILES // 2):
                            in_tile(k, o)
                        x1_transposes(p, 1)
                        for k in range(TILES):
                            if k == TILES // 2:
                                pe.wait_ge(s["v_xl"], 2 * p + 2)
                            over_tiles(k, o)
                        for k in range(TILES // 2, TILES - 1):
                            ins = in_tile(k, o)
                        ins.then_inc(s["p_u"], 1)
                        r3(0, after_mix=False)
                    if t == 6 and cur:
                        if prev:
                            pe.wait_ge(s["v_vl"], 2 * b + 2)
                            x1_transposes(p, 1)
                        else:
                            pe.wait_ge(s["v_w1s"], 1)
                        values(b, 0, 0)
                    if t == 7 and cur:
                        if prev:
                            analysis(p)
                        values(b, 0, 1)

            attention(image, pe)

            A, D = bank(6), bank(7)
            pe.wait_ge(s["a_mag"], 1)
            for b in range(B):
                ins = mm(A[0:NF, b:b + 1], R[:, b * UR + UO + 2 * CH + NF:b * UR + UO + UA],
                         MISC[:, M_MEAN:M_MEAN + 1], True, True)
            ins.then_inc(s["p_c25"], 1)
            pe.wait_ge(s["v_c25"], 1)
            mm(D[0:HID, 0:B], W1S[:], C25[:], True, True).then_inc(s["p_hid"], 1)
            pe.wait_ge(s["v_hid"], 1)
            for j in range(3):
                ins = mm(A[0:NK, 32 + j * B:32 + (j + 1) * B],
                         W2[:, j:j + 1].broadcast_to([HID, NK]), HIDV[:], True, True)
            ins.then_inc(s["p_par"], 1)

            def kernel_and_borders():
                pe.wait_ge(s["a_ex"], 1)
                mm(A[0:NK, 64:64 + B], MISC[0:NK, M_ONES:M_ONES + NK], ML[:, ML_K, :], True, True)\
                    .then_inc(s["p_sum"], 1)
                pe.wait_ge(s["v_k"], 1)
                for g, w in enumerate((M_SEL, M_SELT)):
                    ins = mm(A[0:K_ROWS, K3_AT + g * B:K3_AT + (g + 1) * B],
                             MISC[0:NK, w:w + K_ROWS], K[:], True, True)
                ins.then_inc(s["p_k3"], 1)
                pe.wait_ge(s["v_k3"], 1)
                pe.wait_ge(s["a_r3"], 1)
                pe.wait_ge(s["g_gam"], 1)
                for i in range(2 * NZ):
                    ins = mm(bank(5)[0:CH, i * 2 * B:(i + 1) * 2 * B],
                             GAMR[:, i * CH:(i + 1) * CH], K3[:], True, True)
                ins.then_inc(s["p_g"], 1)
                pe.wait_ge(s["g_gam"], 2)
                for i in range(NK):
                    ins = mm(bank(4)[0:NK, i * B:(i + 1) * B], GAM3R[:, i * NK:(i + 1) * NK],
                             K3[:, 0:B], True, True)
                ins.then_inc(s["p_g"], 1)

            def first():
                kernel_and_borders()
                khat(0, 0)
                pe.wait_ge(s["v_g"], 3)
                v3(0)
                vt(0)
                khat(0, 1)
                rt(1)

            def step(i, more):
                z(i, 0)
                if more:
                    r3(i + 1, after_mix=is_later(i))
                z(i, 1)
                if more:
                    v3(i + 1)
                    khat(i + 1, 0)
                    khat(i + 1, 1)
                    vt(i + 1)
                mix(i, 0, last=more == 0)
                if more > 1:
                    rt(i + 2)
                mix(i, 1, last=more == 0)

            synthesis(first, step, pe)

        @block.scalar
        def _(act):
            act.dma_start(X[:, 0:N], x_v[0]).then_inc(s["d_x0"], 16)
            for i, w in ((3, wp), (2, wv)):
                act.dma_start(WRAW[:, i, :], w).then_inc(s["d_w2"], 16)
            for i, v in enumerate((norm_w, norm_b, bq, bk, bv, bp)):
                act.dma_start(VEC[:, i:i + 1], v.rearrange("(c a) -> c a", a=1))\
                    .then_inc(s["d_vec"], 16)

            act.wait_ge(s["g_one"], 2)
            act.wait_ge(s["g_hl"], 1)
            act.activation(UNUSED[:], ONE[:], ACT.Exp).then_inc(s["a_root"], 1)
            act.wait_ge(s["v_wt"], 4)
            act.activation(WH[:], WT, ACT.Copy).then_inc(s["a_wh"], 1)

            def hn_hi(b):
                act.wait_ge(s["v_t"], b + 2)
                act.activation(HNH[:], T[:], ACT.Copy).then_inc(s["a_hh"], 1)

            for h in range(2):
                act.wait_ge(s["v_t"], h + 1)
                act.activation(HNH[:, h * HALF:(h + 1) * HALF], T[:, h * HALF:(h + 1) * HALF],
                               ACT.Copy).then_inc(s["a_hh"], 1)
            act.wait_ge(s["d_ana"], 16)
            act.activation(ANH[:, 0:UA], R[:, 0:UA], ACT.Copy).then_inc(s["a_ur"], 1)
            act.activation(ANH[:, UA:UW], R[:, UA:UW], ACT.Copy).then_inc(s["a_ah"], 1)

            def project_hi(dst, base, bias, done, out_sem, b):
                for h in range(2):
                    act.wait_ge(s[done], 2 * b + h + 1)
                    act.activation(dst[:, h * HALF:(h + 1) * HALF],
                                   PS[:, base + h * HALF:base + (h + 1) * HALF], ACT.Identity,
                                   bias=bias).then_inc(s[out_sem], 1)

            def exp(b, t):
                act.wait_ge(s["v_mx"], TILES * b + t + 1)
                act.activation(E[:, (t % 4) * N:(t % 4 + 1) * N], s_bank(t), ACT.Exp,
                               bias=NMX[:, t % 2:t % 2 + 1],
                               accum_out=RS[:, t % 4:t % 4 + 1]).then_inc(s["a_exp"], 1)

            def et_hi(b, t):
                h, i = t // 4, t % 4
                et = ETH[:, :].rearrange("p (h j n) -> p h j n", h=2, j=TILES)
                for k in range(2):
                    act.wait_ge(s["p_tr"], 2 * (TILES * b + t) + k + 1)
                    act.activation(et[:, h, 4 * k:4 * k + 4, i * P:(i + 1) * P],
                                   bank(ET_BANK + k).rearrange("p (j n) -> p j n", j=4),
                                   ACT.Copy).then_inc(s["a_hi"], 1)

            def misc_hi(dst, done, n, out_sem):
                act.wait_ge(s[done], n)
                act.activation(dst, bank(MISC_BANK).rearrange("p (j n) -> p j n", j=4), ACT.Copy)\
                    .then_inc(s[out_sem], 1)

            def k_hi(n):
                if is_later(n):
                    act.wait_ge(s["p_kh"], 2 * n)
                else:
                    act.wait_ge(s["v_k3"], 1)
                act.activation(KB[0:K_ROWS, :], K3[:, bass.ds(n, 1)].bitcast(F32)
                               .broadcast_to([K_ROWS, P]), ACT.Copy).then_inc(s["a_kbh"], 1)

            def g_hi(n):
                act.wait_ge(s["v_gf"], n + 1)
                if is_later(n):
                    act.wait_ge(s["p_vt"], n)
                act.activation(GH[0:CH, :], GF[0:CH, :], ACT.Copy).then_inc(s["a_gh"], 1)

            def khat_copy(n, h):
                act.wait_ge(s["p_kh"], 2 * n + h + 1)
                if is_later(n):
                    act.wait_ge(s["g_kx"], 2 * n + h - 1)
                act.activation(KHAT[:, h * HALF:(h + 1) * HALF], bank(2 + h), ACT.Copy)\
                    .then_inc(s["a_kh2"], 1)

            def copy(dst, src, done, n, out_sem):
                act.wait_ge(s[done], n)
                act.activation(dst, src, ACT.Copy).then_inc(s[out_sem], 1)

            def z_hi(b, h):
                d_ = slice(h * HALF, (h + 1) * HALF)
                copy(ZH[:, d_], ZF[:, d_], "v_z", 2 * b + h + 1, "a_zh")

            def rt_hi(n):
                copy(RTH[0:CH, :], bank(4, HALF, CH), "p_rt", n + 1, "a_rth")

            def r3_copy(n):
                copy(R3S, bank(5, P, NK), "p_r3", n + 1, "a_r3")

            def v3_hi(n):
                copy(V3, bank(5)[:, P:2 * P], "p_v3", n + 1, "a_v3h")

            def vt_hi(n):
                copy(VTH[0:CH, :], bank(6, HALF, CH), "p_vt", n + 1, "a_vth")

            def image(b, cur, prev, nxt):
                p = b - 1
                if not cur:
                    act.wait_ge(s["a_root"], 1)
                    act.activation(UNUSED[:], ONE[:], ACT.Sqrt).then_inc(s["a_root"], 1)
                if cur:
                    if not prev:
                        act.wait_ge(s["v_bqs"], 1)
                    project_hi(QH, 0, BQS[:, 0:1], "p_q", "a_qh", b)
                    project_hi(KH, N, VEC[:, 3:4], "p_k", "a_kh", b)
                for t in range(TILES):
                    if prev and t == 0:
                        et_hi(p, 6)
                    if cur and t >= 2:
                        et_hi(b, t - 2)
                    if prev and t == 1:
                        et_hi(p, 7)
                    if not prev and t == 0:
                        misc_hi(VH[:, 0:4, :], "p_v", 1, "a_vh")
                    if cur:
                        exp(b, t)
                    if nxt and t == (TILES - 1 if prev else TILES - 3):
                        hn_hi(b + 1)
                    if prev:
                        if t == 2 and not cur:
                            act.wait_ge(s["d_syn"], 16)
                            act.wait_ge(s["p_pv"], 2 * p + 1)
                            act.activation(SYH, SYN[:], ACT.Copy).then_inc(s["a_sh"], 1)
                        if t == 5 and not cur:
                            rt_hi(0)
                        if t == 2:
                            misc_hi(XTH[:, 0:4, :], "p_xt", 2 * p + 1, "a_xh")
                    if cur:
                        if prev and t == 4:
                            misc_hi(VH[:, 0:4, :], "p_v", 2 * b + 1, "a_vh")
                        if t == (5 if prev else 1):
                            misc_hi(VH[:, 4:8, :], "p_v", 2 * b + 2, "a_vh")
                    if prev:
                        if t == 6:
                            misc_hi(XTH[:, 4:8, :], "p_xt", 2 * p + 2, "a_xh")
                        if t == 7:
                            act.wait_ge(s["p_u"], p + 1)
                            act.activation(R[:, bass.ds(p * UR, UR)],
                                           bank(MISC_BANK if cur else LAST_U_BANK, UR), ACT.Copy)\
                                .then_inc(s["a_ur"], 1)
                            if not cur:
                                act.wait_ge(s["g_x1"], 2 * B)
                                r3_copy(0)

            attention(image, act)

            act.wait_ge(s["v_m2"], 2)
            act.activation(FR[:, :, NF:2 * NF], FR[:, :, 0:NF], ACT.Sqrt).then_inc(s["a_mag"], 1)

            act.wait_ge(s["d_gam"], 16)
            act.wait_ge(s["p_pv"], 2 * B)
            act.activation(GAMR, GAMS, ACT.Copy).then_inc(s["a_gam"], 1)

            def roots():
                act.wait_ge(s["v_n2"], 1)
                act.activation(ML[:, ML_NR, :], ML[:, ML_N2, :], ACT.Sqrt).then_inc(s["a_nr"], 1)
                act.activation(ML[:, ML_LAM, :], ML[:, ML_P2, :], ACT.Exp).then_inc(s["a_lam"], 1)
                act.activation(GAM3R, GAM3S, ACT.Copy).then_inc(s["a_gam"], 1)

            def first():
                roots()
                act.wait_ge(s["v_ex"], 1)
                act.activation(ML[:, ML_K, :], ML[:, ML_E, :], ACT.Exp, scale=-1.0)\
                    .then_inc(s["a_ex"], 1)
                act.wait_ge(s["p_k3"], 1)
                act.activation(K3[:], bank(6)[0:K_ROWS, K3_AT:K3_AT + 2 * B], ACT.Copy)\
                    .then_inc(s["a_k3"], 1)
                k_hi(0)
                g_hi(0)
                khat_copy(0, 0)
                v3_hi(0)
                vt_hi(0)
                khat_copy(0, 1)
                k_hi(1)
                rt_hi(1)

            def step(i, more):
                if more:
                    g_hi(i + 1)
                    r3_copy(i + 1)
                z_hi(i, 0)
                if more:
                    v3_hi(i + 1)
                z_hi(i, 1)
                if more:
                    khat_copy(i + 1, 0)
                    khat_copy(i + 1, 1)
                if more > 1:
                    k_hi(i + 2)
                if more:
                    vt_hi(i + 1)
                if more > 1:
                    rt_hi(i + 2)

            synthesis(first, step, act)

        @block.vector
        def _(dve):
            TT, TS, STT = dve.tensor_tensor, dve.tensor_scalar, dve.scalar_tensor_tensor

            def stats(n):
                for h in range(2):
                    dve.bn_stats(STAT[:, 6 * h:6 * h + 6], X[:, bass.ds(n * N + h * HALF, HALF)])\
                        .then_inc(s["v_st"], 1)
                dve.wait_ge(s["v_st"], 3 * n + 2)

            def stats_end():
                dve.bn_aggr(MV[:], STAT[:]).then_inc(s["v_st"], 1)

            def group_norm_a(n, bk_):
                dve.wait_ge(s["p_gn1"], n + 1)
                TT(GM[:], bank(bk_)[:, GN1_AT:GN1_AT + 1], MV[:, 0:1], ALU.subtract)\
                    .then_inc(s["v_gn"], 1)
                dve.wait_ge(s["v_gn"], 8 * n + 1)
                TT(GS[:], GM[:], GM[:], ALU.mult).then_inc(s["v_gn"], 1)
                dve.wait_ge(s["v_gn"], 8 * n + 2)
                TT(GD[:], GS[:], MV[:, 1:2], ALU.add).then_inc(s["v_gn"], 1)

            def group_norm_b(n, bk_):
                dve.wait_ge(s["p_gn2"], n + 1)
                TS(GS[:], bank(bk_)[:, GN2_AT:GN2_AT + 1], GN_EPS, None, ALU.add)\
                    .then_inc(s["v_gn"], 1)

            def group_norm_c(n):
                dve.wait_ge(s["g_gn"], n + 1)
                TS(GA[:], GD[:], VEC[:, 0:1], None, ALU.mult).then_inc(s["v_gn"], 1)
                TT(GS[:], GM[:], MV[:, 0:1], ALU.add).then_inc(s["v_gn"], 1)
                dve.wait_ge(s["v_gn"], 8 * n + 6)
                TT(GS[:], GS[:], GA[:], ALU.mult).then_inc(s["v_gn"], 1)
                dve.wait_ge(s["v_gn"], 8 * n + 7)
                TS(GB[:], GS[:], -1.0, VEC[:, 1:2], ALU.mult, ALU.add).then_inc(s["v_gn"], 1)
                dve.wait_ge(s["v_gn"], 8 * n + 8)

            dve.wait_ge(s["d_x0"], 16)
            stats(0)
            stats_end()
            group_norm_a(0, PV_BANK)
            dve.wait_ge(s["p_wt"], 1)
            mb = bank(MISC_BANK)
            dve.tensor_copy(WPT, mb[:, 2 * P:3 * P]).then_inc(s["v_wpt"], 1)
            TS(WT[:, QI, :], mb[:, 0:P], SCALE, None, ALU.mult).then_inc(s["v_wt"], 1)
            dve.tensor_copy(WT[:, KI, :], mb[:, P:2 * P]).then_inc(s["v_wt"], 1)
            dve.tensor_copy(WT[:, RI_, :], mb[:, 3 * P:4 * P]).then_inc(s["v_wt"], 1)
            group_norm_b(0, PV_BANK)
            dve.wait_ge(s["p_bvp"], 1)
            dve.tensor_copy(WT[:, VI, :], bank(PV_BANK)[:, 0:P]).then_inc(s["v_wt"], 1)
            dve.wait_ge(s["d_vec"], 16 * 6)
            TT(BVP[:], bank(PV_BANK)[:, P:P + 1], VEC[:, 5:6], ALU.add).then_inc(s["v_bvp"], 1)
            TS(BQS[:], VEC[:, 2:3], SCALE, None, ALU.mult).then_inc(s["v_bqs"], 1)
            group_norm_c(0)

            def hn(b):
                TS(T[:], X[:, bass.ds(b * N, N)], GA[:], GB[:],
                   ALU.mult, ALU.add).then_inc(s["v_t"], 1)

            for h in range(2):
                d_ = slice(h * HALF, (h + 1) * HALF)
                TS(T[:, d_], X[:, d_], GA[:], GB[:], ALU.mult, ALU.add).then_inc(s["v_t"], 1)
            dve.wait_ge(s["a_wh"], 1)
            TT(WL[:], WT, WH[:].bitcast(F32), ALU.subtract).then_inc(s["v_wl"], 1)

            def hn_lo(b):
                dve.wait_ge(s["a_hh"], b + 2)
                TT(HNL[:], T[:], HNH[:].bitcast(F32), ALU.subtract).then_inc(s["v_hl"], 1)

            for h in range(2):
                d_ = slice(h * HALF, (h + 1) * HALF)
                dve.wait_ge(s["a_hh"], h + 1)
                TT(HNL[:, d_], T[:, d_], HNH[:, d_].bitcast(F32), ALU.subtract)\
                    .then_inc(s["v_hl"], 1)
            dve.wait_ge(s["v_bvp"], 1)

            def project_lo(dst, hi, base, bias, done, out_sem, b):
                for h in range(2):
                    d_ = slice(h * HALF, (h + 1) * HALF)
                    dve.wait_ge(s[done], 2 * b + h + 1)
                    STT(out=dst[:, d_], in0=PS[:, base + h * HALF:base + (h + 1) * HALF],
                        scalar=bias, in1=hi[:, d_].bitcast(F32), op0=ALU.add, op1=ALU.subtract)\
                        .then_inc(s[out_sem], 1)

            def row_max(b, t):
                dve.wait_ge(s["p_s"], TILES * b + t + 1)
                dve.tensor_reduce(NMX[:, t % 2:t % 2 + 1], s_bank(t), AX.X, ALU.max, negate=True)\
                    .then_inc(s["v_mx"], 1)

            def row_sum(b, t):
                dve.wait_ge(s["a_exp"], TILES * b + t + 1)
                dve.reciprocal(RI[:, t % 4:t % 4 + 1], RS[:, t % 4:t % 4 + 1])\
                    .then_inc(s["v_ri"], 1)

            def et_lo(b, t):
                h, i = t // 4, t % 4
                etl, eth = (e[:, :].rearrange("p (h j n) -> p h j n", h=2, j=TILES)
                            for e in (ETL, ETH))
                for k in range(2):
                    dve.wait_ge(s["a_hi"], 2 * (TILES * b + t) + k + 1)
                    part = (slice(None), h, slice(4 * k, 4 * k + 4), slice(i * P, (i + 1) * P))
                    TT(etl[part], bank(ET_BANK + k).rearrange("p (j n) -> p j n", j=4),
                       eth[part].bitcast(F32), ALU.subtract).then_inc(s["v_lo"], 1)

            def misc_lo(lo, hi, done, n, out_sem):
                dve.wait_ge(s[done], n)
                TT(lo, bank(MISC_BANK).rearrange("p (j n) -> p j n", j=4), hi.bitcast(F32),
                   ALU.subtract).then_inc(s[out_sem], 1)

            def residual(p, h, pv=PV_BANK):
                dve.wait_ge(s["p_pv"], 2 * p + h + 1)
                STT(out=T[:, h * HALF:(h + 1) * HALF], in0=bank(pv), scalar=BVP[:, 0:1],
                    in1=X[:, bass.ds(p * N + h * HALF, HALF)], op0=ALU.add, op1=ALU.add)\
                    .then_inc(s["v_x1"], 1)

            def lo(dst, full, hi, done, n, out_sem):
                dve.wait_ge(s[done], n)
                TT(dst, full, hi.bitcast(F32), ALU.subtract).then_inc(s[out_sem], 1)

            def g_full(n):
                if is_later(n):
                    dve.wait_ge(s["v_gl"], n)
                gc = GC[:, bass.ds(n * 4 * NZ, 4 * NZ)]
                TT(GF[0:CH, :].rearrange("p (c w q) -> p c w q", c=4, w=16),
                   gc.rearrange("p (c a q) -> p c a q", c=4, a=1).broadcast_to([CH, 4, 16, NZ]),
                   MISC[0:CH, M_MASK:M_MASK + 16].rearrange("p (c w q) -> p c w q", c=1, q=1)
                   .broadcast_to([CH, 4, 16, NZ]), ALU.mult).then_inc(s["v_gf"], 1)

            def g3_copy(n):
                if is_later(n):
                    dve.wait_ge(s["p_v3"], n)
                dve.tensor_copy(G3S.rearrange("p (s c) -> p s c", s=2)[:, :, 0:NK],
                                G3C[:, bass.ds(n * NK, NK)].rearrange("p (s c) -> p s c", s=1)
                                .broadcast_to([NK, 2, NK])).then_inc(s["v_g3s"], 1)

            def g_lo(n):
                dve.wait_ge(s["v_gf"], n + 1)
                lo(GL[0:CH, :], GF[0:CH, :], GH[0:CH, :], "a_gh", n + 1, "v_gl")

            def rt_lo(n):
                lo(RTL[0:CH, :], bank(4, HALF, CH), RTH[0:CH, :], "a_rth", n + 1, "v_rtl")

            def v3_lo(n):
                lo(V3[LO:P, :], bank(5)[LO:P, P:2 * P], V3[LO:P, :], "a_v3h", n + 1, "v_v3l")

            def vt_lo(n):
                lo(VTL[0:CH, :], bank(6, HALF, CH), VTH[0:CH, :], "a_vth", n + 1, "v_vtl")

            def z_sum(b, h):
                d_ = slice(h * HALF, (h + 1) * HALF)
                dve.wait_ge(s["p_z"], 2 * b + h + 1)
                dve.wait_ge(s["g_kx"], 2 * b + h + 1)
                if is_later(b):
                    dve.wait_ge(s["g_zl"], 2 * b + h - 1)
                TT(ZF[:, d_], bank(h), KX[:, d_], ALU.add).then_inc(s["v_z"], 1)

            def z_lo_last(h):
                d_ = slice(h * HALF, (h + 1) * HALF)
                lo(ZL[:, d_], ZF[:, d_], ZH[:, d_], "a_zh", 2 * (B - 1) + h + 1, "v_zl")

            def result(b, h):
                dve.wait_ge(s["p_o"], 2 * b + h + 1)
                xs = X[:, bass.ds(b * N + h * HALF, HALF)]
                TT(xs, bank(MIX_BANK[h]), xs, ALU.add).then_inc(s["v_o"], 1)

            def image(b, cur, prev, nxt):
                p = b - 1
                if cur:
                    project_lo(QL, QH, 0, BQS[:, 0:1], "a_qh", "v_ql", b)
                    project_lo(KL, KH, N, VEC[:, 3:4], "a_kh", "v_kl", b)
                for t in range(TILES):
                    if prev and t == 0:
                        et_lo(p, 6)
                    if nxt and t == 4:
                        group_norm_a(b + 1, MISC_BANK)
                    if not prev and t == 0:
                        misc_lo(VL[:, 0:4, :], VH[:, 0:4, :], "a_vh", 1, "v_vl")
                    if cur:
                        row_max(b, t)
                    if nxt and t == 4:
                        group_norm_b(b + 1, MISC_BANK)
                    if prev and t == 1:
                        et_lo(p, 7)
                    if cur and t >= 2:
                        et_lo(b, t - 2)
                    if cur:
                        if nxt and prev and t == TILES - 1:
                            dve.wait_ge(s["g_x1"], 2 * p + 2)
                            dve.wait_ge(s["p_xt"], 2 * p + 2)
                            hn(b + 1)
                        if nxt and t == 2:
                            dve.wait_ge(s["d_xs"], 16 * (B - 1))
                            stats(b + 1)
                        if prev and t == 1:
                            residual(p, 0)
                        row_sum(b, t)
                        if not prev and t == TILES - 2:
                            hn_lo(1)
                        if nxt:
                            if t == 2:
                                stats_end()
                            if t == 5:
                                group_norm_c(b + 1)
                                if not prev:
                                    hn(1)
                    if prev:
                        if t == 1 and not cur:
                            residual(p, 0)
                            dve.wait_ge(s["a_sh"], 1)
                            TT(SYL[:, 0:T_COS], SYN[:, 0:T_COS],
                               SYH[:, 0:T_COS].bitcast(F32), ALU.subtract)\
                                .then_inc(s["v_syl"], 1)
                            mid = SYH[K_MID:K_LO, T_COS:T_END]
                            TT(mid, SYN[K_MID:K_LO, T_COS:T_END], mid.bitcast(F32),
                               ALU.subtract).then_inc(s["v_syl"], 1)
                        if t == 2:
                            misc_lo(XTL[:, 0:4, :], XTH[:, 0:4, :], "a_xh", 2 * p + 1, "v_xl")
                        if t == 5:
                            if not cur:
                                rt_lo(0)
                            residual(p, 1, PV_BANK if cur else LAST_PV_BANK)
                    if cur:
                        if prev and t == 4:
                            misc_lo(VL[:, 0:4, :], VH[:, 0:4, :], "a_vh", 2 * b + 1, "v_vl")
                        if t == (5 if prev else 1):
                            misc_lo(VL[:, 4:8, :], VH[:, 4:8, :], "a_vh", 2 * b + 2, "v_vl")
                        if t == 3 and not prev:
                            dve.wait_ge(s["p_w1s"], 1)
                            dve.tensor_copy(W1S[:], bank(PV_BANK)[0:NF, W1S_AT:W1S_AT + HID])\
                                    .then_inc(s["v_w1s"], 1)
                    if prev and t == 6:
                        misc_lo(XTL[:, 4:8, :], XTH[:, 4:8, :], "a_xh", 2 * p + 2, "v_xl")

            attention(image, dve)

            A, D = bank(6), bank(7)
            dve.wait_ge(s["a_ur"], B + 1)
            TT(FR, FR, FR, ALU.mult).then_inc(s["v_m2"], 1)
            dve.wait_ge(s["v_m2"], 1)
            TT(FR[:, :, 0:NF], FR[:, :, 0:NF], FR[:, :, NF:2 * NF], ALU.add)\
                .then_inc(s["v_m2"], 1)
            dve.wait_ge(s["p_c25"], 1)
            dve.tensor_copy(C25[:], A[0:NF, 0:B]).then_inc(s["v_c25"], 1)
            dve.wait_ge(s["p_hid"], 1)
            TS(HIDV[:], D[0:HID, 0:B], B1[:, 0:1], 0.0, ALU.add, ALU.max).then_inc(s["v_hid"], 1)

            ml = [0]

            def small(ins):
                ml[0] += 1
                ins.then_inc(s["v_ml"], 1)

            def settle():
                dve.wait_ge(s["v_ml"], ml[0])

            def m(i, n=1):
                return ML[:, i:i + n, :]

            def wide(i, n):
                return m(i).broadcast_to([NK, n, B])

            def params():
                dve.wait_ge(s["p_par"], 1)
                for j, row in enumerate((ML_P, ML_P + 1, ML_P2)):
                    small(TS(ML[:, row, :], A[0:NK, 32 + j * B:32 + (j + 1) * B], B2[:, j:j + 1],
                             None, ALU.add))
                settle()

            def mlp_kernel():
                small(STT(out=m(ML_ABS, 2), in0=m(ML_P, 2), scalar=-1.0, in1=m(ML_P, 2),
                          op0=ALU.mult, op1=ALU.max))
                settle()
                small(TT(m(ML_BIG), m(ML_ABS), m(ML_ABS + 1), ALU.max))
                settle()
                small(TS(m(ML_TINY), m(ML_BIG), 1e-36, None, ALU.is_lt))
                small(TS(m(ML_RB), m(ML_BIG), 1e-36, None, ALU.max))
                settle()
                small(dve.reciprocal(m(ML_RB), m(ML_RB)))
                settle()
                small(TT(m(ML_S, 4), m(ML_P, 4), wide(ML_RB, 4), ALU.mult))
                settle()
                p1 = ML[:, ML_S + 1:ML_S + 4:2, :]
                small(TT(p1, p1, wide(ML_TINY, 2), ALU.add))
                settle()
                small(TT(m(ML_SQ, 2), m(ML_S, 2), m(ML_S, 2), ALU.mult))
                settle()
                TT(m(ML_N2), m(ML_SQ), m(ML_SQ + 1), ALU.add).then_inc(s["v_n2"], 1)
                small(TS(m(ML_GE), m(ML_S + 1), 0.0, None, ALU.is_lt))
                small(TS(m(ML_GE + 1), m(ML_S + 1), 0.0, None, ALU.is_ge))
                small(TS(m(ML_SGN), m(ML_S), 0.0, None, ALU.is_ge))
                settle()
                small(TS(m(ML_SGN), m(ML_SGN), 2.0, -1.0, ALU.mult, ALU.add))
                dve.wait_ge(s["a_nr"], 1)
                small(TT(m(ML_M), m(ML_A + 1), m(ML_NR), ALU.add))
                settle()
                small(TT(m(ML_D), m(ML_M), m(ML_A), ALU.subtract))
                small(TT(m(ML_NN), m(ML_M), m(ML_M), ALU.mult))
                settle()
                small(TT(m(ML_SC, 2), m(ML_GE, 2), wide(ML_D, 2), ALU.mult))
                small(TT(m(ML_NN), m(ML_NN), m(ML_SQ), ALU.add))
                settle()
                small(TT(m(ML_SC, 2), m(ML_SC, 2), wide(ML_A, 2), ALU.add))
                small(dve.reciprocal(m(ML_RN), m(ML_NN)))
                settle()
                small(TT(m(ML_SC), m(ML_SC), m(ML_SGN), ALU.mult))
                settle()
                x_, y_ = MISC[0:NK, M_XY:M_XY + 1], MISC[0:NK, M_XY + 1:M_XY + 2]
                small(TS(m(ML_UV, 2), m(ML_SC, 2), x_, None, ALU.mult))
                dve.wait_ge(s["a_lam"], 1)
                small(TS(m(ML_L2), m(ML_LAM), KEPS, None, ALU.add))
                settle()
                small(STT(out=m(ML_UV), in0=m(ML_SC + 1), scalar=y_, in1=m(ML_UV), op0=ALU.mult,
                          op1=ALU.subtract))
                small(STT(out=m(ML_UV + 1), in0=m(ML_SC), scalar=y_, in1=m(ML_UV + 1),
                          op0=ALU.mult, op1=ALU.add))
                small(dve.reciprocal(m(ML_L2), m(ML_L2)))
                settle()
                small(STT(out=m(ML_LAM, 2), in0=m(ML_LAM, 2), scalar=2.0, in1=m(ML_LAM, 2),
                          op0=ALU.mult, op1=ALU.mult))
                small(TT(m(ML_UV, 2), m(ML_UV, 2), m(ML_UV, 2), ALU.mult))
                settle()
                small(dve.reciprocal(m(ML_LAM, 2), m(ML_LAM, 2)))
                small(TT(m(ML_UV, 2), m(ML_UV, 2), wide(ML_RN, 2), ALU.mult))
                settle()
                small(TT(m(ML_UV, 2), m(ML_UV, 2), m(ML_LAM, 2), ALU.mult))
                settle()
                TT(m(ML_E), m(ML_UV), m(ML_UV + 1), ALU.add).then_inc(s["v_ex"], 1)
                dve.wait_ge(s["p_sum"], 1)
                small(TS(ML[:, ML_RS, :], A[0:NK, 64:64 + B], KEPS, None, ALU.add))
                settle()
                small(dve.reciprocal(m(ML_RS), m(ML_RS)))
                settle()
                TT(K[:], ML[:, ML_K, :], ML[:, ML_RS, :], ALU.mult).then_inc(s["v_k"], 1)
                lo(K3[K_LO:K_ROWS, :], A[K_LO:K_ROWS, K3_AT:K3_AT + 2 * B], K3[K_LO:K_ROWS, :],
                   "a_k3", 1, "v_k3")

            def g_columns():
                dve.wait_ge(s["p_g"], 1)
                for g in range(2):
                    dve.tensor_copy(GC.rearrange("p (b c) -> p c b", b=B)
                                    [:, g * 2 * NZ:(g + 1) * 2 * NZ, :],
                                    bank(5)[0:CH, 0:4 * NZ * B]
                                    .rearrange("p (c b) -> p c b", b=2 * B)
                                    [:, :, g * B:(g + 1) * B]).then_inc(s["v_g"], 1)
                dve.wait_ge(s["v_g"], 2)
                dve.wait_ge(s["g_gam"], 2)

            def g3_columns():
                dve.wait_ge(s["p_g"], 2)
                dve.tensor_copy(G3C.rearrange("p (b c) -> p c b", b=B),
                                bank(4)[0:NK, 0:NK * B].rearrange("p (c b) -> p c b", b=B))\
                    .then_inc(s["v_g"], 1)
                dve.wait_ge(s["v_g"], 3)
                dve.wait_ge(s["g_g3z"], 1)

            def first():
                params()
                mlp_kernel()
                g_columns()
                g_full(0)
                g_lo(0)
                g3_columns()
                g3_copy(0)
                v3_lo(0)
                g_full(1)
                g3_copy(1)
                vt_lo(0)
                rt_lo(1)

            def step(i, more):
                z_sum(i, 0)
                if more:
                    g_lo(i + 1)
                z_sum(i, 1)
                if not more:
                    z_lo_last(0)
                    z_lo_last(1)
                if more:
                    v3_lo(i + 1)
                if more > 1:
                    g_full(i + 2)
                    g3_copy(i + 2)
                if more:
                    vt_lo(i + 1)
                result(i, 0)
                if more > 1:
                    rt_lo(i + 2)
                result(i, 1)

            synthesis(first, step, dve)

        @block.gpsimd
        def _(pool):
            TT = pool.tensor_tensor
            pool.memset(MINUS_HALF[:], -0.5).then_inc(s["g_one"], 1)
            pool.memset(ONE[:], 1.0).then_inc(s["g_one"], 1)
            pool.memset(UNUSED[:], 0.0).then_inc(s["g_hl"], 1)
            pool.wait_ge(s["g_one"], 1)

            def rstd(n):
                pool.wait_ge(s["v_gn"], 8 * n + 4)
                TT(GD[:], GS[:], MINUS_HALF[:], ALU.pow).then_inc(s["g_gn"], 1)

            def hn_lo(b):
                pool.wait_ge(s["a_hh"], b + 2)
                TT(HNL[:], T[:], HNH[:].bitcast(F32), ALU.subtract).then_inc(s["g_hl"], 1)

            rstd(0)
            pool.wait_ge(s["a_ah"], 1)
            TT(ANL[:], R[:, 0:UW], ANH[:].bitcast(F32), ALU.subtract).then_inc(s["g_al"], 1)

            def scale(b, t):
                pool.wait_ge(s["v_ri"], TILES * b + t + 1)
                e = E[:, (t % 4) * N:(t % 4 + 1) * N]
                TT(e, e, RI[:, t % 4:t % 4 + 1].broadcast_to([P, N]), ALU.mult)\
                    .then_inc(s["g_scl"], 1)

            def keep_x1(p, h):
                pool.wait_ge(s["v_x1"], 2 * p + h + 1)
                pool.tensor_copy(X[:, bass.ds(p * N + h * HALF, HALF)],
                                 T[:, h * HALF:(h + 1) * HALF]).then_inc(s["g_x1"], 1)

            def rst(n):
                if is_later(n):
                    pool.wait_ge(s["p_rt"], n)
                else:
                    pool.wait_ge(s["p_xt"], 2 * B - 1)
                    pool.wait_ge(s["g_x1"], 2 * B - 1)
                pool.tensor_copy(RST[:, 0:3 * CH], R[:, bass.ds(n * UR, 3 * CH)])\
                    .then_inc(s["g_rst"], 1)
                pool.tensor_copy(RST[:, 3 * CH:4 * CH], R[:, bass.ds(n * UR + UO + UA, CH)])\
                    .then_inc(s["g_rst"], 1)

            def k_x1(n, h):
                d_ = slice(h * HALF, (h + 1) * HALF)
                pool.wait_ge(s["a_kh2"], 2 * n + h + 1)
                if is_later(n):
                    pool.wait_ge(s["v_z"], 2 * n + h - 1)
                TT(KX[:, d_], KHAT[:, d_], X[:, bass.ds(n * N + h * HALF, HALF)], ALU.mult)\
                    .then_inc(s["g_kx"], 1)

            def z_lo(b, h):
                d_ = slice(h * HALF, (h + 1) * HALF)
                pool.wait_ge(s["a_zh"], 2 * b + h + 1)
                TT(ZL[:, d_], ZF[:, d_], ZH[:, d_].bitcast(F32), ALU.subtract)\
                    .then_inc(s["g_zl"], 1)

            def image(b, cur, prev, nxt):
                p = b - 1
                for t in range(TILES):
                    if cur:
                        scale(b, t)
                    if prev and t == 1:
                        keep_x1(p, 0)
                    if not cur and t == 2:
                        rst(0)
                    if prev and t == 5:
                        keep_x1(p, 1)
                    if nxt and t == 4:
                        rstd(b + 1)
                if nxt and prev:
                    hn_lo(b + 1)

            attention(image, pool)

            pool.wait_ge(s["p_xt"], 2 * B)
            pool.wait_ge(s["g_x1"], 2 * B)
            pool.memset(G3S, 0.0).then_inc(s["g_g3z"], 1)
            for n, (full, part) in enumerate(((GAMS, GAMR), (GAM3S, GAM3R))):
                pool.wait_ge(s["a_gam"], n + 1)
                if n == 0:
                    pool.wait_ge(s["g_g3z"], 1)
                else:
                    pool.wait_ge(s["g_gam"], n)
                mid = part[K_MID:K_LO, :]
                TT(mid, full[K_MID:K_LO, :], mid.bitcast(F32), ALU.subtract)\
                    .then_inc(s["g_gam"], 1)
            pool.wait_ge(s["g_gam"], 2)

            def first():
                rst(1)
                k_x1(0, 0)
                k_x1(0, 1)
                rst(2)

            def step(i, more):
                if more:
                    z_lo(i, 0)
                    z_lo(i, 1)
                    k_x1(i + 1, 0)
                    k_x1(i + 1, 1)
                if more > 2:
                    rst(i + 3)

            synthesis(first, step, pool)


_ORDER = ["x", "L0_conv_norm_w", "L0_conv_norm_b", "L0_conv_wq", "L0_conv_bq", "L0_conv_wk",
          "L0_conv_bk", "L0_conv_wv", "L0_conv_bv", "L0_conv_wp", "L0_conv_bp", "L1_conv_w1",
          "L1_conv_b1", "L1_conv_w2", "L1_conv_b2", "L1_conv_wr"]


def kernel(**inputs):
    import concourse.bacc as bacc
    from concourse.bass_utils import run_bass_kernel_spmd

    nc = bacc.Bacc("TRN2", target_bir_lowering=False, num_devices=1)
    arrays, args = {}, []
    tables = shape_tables()
    named = [(n, np.ascontiguousarray(inputs[n])) for n in _ORDER] + list(tables.items())
    for name, a in named:
        arrays[f"in_{name}"] = a
        args.append(nc.dram_tensor(f"in_{name}", a.shape, mybir.dt.from_np(a.dtype),
                                   kind="ExternalInput").ap())
    out = nc.dram_tensor("out_0", (B, C, SIDE, SIDE), F32, kind="ExternalOutput").ap()
    attention_filter_kernel(nc, *args, out)
    r = run_bass_kernel_spmd(nc, [arrays], core_ids=[0])
    return r.results[0]["out_0"]
```
